# Optimizing a Trainium2 kernel written in Bass

```python
import numpy as np
import jax
import jax.numpy as jnp

def _softmax(x, axis=-1):
    return jax.nn.softmax(x, axis=axis)

def _gelu(x):
    return jax.nn.gelu(x, approximate=True)

def _silu(x):
    return jax.nn.silu(x)

def _sigmoid(x):
    return jax.nn.sigmoid(x)

def _layernorm(x, axis=-1, eps=1e-05):
    m = jnp.mean(x, axis=axis, keepdims=True)
    v = jnp.var(x, axis=axis, keepdims=True)
    return (x - m) / jnp.sqrt(v + eps)

def _scatter_add(tgt, idx, src, axis=0):
    return tgt.at[idx].add(src)

def _segment_sum(src, seg, n):
    return jax.ops.segment_sum(src, seg, n)
kernel_name = 'mk_gnn_preln_d2_gnn_r32_193b51'

def setup_inputs(seed: int=0):
    np.random.seed(seed)
    _w = jnp.asarray

    def _rec_inputs():
        import jax
        import jax.numpy as jnp
        _gk = jax.random.key(seed)
        x = -0.0005121 + 1.001 * jax.random.normal(jax.random.fold_in(_gk, 1), (50000, 64), jnp.float32)
        _s = jax.random.randint(jax.random.fold_in(_gk, 2), (25000,), 0, 50000, jnp.int32)
        _d = jax.random.randint(jax.random.fold_in(_gk, 3), (25000,), 0, 50000, jnp.int32)
        _loop = jnp.arange(50000, dtype=jnp.int32)
        src = jnp.concatenate([_s, _d, _loop])
        dst = jnp.concatenate([_d, _s, _loop])
        _o = jnp.argsort(dst, stable=True)
        src = src[_o]
        dst = dst[_o]
        return (x, src, dst)
    x, src, dst = _rec_inputs()

    def _L0_gnn_setup():
        import jax, jax.numpy as jnp
        import numpy as np
        N_NODES = 50000
        N_EDGES = 25000
        DIM_IN = 64
        DIM_HID = 128
        DIM_OUT = 64

        def _linear_init(key, fan_in, fan_out):
            kw, kb = jax.random.split(key)
            bound = 1.0 / np.sqrt(fan_in)
            W = jax.random.uniform(kw, (fan_in, fan_out), minval=-bound, maxval=bound, dtype=jnp.float32)
            b = jax.random.uniform(kb, (fan_out,), minval=-bound, maxval=bound, dtype=jnp.float32)
            return (W, b)
        key = jax.random.key(seed)
        kx, ke, k0, k1, k2 = jax.random.split(key, 5)
        x = jax.random.normal(kx, (N_NODES, DIM_IN), dtype=jnp.float32)
        edge_idx = jax.random.randint(ke, (2, N_EDGES), 0, N_NODES, dtype=jnp.int64)
        W0, b0 = _linear_init(k0, 2 * DIM_IN, DIM_HID)
        W1, b1 = _linear_init(k1, DIM_HID, DIM_HID)
        W2, b2 = _linear_init(k2, DIM_HID, DIM_OUT)
        return {'x': x, 'edge_idx': edge_idx, 'W0': W0, 'b0': b0, 'W1': W1, 'b1': b1, 'W2': W2, 'b2': b2}
    _L0_gnn_all = _L0_gnn_setup()
    _L0_gnn_in = {k: v for k, v in _L0_gnn_all.items() if k in ('W0', 'b0', 'W1', 'b1', 'W2', 'b2')}
    del _L0_gnn_all

    def _L1_gnn_setup():
        import jax, jax.numpy as jnp
        import numpy as np
        N_NODES = 50000
        N_EDGES = 25000
        D = 64
        EPS_GIN = 0.0
        BN_EPS = 1e-05
        key = jax.random.key(seed)
        ks = jax.random.split(key, 9)
        h = jax.random.normal(ks[0], (N_NODES, D), dtype=jnp.float32)
        src = jax.random.randint(ks[1], (N_EDGES,), 0, N_NODES, dtype=jnp.int64)
        dst = jax.random.randint(ks[2], (N_EDGES,), 0, N_NODES, dtype=jnp.int64)
        s = 1.0 / np.sqrt(D)
        W1 = jax.random.uniform(ks[3], (D, D), jnp.float32, -s, s)
        b1 = jax.random.uniform(ks[4], (D,), jnp.float32, -s, s)
        W2 = jax.random.uniform(ks[5], (D, D), jnp.float32, -s, s)
        b2 = jax.random.uniform(ks[6], (D,), jnp.float32, -s, s)
        gamma = jnp.ones((D,), jnp.float32)
        beta = jnp.zeros((D,), jnp.float32)
        return {'h': h, 'W1': W1, 'b1': b1, 'W2': W2, 'b2': b2, 'gamma': gamma, 'beta': beta, 'src': src, 'dst': dst}
    _L1_gnn_all = _L1_gnn_setup()
    _L1_gnn_in = {k: v for k, v in _L1_gnn_all.items() if k in ('W1', 'b1', 'W2', 'b2', 'gamma', 'beta')}
    del _L1_gnn_all
    return {'x': x, 'src': src, 'dst': dst, 'L0_gnn_W0': _L0_gnn_in['W0'], 'L0_gnn_b0': _L0_gnn_in['b0'], 'L0_gnn_W1': _L0_gnn_in['W1'], 'L0_gnn_b1': _L0_gnn_in['b1'], 'L0_gnn_W2': _L0_gnn_in['W2'], 'L0_gnn_b2': _L0_gnn_in['b2'], 'L1_gnn_W1': _L1_gnn_in['W1'], 'L1_gnn_b1': _L1_gnn_in['b1'], 'L1_gnn_W2': _L1_gnn_in['W2'], 'L1_gnn_b2': _L1_gnn_in['b2'], 'L1_gnn_gamma': _L1_gnn_in['gamma'], 'L1_gnn_beta': _L1_gnn_in['beta']}

def reference(x, src, dst, L0_gnn_W0, L0_gnn_b0, L0_gnn_W1, L0_gnn_b1, L0_gnn_W2, L0_gnn_b2, L1_gnn_W1, L1_gnn_b1, L1_gnn_W2, L1_gnn_b2, L1_gnn_gamma, L1_gnn_beta):
    import jax
    import jax.numpy as jnp

    def _L0_gnn_ref(x, edge_idx, W0, b0, W1, b1, W2, b2):
        import jax, jax.numpy as jnp
        import numpy as np
        N_NODES = 50000
        N_EDGES = 25000
        DIM_IN = 64
        DIM_HID = 128
        DIM_OUT = 64

        def _linear_init(key, fan_in, fan_out):
            kw, kb = jax.random.split(key)
            bound = 1.0 / np.sqrt(fan_in)
            W = jax.random.uniform(kw, (fan_in, fan_out), minval=-bound, maxval=bound, dtype=jnp.float32)
            b = jax.random.uniform(kb, (fan_out,), minval=-bound, maxval=bound, dtype=jnp.float32)
            return (W, b)
        row, col = (edge_idx[0], edge_idx[1])
        h = jnp.concatenate([x[row], x[col]], axis=-1)
        h = jax.nn.softplus(h @ W0 + b0)
        h = jax.nn.softplus(h @ W1 + b1)
        h = h @ W2 + b2
        return jax.ops.segment_sum(h, row, num_segments=x.shape[0])

    def _L1_gnn_ref(h, W1, b1, W2, b2, gamma, beta, src, dst):
        import jax, jax.numpy as jnp
        import numpy as np
        N_NODES = 50000
        N_EDGES = 25000
        D = 64
        EPS_GIN = 0.0
        BN_EPS = 1e-05
        n = h.shape[0]
        neigh = jax.ops.segment_sum(h[src], dst, num_segments=n)
        z = (1.0 + EPS_GIN) * h + neigh
        z = jnp.maximum(z @ W1 + b1, 0.0) @ W2 + b2
        mean = jnp.mean(z, axis=0)
        var = jnp.var(z, axis=0)
        z = (z - mean) * jax.lax.rsqrt(var + BN_EPS) * gamma + beta
        z = jnp.maximum(z, 0.0)
        z = h + z
        return z
    edge_index = jnp.stack([src, dst])
    h = jnp.maximum(_layernorm(x, axis=-1), 0.0)
    x = x + _L0_gnn_ref(h, edge_index, L0_gnn_W0, L0_gnn_b0, L0_gnn_W1, L0_gnn_b1, L0_gnn_W2, L0_gnn_b2)
    h = jnp.maximum(_layernorm(x, axis=-1), 0.0)
    x = x + _L1_gnn_ref(h, L1_gnn_W1, L1_gnn_b1, L1_gnn_W2, L1_gnn_b2, L1_gnn_gamma, L1_gnn_beta, src, dst)
    return x

_drawn_inputs = setup_inputs


def setup_inputs(seed=0):
    import zlib

    import numpy as np

    out = dict(_drawn_inputs(seed))
    spreads = {'L1_gnn_gamma': (1.0, 0.2), 'L1_gnn_beta': (0.0, 0.1)}
    factors = {'L0_gnn_b0': 8.0, 'L1_gnn_b1': 2.816, 'L1_gnn_b2': 8.0}
    for name, (base, spread) in spreads.items():
        noise = np.random.default_rng([zlib.crc32(name.encode()), seed]).standard_normal(out[name].shape)
        drawn = base * np.exp(spread * noise) if base else spread * noise
        out[name] = jnp.asarray(drawn.astype(out[name].dtype))
    for name, factor in factors.items():
        out[name] = (out[name] * factor).astype(out[name].dtype)
    return out
```

```python
import concourse.bass as bass
import concourse.mybir as mybir
from contextlib import ExitStack

F32 = mybir.dt.float32
I32 = mybir.dt.int32
ALU = mybir.AluOpType
ACT = mybir.ActivationFunctionType
AX = mybir.AxisListType

LN_EPS = 1e-5
BN_EPS = 1e-5
SOFTPLUS_CLAMP = 40.0
P = 125
SUBS = 8
TILES = 4
ACCS = 2
RING = 4


def rounds(engine, stages, total):
    last = total + max(lag for lag, _ in stages)

    def step(u, turn, static):
        for lag, body in stages:
            v = u - lag
            slot, t = v % RING, turn + v // RING
            item = t * RING + slot
            if static and not 0 <= item < total:
                continue
            body(item, slot, t)

    head = 2
    tail = total // RING
    for turn in range(head):
        for u in range(RING):
            step(u, turn, True)
    with engine.Fori(head, tail) as turn:
        for u in range(RING):
            step(u, turn, False)
    for s in range(tail * RING, last):
        step(s % RING, s // RING, True)


def hold(engine, semaphore, value, passed):
    engine.wait_ge(semaphore, value)
    if not isinstance(value, int):
        engine.sem_inc(passed, 1)


def wait_from(engine, semaphore, value, passed=None):
    if isinstance(value, int) and value < 1:
        return
    if passed is None:
        engine.wait_ge(semaphore, value)
    else:
        hold(engine, semaphore, value, passed)


def gnn_program(nc, x, src, dst, w0, b0, w1, b1, w2, b2, g_w1, g_b1, g_w2, g_b2, gamma, beta, out):
    N, D = x.shape
    E = src.shape[0]
    HID = w0.shape[1]
    BLOCKS = N // (P * SUBS)
    COLS = E // P
    GROUPS = COLS // TILES
    BW = SUBS * D
    PAIRS = SUBS // 2
    TW = PAIRS * P
    GW = TILES * P
    assert N == BLOCKS * P * SUBS and E == COLS * P and COLS == GROUPS * TILES and HID == 2 * D == 128

    h0_t = nc.dram_tensor("h0_table", [N, D], F32).ap()
    h1_t = nc.dram_tensor("h1_table", [N, D], F32).ap()
    r_t = nc.dram_tensor("x1_plus_h1", [N, D], F32).ap()
    acc0 = [nc.dram_tensor(f"acc0_{k}", [N + P, D], F32).ap() for k in range(ACCS)]
    acc1 = [nc.dram_tensor(f"acc1_{k}", [N + P, D], F32).ap() for k in range(ACCS)]

    def rows(table, block):
        return table[bass.ds(block * (P * SUBS), P * SUBS), :].rearrange("(s p) f -> p s f", p=P)

    def blk(ap):
        return ap.rearrange("p (s f) -> p s f", f=D)

    with ExitStack() as ctx:
        def sb(name, shape, dt=F32):
            return ctx.enter_context(nc.sbuf_tensor(name, shape, dt))

        def sem(name):
            return ctx.enter_context(nc.semaphore(name))

        def sems(name, n=RING):
            return [sem(f"{name}_{i}") for i in range(n)]

        def bank(name):
            return ctx.enter_context(nc.psum_tensor(name, [128, 512], F32))

        ident = sb("ident", [128, 128])
        earlier = sb("earlier", [P, P])
        junk_row = sb("junk_row", [P, 1])
        zeros = sb("zeros", [P, 50 * D])
        ln_eps = sb("ln_eps", [P, 1])
        w0_s = sb("w0_s", [128, HID])
        w1_s = sb("w1_s", [HID, HID])
        w2_s = sb("w2_s", [HID, D])
        b0_s = sb("b0_s", [HID, 1])
        b1_s = sb("b1_s", [HID, 1])
        b2_s = sb("b2_s", [P, D])
        gw1_s = sb("gw1_s", [128, 128])
        gw2_s = sb("gw2_s", [128, 128])
        gb1_s = sb("gb1_s", [128, 1])
        gb2_s = sb("gb2_s", [128, 1])
        gamma_s = sb("gamma_s", [128, 1])
        beta_s = sb("beta_s", [128, 1])
        pair_mean = sb("pair_mean", [128, 128])
        src_s = sb("src_s", [P, COLS], I32)
        dst_s = sb("dst_s", [P, COLS], I32)

        banks = [bank(f"bank{i}") for i in range(8)]

        s_cz, s_ci, s_w, s_pm = sem("const_zeroed"), sem("const_made"), sem("weights_loaded"), sem("pair_mean_made")
        s_gz = sem("diagonal_zeroed")
        passed_sp, passed_pool = sem("passed_sp"), sem("passed_pool")
        with nc.Block("setup") as block:
            @block.gpsimd
            def _(pool):
                nc.gpsimd.memset(ident[:, :], 0.0).then_inc(s_cz, 1)
                nc.gpsimd.memset(earlier[:, :], 1.0).then_inc(s_cz, 1)
                nc.gpsimd.memset(pair_mean[:, :], 0.0).then_inc(s_cz, 1)
                nc.gpsimd.memset(ln_eps[:, :], LN_EPS).then_inc(s_cz, 1)
                nc.gpsimd.iota(junk_row[:, :], [[0, 1]], base=N, channel_multiplier=1,
                               allow_small_or_imprecise_dtypes=True).then_inc(s_cz, 1)
                pool.wait_ge(s_cz, 5)
                nc.gpsimd.affine_select(out=ident[:, :], in_=ident[:, :], compare_op=ALU.not_equal, fill=1.0,
                                        base=0, pattern=[[-1, 128]], channel_multiplier=1).then_inc(s_ci, 1)
                nc.gpsimd.affine_select(out=earlier[:, :], in_=earlier[:, :], compare_op=ALU.is_gt, fill=0.0,
                                        base=0, pattern=[[-1, P]], channel_multiplier=1).then_inc(s_ci, 1)
                for n, off in enumerate((0, D, -D)):
                    if n:
                        pool.wait_ge(s_pm, n)
                    nc.gpsimd.affine_select(out=pair_mean[:, :], in_=pair_mean[:, :], compare_op=ALU.not_equal,
                                            fill=0.5, base=off, pattern=[[-1, 128]],
                                            channel_multiplier=1).then_inc(s_pm, 1)
                pool.wait_ge(s_pm, 3)
                pool.wait_ge(s_ci, 2)

            @block.vector
            def _(dve):
                nc.vector.memset(gw1_s[:, :], 0.0).then_inc(s_gz, 1)
                nc.vector.memset(gw2_s[:, :], 0.0).then_inc(s_gz, 1)
                nc.vector.memset(zeros[:, :], 0.0).then_inc(s_gz, 1)

            @block.sync
            def _(sp):
                col = lambda v: v.rearrange("(p a) -> p a", a=1)
                loads = [(w0_s[:, :], w0), (w1_s[:, :], w1), (w2_s[:, :], w2),
                         (b0_s[:, :], col(b0)), (b1_s[:, :], col(b1)),
                         (b2_s[:, :], b2.rearrange("(a f) -> a f", a=1).to_broadcast([P, D])),
                         (src_s[:, :], src.rearrange("(p j) -> p j", p=P)),
                         (dst_s[:, :], dst.rearrange("(p j) -> p j", p=P))]
                for h in (0, D):
                    loads += [(gb1_s[h:h + D, :], col(g_b1)), (gb2_s[h:h + D, :], col(g_b2)),
                              (gamma_s[h:h + D, :], col(gamma)), (beta_s[h:h + D, :], col(beta))]
                for to, fr in loads:
                    sp.dma_start(to, fr).then_inc(s_w, 16)
                sp.wait_ge(s_gz, 3)
                diag = [(gw1_s[h:h + D, h:h + D], g_w1) for h in (0, D)]
                diag += [(gw2_s[h:h + D, h:h + D], g_w2) for h in (0, D)]
                for to, fr in diag:
                    sp.dma_start(to, fr).then_inc(s_w, 16)
                sp.wait_ge(s_w, 16 * (len(loads) + len(diag)))



        def norm_phase(name, sources, table, residual, zeroed):
            with ExitStack() as ph:
                def t(n, shape, k=RING):
                    return [ph.enter_context(nc.sbuf_tensor(f"{name}_{n}_{i}", shape, F32)) for i in range(k)]

                def s(n):
                    return ph.enter_context(nc.semaphore(f"{name}_{n}"))

                def ss(n):
                    return [s(f"{n}_{i}") for i in range(RING)]

                parts = [t(f"part{k}", [P, BW]) for k in range(len(sources))]
                centred, squared, normed = t("centred", [P, BW]), t("squared", [P, BW]), t("normed", [P, BW])
                mean, var, std, rstd = (t(n, [P, SUBS]) for n in ("mean", "var", "std", "rstd"))
                loaded = ss("loaded")
                table_out, resid_out = ss("table_out"), ss("resid_out")
                zero_out = s("zero_out")
                accs_summed, x_summed = s("accs_summed"), s("x_summed")
                rowsum_done, mean_done, centred_done = s("rowsum_done"), s("mean_done"), s("centred_done")
                squared_done, var_done, std_done = s("squared_done"), s("var_done"), s("std_done")
                rstd_done, normed_done, resid_done = s("rstd_done"), s("normed_done"), s("resid_done")
                summed = len(sources) > 1
                ZW = zeros.shape[1] // D
                resid_lag = 3

                with nc.Block(name) as block:
                    @block.sync
                    def _(sp):
                        def load(b, q, turn):
                            if residual is not None:
                                wait_from(sp, resid_done, b - RING + 1, passed_sp)
                            else:
                                wait_from(sp, centred_done, b - RING + 1, passed_sp)
                            for k, source in enumerate(sources):
                                sp.dma_start(blk(parts[k][q][:, :]), rows(source, b)).then_inc(loaded[q], 16)

                        def store(b, q, turn):
                            hold(sp, normed_done, b + 1, passed_sp)
                            sp.dma_start(rows(table, b), blk(normed[q][:, :])).then_inc(table_out[q], 16)

                        def store_resid(b, q, turn):
                            hold(sp, resid_done, b + 1, passed_sp)
                            sp.dma_start(rows(residual, b), blk(parts[1][q][:, :])).then_inc(resid_out[q], 16)

                        if residual is None:
                            rounds(sp, [(0, load), (3, store)], BLOCKS)
                        else:
                            def load_after_store(b, q, turn):
                                wait_from(sp, resid_out[q], 16 * turn, passed_sp)
                                load(b, q, turn)
                            rounds(sp, [(0, load_after_store), (3, store), (3, store_resid)], BLOCKS)
                        for q in range(RING):
                            n = (BLOCKS - q + RING - 1) // RING
                            sp.wait_ge(table_out[q], 16 * n)
                            if residual is not None:
                                sp.wait_ge(resid_out[q], 16 * n)

                    @block.gpsimd
                    def _(pool):
                        def sum_accs(b, q, turn):
                            hold(pool, loaded[q], 16 * len(sources) * (turn + 1), passed_pool)
                            nc.gpsimd.tensor_tensor(parts[1][q][:, :], parts[1][q][:, :], parts[2][q][:, :],
                                                    ALU.add).then_inc(accs_summed, 1)

                        def add_resid(b, q, turn):
                            hold(pool, normed_done, b + 1, passed_pool)
                            nc.gpsimd.tensor_tensor(parts[1][q][:, :], parts[0][q][:, :], normed[q][:, :],
                                                    ALU.add).then_inc(resid_done, 1)

                        if summed:
                            rounds(pool, [(0, sum_accs), (resid_lag, add_resid)], BLOCKS)

                    @block.vector
                    def _(dve):
                        def centre(b, q, turn):
                            if summed:
                                dve.wait_ge(accs_summed, b + 1)
                                nc.vector.tensor_tensor(parts[0][q][:, :], parts[0][q][:, :], parts[1][q][:, :],
                                                        ALU.add).then_inc(x_summed, 1)
                                dve.wait_ge(x_summed, b + 1)
                            else:
                                dve.wait_ge(loaded[q], 16 * (turn + 1))
                            nc.vector.tensor_reduce(mean[q][:, :], blk(parts[0][q][:, :]), AX.X, ALU.add)\
                              .then_inc(rowsum_done, 1)
                            dve.wait_ge(rowsum_done, b + 1)
                            nc.vector.tensor_scalar(mean[q][:, :], mean[q][:, :], 1.0 / D, None, ALU.mult)\
                              .then_inc(mean_done, 1)
                            dve.wait_ge(mean_done, b + 1)
                            nc.vector.tensor_tensor(blk(centred[q][:, :]), blk(parts[0][q][:, :]),
                                                    mean[q][:, :].unsqueeze(2).to_broadcast([P, SUBS, D]),
                                                    ALU.subtract).then_inc(centred_done, 1)

                        def variance(b, q, turn):
                            dve.wait_ge(squared_done, b + 1)
                            nc.vector.tensor_reduce(var[q][:, :], blk(squared[q][:, :]), AX.X, ALU.add)\
                              .then_inc(var_done, 1)

                        def normalise(b, q, turn):
                            dve.wait_ge(std_done, b + 1)
                            nc.vector.reciprocal(rstd[q][:, :], std[q][:, :]).then_inc(rstd_done, 1)
                            wait_from(dve, table_out[q], 16 * turn)
                            if summed:
                                wait_from(dve, resid_done, b - RING + 1)
                            dve.wait_ge(rstd_done, b + 1)
                            nc.vector.scalar_tensor_tensor(blk(normed[q][:, :]), blk(centred[q][:, :]), 0.0,
                                                           rstd[q][:, :].unsqueeze(2).to_broadcast([P, SUBS, D]),
                                                           ALU.max, ALU.mult).then_inc(normed_done, 1)

                        rounds(dve, [(0, centre), (1, variance), (2, normalise)], BLOCKS)

                    @block.scalar
                    def _(act):
                        zn = 0
                        for acc in zeroed:
                            for r0 in range(0, N + P, P * ZW):
                                w = min(ZW, (N + P - r0) // P)
                                act.dma_start(acc[r0:r0 + P * w, :].rearrange("(p w) f -> p (w f)", p=P),
                                              zeros[:, 0:w * D]).then_inc(zero_out, 16)
                                zn += 1

                        def square(b, q, turn):
                            act.wait_ge(centred_done, b + 1)
                            wait_from(act, var_done, b - RING + 1)
                            nc.scalar.activation(squared[q][:, :], centred[q][:, :], ACT.Square)\
                              .then_inc(squared_done, 1)

                        def deviation(b, q, turn):
                            act.wait_ge(var_done, b + 1)
                            wait_from(act, rstd_done, b - RING + 1)
                            nc.scalar.activation(std[q][:, :], var[q][:, :], ACT.Sqrt, bias=ln_eps[:, :],
                                                 scale=1.0 / D).then_inc(std_done, 1)

                        rounds(act, [(0, square), (1, deviation)], BLOCKS)
                        act.wait_ge(zero_out, 16 * zn)

        norm_phase("norm0", [x], h0_t, None, acc0)

        def edge_phase(name, table, seg_s, accs, mlp):
            with ExitStack() as ph:
                def t(n, shape, k=RING, dt=F32):
                    return [ph.enter_context(nc.sbuf_tensor(f"{name}_{n}_{i}", shape, dt)) for i in range(k)]

                def s(n):
                    return ph.enter_context(nc.semaphore(f"{name}_{n}"))

                def ss(n):
                    return [s(f"{n}_{i}") for i in range(RING)]

                SIDES = 2 if mlp else 1
                W = SIDES * D
                src_i, dst_i, put_i = (t(n, [P, TILES], RING, I32) for n in ("src_i", "dst_i", "put_i"))
                seg_f = t("seg_f", [P, TILES])
                repeat_n, to_junk = t("repeat_n", [P, TILES]), t("to_junk", [P, TILES])
                gathered = t("gathered", [P, TILES * W])
                same, same_earlier = t("same", [P, GW], 2), t("same_earlier", [P, GW], 2)
                summed = t("summed", [P, TILES * D])
                indices_ready, same_ready, put_ready = s("indices_ready"), s("same_ready"), s("put_ready")
                seg_spread, same_masked, repeats_counted, junk_offset, junk_scaled = (
                    s(n) for n in ("seg_spread", "same_masked", "repeats_counted", "junk_offset", "junk_scaled"))
                gather_done = ss("gather_done")
                acc_done = [s(f"acc_done_{k}") for k in range(ACCS)]
                merged, summed_ready = s("merged"), s("summed_ready")
                gathered_used = s("gathered_used")
                if mlp:
                    pair_t, t1, e1, h1, t2, e2, h2 = (t(n, [128, GW], 1)[0] for n in
                                                      ("pair_t", "t1", "e1", "h1", "t2", "e2", "h2"))
                    message = t("message", [P, TILES * D], 1)[0]
                    (pair_t_ready, pre1_done, t1_ready, e1_ready, l1_ready, h1_ready, pre2_done, t2_ready,
                     e2_ready, l2_ready, h2_ready, raw_done, message_ready) = (s(n) for n in (
                         "pair_t_ready", "pre1_done", "t1_ready", "e1_ready", "l1_ready", "h1_ready", "pre2_done",
                         "t2_ready", "e2_ready", "l2_ready", "h2_ready", "raw_done", "message_ready"))
                ps_seg, ps_pair, ps_1, ps_2, ps_raw, ps_sum = (banks[i] for i in range(6))
                SCATTER_LAG = 2
                COMPUTE_LAG = 2

                def tiles(ap, w):
                    return ap.rearrange("p (j w) -> p j w", w=w)

                with nc.Block(name) as block:
                    @block.gpsimd
                    def _(pool):
                        def gather(g, q, turn):
                            hold(pool, indices_ready, g + 1, passed_pool)
                            wait_from(pool, gathered_used if mlp else merged, g - RING + 1, passed_pool)
                            for j in range(TILES):
                                for side in range(SIDES):
                                    idx = (src_i, dst_i)[side][q][:, j:j + 1]
                                    at = j * W + side * D
                                    pool.indirect_dma_start(
                                        gathered[q][:, at:at + D], None, table,
                                        bass.IndirectOffsetOnAxis(ap=idx, axis=0)).then_inc(gather_done[q], 16)

                        def scatter(g, q, turn):
                            hold(pool, summed_ready, g + 1, passed_pool)
                            hold(pool, put_ready, g + 1, passed_pool)
                            for j in range(TILES):
                                k = j % ACCS
                                wait_from(pool, acc_done[k], 16 * (g * (TILES // ACCS) + j // ACCS), passed_pool)
                                pool.indirect_dma_start(
                                    accs[k], bass.IndirectOffsetOnAxis(ap=put_i[q][:, j:j + 1], axis=0),
                                    summed[q][:, j * D:(j + 1) * D], None, compute_op=ALU.add)\
                                    .then_inc(acc_done[k], 16)

                        rounds(pool, [(0, gather), (SCATTER_LAG, scatter)], GROUPS)
                        for k in range(ACCS):
                            pool.wait_ge(acc_done[k], 16 * GROUPS * TILES // ACCS)

                    @block.vector
                    def _(dve):
                        def indices(g, q, turn):
                            wait_from(dve, gather_done[q], 16 * TILES * SIDES * turn)
                            wait_from(dve, seg_spread, g - RING + 1)
                            at = bass.ds(g * TILES, TILES)
                            nc.vector.tensor_copy(src_i[q][:, :], src_s[:, at])
                            if mlp:
                                nc.vector.tensor_copy(dst_i[q][:, :], dst_s[:, at])
                            nc.vector.tensor_copy(seg_f[q][:, :], seg_s[:, at]).then_inc(indices_ready, 1)

                        def repeats(g, q, turn):
                            r = q % 2
                            dve.wait_ge(seg_spread, g + 1)
                            wait_from(dve, merged, g - 1)
                            nc.vector.tensor_tensor(
                                tiles(same[r][:, :], P), tiles(ps_seg[0:P, 0:GW], P),
                                seg_f[q][:, :].unsqueeze(2).to_broadcast([P, TILES, P]),
                                ALU.is_equal).then_inc(same_ready, 1)
                            dve.wait_ge(same_ready, g + 1)
                            nc.vector.tensor_tensor(
                                tiles(same_earlier[r][:, :], P), tiles(same[r][:, :], P),
                                earlier[:, :].unsqueeze(1).to_broadcast([P, TILES, P]),
                                ALU.mult).then_inc(same_masked, 1)
                            dve.wait_ge(same_masked, g + 1)
                            nc.vector.tensor_reduce(repeat_n[q][:, :], tiles(same_earlier[r][:, :], P), AX.X,
                                                    ALU.add).then_inc(repeats_counted, 1)
                            nc.vector.scalar_tensor_tensor(
                                to_junk[q][:, :], seg_f[q][:, :], -1.0, junk_row[:, :].to_broadcast([P, TILES]),
                                ALU.mult, ALU.add).then_inc(junk_offset, 1)
                            dve.wait_ge(repeats_counted, g + 1)
                            dve.wait_ge(junk_offset, g + 1)
                            nc.vector.scalar_tensor_tensor(
                                to_junk[q][:, :], repeat_n[q][:, :], 1.0, to_junk[q][:, :],
                                ALU.min, ALU.mult).then_inc(junk_scaled, 1)
                            dve.wait_ge(junk_scaled, g + 1)
                            for k in range(ACCS):
                                wait_from(dve, acc_done[k], 16 * (g - RING + 1) * (TILES // ACCS))
                            nc.vector.tensor_tensor(put_i[q][:, :], to_junk[q][:, :], seg_f[q][:, :],
                                                    ALU.add).then_inc(put_ready, 1)

                        def clamp(g, psum, bias, to, done, pre):
                            dve.wait_ge(pre, g + 1)
                            nc.vector.tensor_scalar(to[:, :], psum[:, 0:GW], bias[:, :], SOFTPLUS_CLAMP,
                                                    ALU.add, ALU.min).then_inc(done, 1)

                        def softplus(g, psum, bias, ln, ln_done, to, done):
                            dve.wait_ge(ln_done, g + 1)
                            nc.vector.scalar_tensor_tensor(to[:, :], psum[:, 0:GW], bias[:, :], ln[:, :],
                                                           ALU.add, ALU.max).then_inc(done, 1)

                        def mlp_steps(g, q, turn):
                            clamp(g, ps_1, b0_s, t1, t1_ready, pre1_done)
                            softplus(g, ps_1, b0_s, e1, l1_ready, h1, h1_ready)
                            clamp(g, ps_2, b1_s, t2, t2_ready, pre2_done)
                            softplus(g, ps_2, b1_s, e2, l2_ready, h2, h2_ready)
                            dve.wait_ge(raw_done, g + 1)
                            nc.vector.tensor_tensor(
                                tiles(message[:, :], D), tiles(ps_raw[0:P, 0:TILES * D], D),
                                b2_s[:, :].unsqueeze(1).to_broadcast([P, TILES, D]),
                                ALU.add).then_inc(message_ready, 1)

                        stages = [(0, indices), (COMPUTE_LAG, repeats)]
                        if mlp:
                            stages.append((COMPUTE_LAG, mlp_steps))
                        rounds(dve, stages, GROUPS)

                    @block.tensor
                    def _(pe):
                        def spread(g, q, turn):
                            pe.wait_ge(indices_ready, g + 1)
                            wait_from(pe, same_ready, g)
                            for j in range(TILES):
                                last = nc.tensor.matmul(ps_seg[0:P, j * P:(j + 1) * P],
                                                        seg_f[q][:, j:j + 1].to_broadcast([P, P]), ident[0:P, 0:P],
                                                        start=True, stop=True)
                            last.then_inc(seg_spread, 1)

                        def pairs(g, q, turn):
                            pe.wait_ge(gather_done[q], 16 * TILES * SIDES * (turn + 1))
                            wait_from(pe, pair_t_ready, g)
                            for j in range(TILES):
                                last = nc.tensor.transpose(ps_pair[0:W, j * P:(j + 1) * P],
                                                           gathered[q][:, j * W:(j + 1) * W], ident[0:P, 0:P])
                            last.then_inc(gathered_used, 1)

                        def layers(g, q, turn):
                            pe.wait_ge(pair_t_ready, g + 1)
                            nc.tensor.matmul(ps_1[:, 0:GW], w0_s[:, :], pair_t[:, :], start=True, stop=True)\
                              .then_inc(pre1_done, 1)
                            pe.wait_ge(h1_ready, g + 1)
                            nc.tensor.matmul(ps_2[:, 0:GW], w1_s[:, :], h1[:, :], start=True, stop=True)\
                              .then_inc(pre2_done, 1)
                            pe.wait_ge(h2_ready, g + 1)
                            for j in range(TILES):
                                last = nc.tensor.matmul(ps_raw[0:P, j * D:(j + 1) * D], h2[:, j * P:(j + 1) * P],
                                                        w2_s[:, :], start=True, stop=True)
                            last.then_inc(raw_done, 1)

                        def merge(g, q, turn):
                            pe.wait_ge(same_ready, g + 1)
                            if mlp:
                                pe.wait_ge(message_ready, g + 1)
                            else:
                                pe.wait_ge(gather_done[q], 16 * TILES * SIDES * (turn + 1))
                            wait_from(pe, summed_ready, g)
                            rows_in = message if mlp else gathered[q]
                            for j in range(TILES):
                                last = nc.tensor.matmul(ps_sum[0:P, j * D:(j + 1) * D],
                                                        same[q % 2][:, j * P:(j + 1) * P],
                                                        rows_in[:, j * D:(j + 1) * D], start=True, stop=True)
                            last.then_inc(merged, 1)
                        stages = [(COMPUTE_LAG, spread)]
                        if mlp:
                            stages += [(COMPUTE_LAG, pairs), (COMPUTE_LAG, layers)]
                        rounds(pe, stages + [(COMPUTE_LAG, merge)], GROUPS)

                    @block.scalar
                    def _(act):
                        def mlp_steps(g, q, turn):
                            act.wait_ge(gathered_used, g + 1)
                            wait_from(act, pre1_done, g)
                            nc.scalar.activation(pair_t[:, :], ps_pair[:, 0:GW], ACT.Copy).then_inc(pair_t_ready, 1)
                            for (t_in, t_ready, e, e_ready, l_ready) in ((t1, t1_ready, e1, e1_ready, l1_ready),
                                                                         (t2, t2_ready, e2, e2_ready, l2_ready)):
                                act.wait_ge(t_ready, g + 1)
                                nc.scalar.activation(e[:, :], t_in[:, :], ACT.Exp).then_inc(e_ready, 1)
                                act.wait_ge(e_ready, g + 1)
                                nc.scalar.activation(e[:, :], e[:, :], ACT.Ln, bias=1.0).then_inc(l_ready, 1)

                        def move(g, q, turn):
                            act.wait_ge(merged, g + 1)
                            for k in range(ACCS):
                                wait_from(act, acc_done[k], 16 * (g - RING + 1) * (TILES // ACCS))
                            nc.scalar.activation(summed[q][:, :], ps_sum[0:P, 0:TILES * D], ACT.Copy)\
                               .then_inc(summed_ready, 1)

                        stages = ([(COMPUTE_LAG, mlp_steps)] if mlp else []) + [(COMPUTE_LAG, move)]
                        rounds(act, stages, GROUPS)

        edge_phase("edges0", h0_t, src_s, acc0, True)
        norm_phase("norm1", [x] + acc0, h1_t, r_t, acc1)
        edge_phase("edges1", h1_t, dst_s, acc1, False)

        z_t = sb("z_t", [128, BLOCKS * TW])
        z_stats = sb("z_stats", [128, BLOCKS * 6])
        with ExitStack() as ph:
            def t(n, shape, k=RING):
                return [ph.enter_context(nc.sbuf_tensor(f"node_{n}_{i}", shape, F32)) for i in range(k)]

            def s(n):
                return ph.enter_context(nc.semaphore(f"node_{n}"))

            parts = [t(f"part{k}", [P, BW]) for k in range(3)]
            z_in, hid = t("z_in", [128, TW], 2), t("hid", [128, TW], 2)
            loaded = [s(f"loaded_{i}") for i in range(RING)]
            accs_summed, z_summed, turned, z_in_ready, pre_done, hid_ready, post_done, z_ready, stats_done = (
                s(n) for n in ("accs_summed", "z_summed", "turned", "z_in_ready", "pre_done", "hid_ready",
                               "post_done", "z_ready", "stats_done"))
            with nc.Block("node_mlp") as block:
                @block.sync
                def _(sp):
                    def load(b, q, turn):
                        wait_from(sp, turned, b - RING + 1, passed_sp)
                        for k, source in enumerate([h1_t] + acc1):
                            sp.dma_start(blk(parts[k][q][:, :]), rows(source, b)).then_inc(loaded[q], 16)
                    rounds(sp, [(0, load)], BLOCKS)

                @block.gpsimd
                def _(pool):
                    def sum_accs(b, q, turn):
                        hold(pool, loaded[q], 16 * 3 * (turn + 1), passed_pool)
                        nc.gpsimd.tensor_tensor(parts[1][q][:, :], parts[1][q][:, :], parts[2][q][:, :],
                                                ALU.add).then_inc(accs_summed, 1)
                    rounds(pool, [(0, sum_accs)], BLOCKS)

                @block.vector
                def _(dve):
                    def add_self(b, q, turn):
                        dve.wait_ge(accs_summed, b + 1)
                        nc.vector.tensor_tensor(parts[0][q][:, :], parts[0][q][:, :], parts[1][q][:, :],
                                                ALU.add).then_inc(z_summed, 1)

                    def stats(b, q, turn):
                        dve.wait_ge(z_ready, b + 1)
                        nc.vector.bn_stats(z_stats[:, bass.ds(b * 6, 6)], z_t[:, bass.ds(b * TW, TW)])\
                          .then_inc(stats_done, 1)
                    rounds(dve, [(0, add_self), (2, stats)], BLOCKS)
                    dve.wait_ge(stats_done, BLOCKS)

                @block.tensor
                def _(pe):
                    def turn_rows(b, q, turn):
                        pe.wait_ge(z_summed, b + 1)
                        wait_from(pe, z_in_ready, b - 1)
                        for j in range(PAIRS):
                            last = nc.tensor.transpose(banks[q % 2][:, j * P:(j + 1) * P],
                                                       parts[0][q][:, j * 2 * D:(j + 1) * 2 * D], ident[0:P, 0:P])
                        last.then_inc(turned, 1)

                    def first(b, q, turn):
                        pe.wait_ge(z_in_ready, b + 1)
                        wait_from(pe, hid_ready, b - 1)
                        nc.tensor.matmul(banks[2 + q % 2][:, 0:TW], gw1_s[:, :], z_in[q % 2][:, :],
                                         start=True, stop=True).then_inc(pre_done, 1)

                    def second(b, q, turn):
                        pe.wait_ge(hid_ready, b + 1)
                        wait_from(pe, z_ready, b - 1)
                        nc.tensor.matmul(banks[4 + q % 2][:, 0:TW], gw2_s[:, :], hid[q % 2][:, :],
                                         start=True, stop=True).then_inc(post_done, 1)
                    rounds(pe, [(0, turn_rows), (1, first), (2, second)], BLOCKS)

                @block.scalar
                def _(act):
                    def take_in(b, q, turn):
                        act.wait_ge(turned, b + 1)
                        wait_from(act, pre_done, b - 1)
                        nc.scalar.activation(z_in[q % 2][:, :], banks[q % 2][:, 0:TW], ACT.Copy)\
                           .then_inc(z_in_ready, 1)

                    def hidden(b, q, turn):
                        act.wait_ge(pre_done, b + 1)
                        wait_from(act, post_done, b - 1)
                        nc.scalar.activation(hid[q % 2][:, :], banks[2 + q % 2][:, 0:TW], ACT.Relu,
                                             bias=gb1_s[:, :]).then_inc(hid_ready, 1)

                    def result(b, q, turn):
                        act.wait_ge(post_done, b + 1)
                        nc.scalar.activation(z_t[:, bass.ds(b * TW, TW)], banks[4 + q % 2][:, 0:TW], ACT.Identity,
                                             bias=gb2_s[:, :]).then_inc(z_ready, 1)
                    rounds(act, [(0, take_in), (1, hidden), (2, result)], BLOCKS)

        with ExitStack() as ph:
            def t(n, shape, k=RING):
                return [ph.enter_context(nc.sbuf_tensor(f"last_{n}_{i}", shape, F32)) for i in range(k)]

            def s(n):
                return ph.enter_context(nc.semaphore(f"last_{n}"))

            halves, both, dev, var2, std, scale, shift = (
                t(n, [128, w], 1)[0] for n, w in (("halves", 2), ("both", 1), ("dev", 1), ("var2", 1),
                                                  ("std", 1), ("scale", 1), ("shift", 1)))
            bn_eps = t("bn_eps", [128, 1], 1)[0]
            resid, outs = t("resid", [P, BW]), t("outs", [P, BW])
            y = t("y", [128, TW], 2)
            stat, mean_ps, var_ps, std_ready, scale_ready = (
                s(n) for n in ("stat", "mean_ps", "var_ps", "std_ready", "scale_ready"))
            loaded, stored = ([s(f"{n}_{i}") for i in range(RING)] for n in ("loaded", "stored"))
            y_ready, turned, out_ready = s("y_ready"), s("turned"), s("out_ready")
            with nc.Block("finish") as block:
                @block.sync
                def _(sp):
                    def load(b, q, turn):
                        wait_from(sp, out_ready, b - RING + 1, passed_sp)
                        sp.dma_start(blk(resid[q][:, :]), rows(r_t, b)).then_inc(loaded[q], 16)

                    def store(b, q, turn):
                        hold(sp, out_ready, b + 1, passed_sp)
                        sp.dma_start(rows(out, b), blk(outs[q][:, :])).then_inc(stored[q], 16)
                    rounds(sp, [(0, load), (3, store)], BLOCKS)
                    for q in range(RING):
                        sp.wait_ge(stored[q], 16 * ((BLOCKS - q + RING - 1) // RING))

                @block.vector
                def _(dve):
                    n = 0
                    nc.vector.memset(bn_eps[:, :], BN_EPS).then_inc(stat, 1)
                    nc.vector.bn_aggr(halves[:, :], z_stats[:, :].rearrange("p (b k) -> p b k", k=6)).then_inc(stat, 1)
                    dve.wait_ge(mean_ps, 1)
                    nc.vector.tensor_copy(both[:, :], banks[6][:, 0:1]).then_inc(stat, 1)
                    dve.wait_ge(stat, 3)
                    nc.vector.tensor_tensor(dev[:, :], halves[:, 0:1], both[:, :], ALU.subtract).then_inc(stat, 1)
                    dve.wait_ge(stat, 4)
                    nc.vector.tensor_tensor(dev[:, :], dev[:, :], dev[:, :], ALU.mult).then_inc(stat, 1)
                    dve.wait_ge(stat, 5)
                    nc.vector.tensor_tensor(var2[:, :], dev[:, :], halves[:, 1:2], ALU.add).then_inc(stat, 1)
                    dve.wait_ge(std_ready, 1)
                    nc.vector.reciprocal(std[:, :], std[:, :]).then_inc(stat, 1)
                    dve.wait_ge(stat, 7)
                    nc.vector.tensor_tensor(scale[:, :], std[:, :], gamma_s[:, :], ALU.mult).then_inc(stat, 1)
                    dve.wait_ge(stat, 8)
                    nc.vector.tensor_tensor(shift[:, :], both[:, :], scale[:, :], ALU.mult).then_inc(stat, 1)
                    dve.wait_ge(stat, 9)
                    nc.vector.tensor_tensor(shift[:, :], beta_s[:, :], shift[:, :], ALU.subtract)\
                      .then_inc(scale_ready, 1)

                    def add(b, q, turn):
                        dve.wait_ge(turned, b + 1)
                        dve.wait_ge(loaded[q], 16 * (turn + 1))
                        wait_from(dve, stored[q], 16 * turn)
                        nc.vector.tensor_tensor(outs[q][:, :], banks[q % 2][0:P, 0:BW], resid[q][:, :], ALU.add)\
                          .then_inc(out_ready, 1)
                    rounds(dve, [(1, add)], BLOCKS)

                @block.tensor
                def _(pe):
                    pe.wait_ge(stat, 2)
                    nc.tensor.matmul(banks[6][:, 0:1], pair_mean[:, :], halves[:, 0:1], start=True, stop=True)\
                      .then_inc(mean_ps, 1)
                    pe.wait_ge(stat, 6)
                    nc.tensor.matmul(banks[7][:, 0:1], pair_mean[:, :], var2[:, :], start=True, stop=True)\
                      .then_inc(var_ps, 1)

                    def turn_back(b, q, turn):
                        pe.wait_ge(y_ready, b + 1)
                        wait_from(pe, out_ready, b - 1)
                        for j in range(PAIRS):
                            last = nc.tensor.transpose(banks[q % 2][0:P, j * 2 * D:(j + 1) * 2 * D],
                                                       y[q % 2][:, j * P:(j + 1) * P], ident[:, :])
                        last.then_inc(turned, 1)
                    rounds(pe, [(0, turn_back)], BLOCKS)

                @block.scalar
                def _(act):
                    act.wait_ge(var_ps, 1)
                    nc.scalar.activation(std[:, :], banks[7][:, 0:1], ACT.Sqrt, bias=bn_eps[:, :])\
                       .then_inc(std_ready, 1)
                    act.wait_ge(scale_ready, 1)

                    def normalise(b, q, turn):
                        wait_from(act, turned, b - 1)
                        nc.scalar.activation(y[q % 2][:, :], z_t[:, bass.ds(b * TW, TW)], ACT.Relu,
                                             bias=shift[:, :], scale=scale[:, :]).then_inc(y_ready, 1)
                    rounds(act, [(0, normalise)], BLOCKS)


_INS = ["x", "src", "dst", "L0_gnn_W0", "L0_gnn_b0", "L0_gnn_W1", "L0_gnn_b1", "L0_gnn_W2", "L0_gnn_b2",
        "L1_gnn_W1", "L1_gnn_b1", "L1_gnn_W2", "L1_gnn_b2", "L1_gnn_gamma", "L1_gnn_beta"]


def kernel(**inputs):
    import numpy as _np
    import concourse.bacc as _bacc
    from concourse import mybir as _mybir
    from concourse.bass_utils import run_bass_kernel_spmd as _run

    nc = _bacc.Bacc("TRN2", target_bir_lowering=False, num_devices=1)
    arrays, args = {}, []
    for name in _INS:
        a = _np.ascontiguousarray(inputs[name])
        arrays[f"in_{name}"] = a
        args.append(nc.dram_tensor(f"in_{name}", a.shape, _mybir.dt.from_np(a.dtype), kind="ExternalInput").ap())
    shape = inputs["x"].shape
    args.append(nc.dram_tensor("out_0", shape, _mybir.dt.float32, kind="ExternalOutput").ap())
    gnn_program(nc, *args)
    r = _run(nc, [arrays], core_ids=[0])
    return r.results[0]["out_0"]
```

```python
import concourse.bass as bass
import concourse.mybir as mybir
from contextlib import ExitStack

F32 = mybir.dt.float32
I32 = mybir.dt.int32
BF16 = mybir.dt.bfloat16
ALU = mybir.AluOpType
ACT = mybir.ActivationFunctionType
AX = mybir.AxisListType

EXP_LN_SET = "natural_log_exp_and_others"
LN_EPS = 1e-5
BN_EPS = 1e-5
SOFTPLUS_CLAMP = 40.0
P = 125
SUBS = 8
TILES = 4
ACCS = 2
RING = 4


def rounds(engine, stages, total, ring=RING):
    last = total + max(lag for lag, _ in stages)

    def step(u, turn, static):
        for lag, body in stages:
            v = u - lag
            slot, t = v % ring, turn + v // ring
            item = t * ring + slot
            if static and not 0 <= item < total:
                continue
            body(item, slot, t)

    head = 2
    tail = total // ring
    for turn in range(head):
        for u in range(ring):
            step(u, turn, True)
    with engine.Fori(head, tail) as turn:
        for u in range(ring):
            step(u, turn, False)
    for s in range(tail * ring, last):
        step(s % ring, s // ring, True)


def hold(engine, semaphore, value, passed):
    engine.wait_ge(semaphore, value)
    if not isinstance(value, int):
        engine.sem_inc(passed, 1)


def wait_from(engine, semaphore, value, passed=None):
    if isinstance(value, int) and value < 1:
        return
    if passed is None:
        engine.wait_ge(semaphore, value)
    else:
        hold(engine, semaphore, value, passed)


def gnn_program(nc, x, src, dst, w0, b0, w1, b1, w2, b2, g_w1, g_b1, g_w2, g_b2, gamma, beta, out):
    N, D = x.shape
    E = src.shape[0]
    HID = w0.shape[1]
    BLOCKS = N // (P * SUBS)
    COLS = E // P
    GROUPS = COLS // TILES
    BW = SUBS * D
    PAIRS = SUBS // 2
    TW = PAIRS * P
    GW = TILES * P
    NB = P * SUBS
    EP = 128
    CT = 9
    RAW = -(-(NB + CT * EP) // EP)
    PAD = -(-RAW * EP // (P * 2)) * P * 2
    FIELDS = 7
    assert N == BLOCKS * P * SUBS and E == COLS * P and COLS == GROUPS * TILES and HID == 2 * D == 128

    h0_t = nc.dram_tensor("h0_table", [N, D], F32).ap()
    h1_t = nc.dram_tensor("h1_table", [N, D], F32).ap()
    r_t = nc.dram_tensor("x1_plus_h1", [N, D], F32).ap()
    own_t = nc.dram_tensor("own_table", [N, D], F32).ap()
    acc0 = [nc.dram_tensor(f"acc0_{k}", [N + 128, D], F32).ap() for k in range(ACCS)]
    acc1 = [nc.dram_tensor(f"acc1_{k}", [N + 128, D], F32).ap() for k in range(ACCS)]

    def rows(table, block):
        return table[bass.ds(block * NB, NB), :].rearrange("(p s) f -> p (s f)", p=P)

    def pair_rows(table, block):
        return table[bass.ds(block * NB, NB), :].rearrange("(t i h) f -> i t (h f)", i=P, h=2)

    def blk(ap):
        return ap.rearrange("p (s f) -> p s f", f=D)

    def pairs_of(ap):
        return ap.rearrange("p (t w) -> p t w", w=2 * D)

    with ExitStack() as ctx:
        def sb(name, shape, dt=F32):
            return ctx.enter_context(nc.sbuf_tensor(name, shape, dt))

        def sem(name):
            return ctx.enter_context(nc.semaphore(name))

        def phase_semaphores(phase, prefix):
            taken = []

            def clear():
                nc.clear_and_free_semaphores(taken)
                nc.all_engine_barrier()
            phase.callback(clear)

            def take(name):
                taken.append(nc.alloc_semaphore(f"{prefix}_{name}"))
                return taken[-1]
            return take

        def bank(name):
            return ctx.enter_context(nc.psum_tensor(name, [128, 512], F32))

        ident = sb("ident", [128, 128])
        earlier = sb("earlier", [128, 128])
        junk_row = sb("junk_row", [128, 1])
        zeros = sb("zeros", [128, 10 * D])
        ln_eps = sb("ln_eps", [P, 1])
        w0_s = sb("w0_s", [128, HID])
        w1_s = sb("w1_s", [HID, HID])
        w2_s = sb("w2_s", [HID, D])
        b0_s = sb("b0_s", [HID, 1])
        b1_s = sb("b1_s", [HID, 1])
        b2_s = sb("b2_s", [128, D])
        gw1_s = sb("gw1_s", [128, 128])
        gw2_s = sb("gw2_s", [128, 128])
        gb1_s = sb("gb1_s", [128, 1])
        gb2_s = sb("gb2_s", [128, 1])
        gamma_s = sb("gamma_s", [128, 1])
        beta_s = sb("beta_s", [128, 1])
        pair_mean = sb("pair_mean", [128, 128])
        ones = sb("ones", [128, 128])
        twice = sb("twice", [P, P])
        iota_row = sb("iota_row", [128, NB])
        iota_tile = sb("iota_tile", [128, BLOCKS * CT])
        block_base = sb("block_base", [128, BLOCKS])
        src_s = sb("src_s", [P, COLS], I32)
        dst_s = sb("dst_s", [P, COLS], I32)

        edge_fields = nc.dram_tensor("edge_fields", [E + PAD, FIELDS], F32).ap()
        block_start = sb("block_start", [128, BLOCKS], I32)
        fast_ok = sb("fast_ok", [128, 1], I32)
        far_src = sb("far_src", [EP, BLOCKS * CT], I32)
        far_local = sb("far_local", [EP, BLOCKS * CT])

        banks = [bank(f"bank{i}") for i in range(8)]

        s_cz, s_ci, s_w, s_pm = sem("const_zeroed"), sem("const_made"), sem("weights_loaded"), sem("pair_mean_made")
        s_gz = sem("diagonal_zeroed")
        passed_sp, passed_pool, passed_act = sem("passed_sp"), sem("passed_pool"), sem("passed_act")
        with nc.Block("setup") as block:
            @block.gpsimd
            def _(pool):
                nc.gpsimd.memset(ident[:, :], 0.0).then_inc(s_cz, 1)
                nc.gpsimd.memset(earlier[:, :], 1.0).then_inc(s_cz, 1)
                nc.gpsimd.memset(pair_mean[:, :], 0.0).then_inc(s_cz, 1)
                nc.gpsimd.memset(ln_eps[:, :], LN_EPS).then_inc(s_cz, 1)
                nc.gpsimd.memset(ones[:, :], 1.0).then_inc(s_cz, 1)
                nc.gpsimd.iota(iota_row[:, :], [[1, NB]], base=0, channel_multiplier=0,
                               allow_small_or_imprecise_dtypes=True).then_inc(s_cz, 1)
                nc.gpsimd.iota(iota_tile[:, :], [[1, BLOCKS * CT]], base=0, channel_multiplier=0,
                               allow_small_or_imprecise_dtypes=True).then_inc(s_cz, 1)
                nc.gpsimd.iota(block_base[:, :], [[NB, BLOCKS]], base=0, channel_multiplier=0,
                               allow_small_or_imprecise_dtypes=True).then_inc(s_cz, 1)
                nc.gpsimd.iota(junk_row[:, :], [[0, 1]], base=N, channel_multiplier=1,
                               allow_small_or_imprecise_dtypes=True).then_inc(s_cz, 1)
                pool.wait_ge(s_cz, 9)
                nc.gpsimd.affine_select(out=ident[:, :], in_=ident[:, :], compare_op=ALU.not_equal, fill=1.0,
                                        base=0, pattern=[[-1, 128]], channel_multiplier=1).then_inc(s_ci, 1)
                nc.gpsimd.affine_select(out=earlier[:, :], in_=earlier[:, :], compare_op=ALU.is_gt, fill=0.0,
                                        base=0, pattern=[[-1, 128]], channel_multiplier=1).then_inc(s_ci, 1)
                for n, off in enumerate((0, D, -D)):
                    if n:
                        pool.wait_ge(s_pm, n)
                    nc.gpsimd.affine_select(out=pair_mean[:, :], in_=pair_mean[:, :], compare_op=ALU.not_equal,
                                            fill=0.5, base=off, pattern=[[-1, 128]],
                                            channel_multiplier=1).then_inc(s_pm, 1)
                pool.wait_ge(s_pm, 3)
                pool.wait_ge(s_ci, 2)

            @block.vector
            def _(dve):
                dve.wait_ge(s_ci, 1)
                nc.vector.tensor_scalar(twice[:, :], ident[0:P, 0:P], 2.0, None, ALU.mult)
                nc.vector.memset(gw1_s[:, :], 0.0).then_inc(s_gz, 1)
                nc.vector.memset(gw2_s[:, :], 0.0).then_inc(s_gz, 1)
                nc.vector.memset(zeros[:, :], 0.0).then_inc(s_gz, 1)

            @block.sync
            def _(sp):
                col = lambda v: v.rearrange("(p a) -> p a", a=1)
                loads = [(w0_s[:, :], w0), (w1_s[:, :], w1), (w2_s[:, :], w2),
                         (b0_s[:, :], col(b0)), (b1_s[:, :], col(b1)),
                         (b2_s[:, :], b2.rearrange("(a f) -> a f", a=1).to_broadcast([128, D])),
                         (src_s[:, :], src.rearrange("(p j) -> p j", p=P)),
                         (dst_s[:, :], dst.rearrange("(p j) -> p j", p=P))]
                for h in (0, D):
                    loads += [(gb1_s[h:h + D, :], col(g_b1)), (gb2_s[h:h + D, :], col(g_b2)),
                              (gamma_s[h:h + D, :], col(gamma)), (beta_s[h:h + D, :], col(beta))]
                for to, fr in loads:
                    sp.dma_start(to, fr).then_inc(s_w, 16)
                sp.wait_ge(s_gz, 3)
                diag = [(gw1_s[h:h + D, h:h + D], g_w1) for h in (0, D)]
                diag += [(gw2_s[h:h + D, h:h + D], g_w2) for h in (0, D)]
                for to, fr in diag:
                    sp.dma_start(to, fr).then_inc(s_w, 16)
                sp.wait_ge(s_w, 16 * (len(loads) + len(diag)))



        def clear_rows(engine, tables, done):
            zw = zeros.shape[1] // D
            count = 0
            for table in tables:
                for r0 in range(0, N, P * zw):
                    engine.dma_start(table[r0:r0 + P * zw, :].rearrange("(p w) f -> p (w f)", p=P),
                                     zeros[0:P, :]).then_inc(done, 16)
                engine.dma_start(table[N:N + 128, :], zeros[:, 0:D]).then_inc(done, 16)
                count += N // (P * zw) + 1
            return count

        def norm_phase(name, sources, table, residual, zeroed, zero_wait=None):
            with ExitStack() as ph:
                def t(n, shape, k=RING):
                    return [ph.enter_context(nc.sbuf_tensor(f"{name}_{n}_{i}", shape, F32)) for i in range(k)]

                s = phase_semaphores(ph, f"{name}")

                def ss(n):
                    return [s(f"{n}_{i}") for i in range(RING)]

                parts = [t(f"part{k}", [P, BW]) for k in range(len(sources))]
                resid = t("resid", [P, BW]) if residual is not None else None
                centred, squared, normed = t("centred", [P, BW]), t("squared", [P, BW]), t("normed", [P, BW])
                mean, var, std, rstd = (t(n, [P, SUBS]) for n in ("mean", "var", "std", "rstd"))
                loaded = ss("loaded")
                table_out, resid_out = ss("table_out"), ss("resid_out")
                zero_out = s("zero_out")
                accs_summed, x_summed = s("accs_summed"), s("x_summed")
                rowsum_done, mean_done, centred_done = s("rowsum_done"), s("mean_done"), s("centred_done")
                squared_done, var_done, std_done = s("squared_done"), s("var_done"), s("std_done")
                rstd_done, normed_done, resid_done = s("rstd_done"), s("normed_done"), s("resid_done")
                summed = len(sources) > 1
                resid_lag = 3

                with nc.Block(name) as block:
                    @block.sync
                    def _(sp):
                        def load(b, q, turn):
                            wait_from(sp, centred_done if residual is None else resid_done, b - RING + 1, passed_sp)
                            for k, source in enumerate(sources):
                                sp.dma_start(parts[k][q][:, :], rows(source, b)).then_inc(loaded[q], 16)
                        rounds(sp, [(0, load)], BLOCKS)

                    @block.gpsimd
                    def _(pool):
                        def sum_accs(b, q, turn):
                            hold(pool, loaded[q], 16 * len(sources) * (turn + 1), passed_pool)
                            nc.gpsimd.tensor_tensor(parts[1][q][:, :], parts[1][q][:, :], parts[2][q][:, :],
                                                    ALU.add).then_inc(accs_summed, 1)

                        def centre(b, q, turn):
                            hold(pool, mean_done, b + 1, passed_pool)
                            wait_from(pool, normed_done, b - RING + 1, passed_pool)
                            nc.gpsimd.tensor_tensor(blk(centred[q][:, :]), blk(parts[0][q][:, :]),
                                                    mean[q][:, :].unsqueeze(2).to_broadcast([P, SUBS, D]),
                                                    ALU.subtract).then_inc(centred_done, 1)

                        def add_resid(b, q, turn):
                            hold(pool, normed_done, b + 1, passed_pool)
                            wait_from(pool, resid_out[q], 16 * turn, passed_pool)
                            nc.gpsimd.tensor_tensor(resid[q][:, :], parts[0][q][:, :], normed[q][:, :],
                                                    ALU.add).then_inc(resid_done, 1)

                        if summed:
                            rounds(pool, [(0, sum_accs), (resid_lag, add_resid)], BLOCKS)
                        else:
                            rounds(pool, [(0, centre)], BLOCKS)

                    @block.vector
                    def _(dve):
                        def centre(b, q, turn):
                            if summed:
                                dve.wait_ge(accs_summed, b + 1)
                                nc.vector.tensor_tensor(parts[0][q][:, :], parts[0][q][:, :], parts[1][q][:, :],
                                                        ALU.add).then_inc(x_summed, 1)
                                dve.wait_ge(x_summed, b + 1)
                            else:
                                dve.wait_ge(loaded[q], 16 * (turn + 1))
                            nc.vector.tensor_reduce(mean[q][:, :], blk(parts[0][q][:, :]), AX.X, ALU.add)\
                              .then_inc(rowsum_done, 1)
                            dve.wait_ge(rowsum_done, b + 1)
                            nc.vector.tensor_scalar(mean[q][:, :], mean[q][:, :], 1.0 / D, None, ALU.mult)\
                              .then_inc(mean_done, 1)
                            if summed:
                                dve.wait_ge(mean_done, b + 1)
                                nc.vector.tensor_tensor(blk(centred[q][:, :]), blk(parts[0][q][:, :]),
                                                        mean[q][:, :].unsqueeze(2).to_broadcast([P, SUBS, D]),
                                                        ALU.subtract).then_inc(centred_done, 1)

                        def variance(b, q, turn):
                            dve.wait_ge(squared_done, b + 1)
                            nc.vector.tensor_reduce(var[q][:, :], blk(squared[q][:, :]), AX.X, ALU.add)\
                              .then_inc(var_done, 1)

                        def normalise(b, q, turn):
                            dve.wait_ge(std_done, b + 1)
                            nc.vector.reciprocal(rstd[q][:, :], std[q][:, :]).then_inc(rstd_done, 1)
                            wait_from(dve, table_out[q], 16 * turn)
                            if summed:
                                wait_from(dve, resid_done, b - RING + 1)
                            dve.wait_ge(rstd_done, b + 1)
                            nc.vector.scalar_tensor_tensor(blk(normed[q][:, :]), blk(centred[q][:, :]), 0.0,
                                                           rstd[q][:, :].unsqueeze(2).to_broadcast([P, SUBS, D]),
                                                           ALU.max, ALU.mult).then_inc(normed_done, 1)

                        rounds(dve, [(0, centre), (1, variance), (2, normalise)], BLOCKS)

                    @block.scalar
                    def _(act):
                        zn = clear_rows(act, zeroed, zero_out)

                        def square(b, q, turn):
                            act.wait_ge(centred_done, b + 1)
                            wait_from(act, var_done, b - RING + 1)
                            nc.scalar.activation(squared[q][:, :], centred[q][:, :], ACT.Square)\
                              .then_inc(squared_done, 1)

                        def deviation(b, q, turn):
                            act.wait_ge(var_done, b + 1)
                            wait_from(act, rstd_done, b - RING + 1)
                            nc.scalar.activation(std[q][:, :], var[q][:, :], ACT.Sqrt, bias=ln_eps[:, :],
                                                 scale=1.0 / D).then_inc(std_done, 1)

                        def store(b, q, turn):
                            hold(act, normed_done, b + 1, passed_act)
                            act.dma_start(rows(table, b), normed[q][:, :]).then_inc(table_out[q], 16)

                        def store_resid(b, q, turn):
                            hold(act, resid_done, b + 1, passed_act)
                            act.dma_start(rows(residual, b), resid[q][:, :]).then_inc(resid_out[q], 16)

                        stages = [(0, square), (1, deviation), (3, store)]
                        if residual is not None:
                            stages.append((resid_lag + 1, store_resid))
                        rounds(act, stages, BLOCKS)
                        if zn:
                            act.wait_ge(zero_out, 16 * zn)
                        if zero_wait:
                            act.wait_ge(*zero_wait)
                        for q in range(RING):
                            n = (BLOCKS - q + RING - 1) // RING
                            act.wait_ge(table_out[q], 16 * n)
                            if residual is not None:
                                act.wait_ge(resid_out[q], 16 * n)

        cleared0 = sem("cleared0")
        cleared0_total = []
        with ExitStack() as ph:
            def whole(n, dt=F32):
                return ph.enter_context(nc.sbuf_tensor(f"survey_{n}", [P, COLS], dt))

            def small(n, w=1, p=P):
                return ph.enter_context(nc.sbuf_tensor(f"survey_{n}", [p, w], F32))

            s = phase_semaphores(ph, "survey")

            next_s, as_int = whole("next_s", I32), whole("as_int", I32)
            (src_f, dst_f, next_f, own, own_upto, own_before, edge, rank, blk_of, next_blk, seam, tile_of, sub_of,
             local, place, far, work, none) = (whole(n) for n in (
                 "src_f", "dst_f", "next_f", "own", "own_upto", "own_before", "edge", "rank", "blk_of", "next_blk",
                 "seam", "tile_of", "sub_of", "local", "place", "far", "work", "none"))
            fields = ph.enter_context(nc.sbuf_tensor("survey_fields", [P, COLS, FIELDS], F32))
            pad = ph.enter_context(nc.sbuf_tensor("survey_pad", [P, PAD // P * FIELDS], F32))
            later = small("later", 128, 128)
            end_of_all = ph.enter_context(nc.sbuf_tensor("survey_end_of_all", [1, 1], I32))
            offset, total, seam_at, seam_blk, first_start, start_step = (
                small(n) for n in ("offset", "total", "seam_at", "seam_blk", "first_start", "start_step"))
            seam_hot, starts = small("seam_hot", BLOCKS), small("starts", BLOCKS, 128)
            faults, fault_sums, fault_sum, total_off = (small("faults", 4), small("fault_sums", 4, 128),
                                                        small("fault_sum", 1, 128), small("total_off", 1, 128))
            s_next, s_end, s_const, s_later, s_chain, s_pe, s_out = (
                s(n) for n in ("next_loaded", "end_made", "const_made", "later_made", "dve_steps", "pe_steps",
                               "fields_out"))
            UPTO, SEAM, FAULTS, PLACED = "upto", "seam", "faults", "placed"
            at_step = {}
            with nc.Block("survey") as block:
                @block.vector
                def _(dve):
                    steps = [0]

                    def link(instruction, mark=None):
                        steps[0] += 1
                        instruction.then_inc(s_chain, 1)
                        dve.wait_ge(s_chain, steps[0])
                        if mark:
                            at_step[mark] = steps[0]

                    V = nc.vector

                    def floor_of(to, value, divisor):
                        link(V.tensor_scalar(as_int[:, :], value, 1.0 / divisor, 0.5 / divisor - 0.5,
                                             ALU.mult, ALU.add))
                        link(V.tensor_copy(to, as_int[:, :]))

                    V.memset(none[:, :], 0.0)
                    V.memset(pad[:, :], -1.0)
                    V.memset(fields[:, :, 6], 1.0)
                    V.tensor_copy(src_f[:, :], src_s[:, :])
                    link(V.tensor_copy(dst_f[:, :], dst_s[:, :]))
                    dve.wait_ge(s_next, 16 * 3)
                    link(V.tensor_copy(next_f[:, :], next_s[:, :]))
                    V.tensor_tensor(own[:, :], src_f[:, :], dst_f[:, :], ALU.is_equal)
                    link(V.tensor_tensor(work[:, :], next_f[:, :], dst_f[:, :], ALU.not_equal))
                    link(V.tensor_tensor(own[:, :], own[:, :], work[:, :], ALU.mult))
                    link(V.tensor_tensor_scan(own_upto[:, :], own[:, :], none[:, :], 0.0, ALU.add, ALU.add), UPTO)
                    V.tensor_scalar(far[:, :], own[:, :], -1.0, 1.0, ALU.mult, ALU.add)
                    floor_of(blk_of[:, :], dst_f[:, :], NB)
                    floor_of(next_blk[:, :], next_f[:, :], NB)
                    dve.wait_ge(s_pe, 1)
                    link(V.tensor_copy(offset[:, :], banks[0][0:P, 0:1]))
                    link(V.scalar_tensor_tensor(own_before[:, :], own_upto[:, :], offset[:, :], own[:, :],
                                                ALU.add, ALU.subtract))
                    dve.wait_ge(s_const, 1)
                    V.tensor_tensor(rank[:, :], edge[:, :], own_before[:, :], ALU.subtract)
                    link(V.tensor_tensor(seam[:, :], next_blk[:, :], blk_of[:, :], ALU.not_equal))
                    link(V.scalar_tensor_tensor(seam[:, :], next_blk[:, :], float(BLOCKS), seam[:, :],
                                                ALU.is_lt, ALU.mult))
                    link(V.scalar_tensor_tensor(work[:, :], edge[:, :], 1.0, seam[:, :], ALU.add, ALU.mult,
                                                accum_out=seam_at[:, :]))
                    link(V.scalar_tensor_tensor(work[:, :], next_blk[:, :], 1.0, seam[:, :], ALU.mult, ALU.mult,
                                                accum_out=seam_blk[:, :]))
                    link(V.tensor_scalar(seam_hot[:, :], iota_row[0:P, 0:BLOCKS], seam_blk[:, :], seam_at[:, :],
                                         ALU.is_equal, ALU.mult), SEAM)
                    dve.wait_ge(s_pe, 2)
                    V.tensor_copy(block_start[:, :], banks[1][:, 0:BLOCKS])
                    link(V.tensor_copy(starts[:, :], banks[1][:, 0:BLOCKS]))
                    link(V.scalar_tensor_tensor(seam_hot[:, :], iota_row[0:P, 0:BLOCKS], blk_of[:, 0:1],
                                                starts[0:P, :], ALU.is_equal, ALU.mult,
                                                accum_out=first_start[:, :]))
                    link(V.tensor_tensor(start_step[:, :], seam_at[:, :], first_start[:, :], ALU.subtract))
                    link(V.tensor_scalar(work[:, :], blk_of[:, :], blk_of[:, 0:1], start_step[:, :],
                                         ALU.subtract, ALU.mult))
                    link(V.scalar_tensor_tensor(work[:, :], work[:, :], first_start[:, :], rank[:, :],
                                                ALU.add, ALU.subtract))
                    link(V.scalar_tensor_tensor(place[:, :], blk_of[:, :], float(NB), work[:, :],
                                                ALU.mult, ALU.subtract))
                    V.scalar_tensor_tensor(local[:, :], blk_of[:, :], -float(NB), dst_f[:, :], ALU.mult, ALU.add)
                    floor_of(tile_of[:, :], place[:, :], EP)
                    floor_of(sub_of[:, :], local[:, :], P)
                    V.scalar_tensor_tensor(fields[:, :, 1], tile_of[:, :], -float(EP), place[:, :], ALU.mult, ALU.add)
                    link(V.scalar_tensor_tensor(work[:, :], blk_of[:, :], float(CT), tile_of[:, :],
                                                ALU.mult, ALU.add))
                    link(V.scalar_tensor_tensor(work[:, :], work[:, :], 1.0, far[:, :], ALU.add, ALU.mult))
                    V.tensor_scalar(fields[:, :, 0], work[:, :], -1.0, None, ALU.add)
                    floor_of(fields[:, :, 2], src_f[:, :], 256)
                    V.scalar_tensor_tensor(fields[:, :, 3], fields[:, :, 2], -256.0, src_f[:, :], ALU.mult, ALU.add)
                    floor_of(fields[:, :, 4], local[:, :], 256)
                    link(V.scalar_tensor_tensor(fields[:, :, 5], fields[:, :, 4], -256.0, local[:, :],
                                                ALU.mult, ALU.add), PLACED)
                    V.tensor_tensor(place[:, :], own_before[:, :], dst_f[:, :], ALU.not_equal)
                    link(V.tensor_tensor(sub_of[:, :], sub_of[:, :], tile_of[:, :], ALU.subtract))
                    link(V.tensor_tensor(sub_of[:, :], sub_of[:, :], sub_of[:, :], ALU.mult))
                    for n, (in0, scalar, op0, in1, op1) in enumerate((
                            (place, 1.0, ALU.mult, own, ALU.mult), (next_f, 0.0, ALU.add, dst_f, ALU.is_lt),
                            (sub_of, 1.5, ALU.is_gt, far, ALU.mult), (tile_of, CT - 0.5, ALU.is_gt, far, ALU.mult))):
                        link(V.scalar_tensor_tensor(work[:, :], in0[:, :], scalar, in1[:, :], op0, op1,
                                                    accum_out=faults[:, n:n + 1]), FAULTS)
                    dve.wait_ge(s_pe, 3)
                    link(V.tensor_copy(fault_sums[:, :], banks[2][:, 0:4]))
                    V.tensor_scalar(total_off[:, :], banks[0][:, 1:2], float(N), None, ALU.not_equal)
                    link(V.tensor_reduce(fault_sum[:, :], fault_sums[:, :], AX.X, ALU.add))
                    link(V.tensor_tensor(fault_sum[:, :], fault_sum[:, :], total_off[:, :], ALU.add))
                    link(V.tensor_scalar(fast_ok[:, :], fault_sum[:, :], 0.0, None, ALU.is_equal))

                @block.tensor
                def _(pe):
                    pe.wait_ge(s_later, 1)
                    pe.wait_ge(s_chain, at_step[UPTO])
                    nc.tensor.matmul(banks[0][:, 0:1], later[0:P, :], own_upto[:, COLS - 1:COLS], start=True, stop=True)
                    nc.tensor.matmul(banks[0][:, 1:2], ones[0:P, :], own_upto[:, COLS - 1:COLS],
                                     start=True, stop=True).then_inc(s_pe, 1)
                    pe.wait_ge(s_chain, at_step[SEAM])
                    nc.tensor.matmul(banks[1][:, 0:BLOCKS], ones[0:P, :], seam_hot[:, :],
                                     start=True, stop=True).then_inc(s_pe, 1)
                    pe.wait_ge(s_chain, at_step[FAULTS])
                    nc.tensor.matmul(banks[2][:, 0:4], ones[0:P, :], faults[:, :],
                                     start=True, stop=True).then_inc(s_pe, 1)

                @block.scalar
                def _(act):
                    cleared0_total.append(16 * clear_rows(act, acc0, cleared0))

                @block.gpsimd
                def _(pool):
                    nc.gpsimd.iota(end_of_all[:, :], [[0, 1]], base=N, channel_multiplier=0).then_inc(s_end, 1)
                    nc.gpsimd.iota(edge[:, :], [[1, COLS]], base=0, channel_multiplier=COLS,
                                   allow_small_or_imprecise_dtypes=True).then_inc(s_const, 1)
                    nc.gpsimd.affine_select(out=later[:, :], in_=ones[:, :], compare_op=ALU.is_gt, fill=0.0,
                                            base=0, pattern=[[1, 128]], channel_multiplier=-1).then_inc(s_later, 1)

                @block.sync
                def _(sp):
                    sp.dma_start(next_s[0:P - 1, :], dst[1:1 + (P - 1) * COLS].rearrange("(p j) -> p j", j=COLS))\
                      .then_inc(s_next, 16)
                    sp.dma_start(next_s[P - 1:P, 0:COLS - 1], dst[1 + (P - 1) * COLS:E].rearrange("(p j) -> p j", p=1))\
                      .then_inc(s_next, 16)
                    sp.wait_ge(s_end, 1)
                    sp.dma_start(next_s[P - 1:P, COLS - 1:COLS], end_of_all[:, :]).then_inc(s_next, 16)
                    sp.wait_ge(s_chain, at_step[PLACED])
                    sp.dma_start(edge_fields[0:E, :].rearrange("(p j) k -> p (j k)", p=P),
                                 fields[:, :, :].rearrange("p j k -> p (j k)")).then_inc(s_out, 16)
                    sp.dma_start(edge_fields[E:E + PAD, :].rearrange("(p j) k -> p (j k)", p=P), pad[:, :])\
                      .then_inc(s_out, 16)
                    sp.wait_ge(s_out, 32)

        norm_phase("norm0", [x], h0_t, None, [], (cleared0, cleared0_total[0]))

        def edge_phase(name, table, seg_s, accs, mlp):
            with ExitStack() as ph:
                def t(n, shape, k=RING, dt=F32):
                    return [ph.enter_context(nc.sbuf_tensor(f"{name}_{n}_{i}", shape, dt)) for i in range(k)]

                s = phase_semaphores(ph, f"{name}")

                def ss(n):
                    return [s(f"{n}_{i}") for i in range(RING)]

                SIDES = 2 if mlp else 1
                W = SIDES * D
                src_i, dst_i, put_i = (t(n, [P, TILES], RING, I32) for n in ("src_i", "dst_i", "put_i"))
                seg_f = t("seg_f", [P, TILES])
                repeat_n, to_junk = t("repeat_n", [P, TILES]), t("to_junk", [P, TILES])
                gathered = t("gathered", [P, TILES * W])
                same, same_earlier = t("same", [P, GW], 2), t("same_earlier", [P, GW], 2)
                summed = t("summed", [P, TILES * D])
                indices_ready, same_ready, put_ready = s("indices_ready"), s("same_ready"), s("put_ready")
                seg_spread, same_masked, repeats_counted, junk_offset, junk_scaled = (
                    s(n) for n in ("seg_spread", "same_masked", "repeats_counted", "junk_offset", "junk_scaled"))
                gather_done = ss("gather_done")
                acc_done = [s(f"acc_done_{k}") for k in range(ACCS)]
                merged, summed_ready = s("merged"), s("summed_ready")
                gathered_used = s("gathered_used")
                if mlp:
                    pair_t, t1, e1, h1, t2, e2, h2 = (t(n, [128, GW], 1)[0] for n in
                                                      ("pair_t", "t1", "e1", "h1", "t2", "e2", "h2"))
                    message = t("message", [P, TILES * D], 1)[0]
                    (pair_t_ready, pre1_done, t1_ready, e1_ready, l1_ready, h1_ready, pre2_done, t2_ready,
                     e2_ready, l2_ready, h2_ready, raw_done, message_ready) = (s(n) for n in (
                         "pair_t_ready", "pre1_done", "t1_ready", "e1_ready", "l1_ready", "h1_ready", "pre2_done",
                         "t2_ready", "e2_ready", "l2_ready", "h2_ready", "raw_done", "message_ready"))
                ps_seg, ps_pair, ps_1, ps_2, ps_raw, ps_sum = (banks[i] for i in range(6))
                SCATTER_LAG = 2
                COMPUTE_LAG = 2

                def tiles(ap, w):
                    return ap.rearrange("p (j w) -> p j w", w=w)

                with nc.Block(name) as block:
                    @block.gpsimd
                    def _(pool):
                        def gather(j):
                            def body(g, q, turn):
                                if j == 0:
                                    hold(pool, indices_ready, g + 1, passed_pool)
                                    wait_from(pool, gathered_used if mlp else merged, g - RING + 1, passed_pool)
                                for side in range(SIDES):
                                    idx = (src_i, dst_i)[side][q][:, j:j + 1]
                                    at = j * W + side * D
                                    pool.indirect_dma_start(
                                        gathered[q][:, at:at + D], None, table,
                                        bass.IndirectOffsetOnAxis(ap=idx, axis=0)).then_inc(gather_done[q], 16)
                            return body

                        def scatter(j):
                            def body(g, q, turn):
                                if j == 0:
                                    hold(pool, summed_ready, g + 1, passed_pool)
                                    hold(pool, put_ready, g + 1, passed_pool)
                                k = j % ACCS
                                wait_from(pool, acc_done[k], 16 * (g * (TILES // ACCS) + j // ACCS), passed_pool)
                                pool.indirect_dma_start(
                                    accs[k], bass.IndirectOffsetOnAxis(ap=put_i[q][:, j:j + 1], axis=0),
                                    summed[q][:, j * D:(j + 1) * D], None, compute_op=ALU.add)\
                                    .then_inc(acc_done[k], 16)
                            return body

                        steps = []
                        for j in range(TILES):
                            steps += [(0, gather(j)), (SCATTER_LAG, scatter(j))]
                        rounds(pool, steps, GROUPS)
                        for k in range(ACCS):
                            pool.wait_ge(acc_done[k], 16 * GROUPS * TILES // ACCS)

                    @block.vector
                    def _(dve):
                        def indices(g, q, turn):
                            wait_from(dve, gather_done[q], 16 * TILES * SIDES * turn)
                            wait_from(dve, seg_spread, g - RING + 1)
                            at = bass.ds(g * TILES, TILES)
                            nc.vector.tensor_copy(src_i[q][:, :], src_s[:, at])
                            if mlp:
                                nc.vector.tensor_copy(dst_i[q][:, :], dst_s[:, at])
                            nc.vector.tensor_copy(seg_f[q][:, :], seg_s[:, at]).then_inc(indices_ready, 1)

                        def repeats(g, q, turn):
                            r = q % 2
                            dve.wait_ge(seg_spread, g + 1)
                            wait_from(dve, merged, g - 1)
                            nc.vector.tensor_tensor(
                                tiles(same[r][:, :], P), tiles(ps_seg[0:P, 0:GW], P),
                                seg_f[q][:, :].unsqueeze(2).to_broadcast([P, TILES, P]),
                                ALU.is_equal).then_inc(same_ready, 1)
                            dve.wait_ge(same_ready, g + 1)
                            nc.vector.tensor_tensor(
                                tiles(same_earlier[r][:, :], P), tiles(same[r][:, :], P),
                                earlier[0:P, 0:P].unsqueeze(1).to_broadcast([P, TILES, P]),
                                ALU.mult).then_inc(same_masked, 1)
                            dve.wait_ge(same_masked, g + 1)
                            nc.vector.tensor_reduce(repeat_n[q][:, :], tiles(same_earlier[r][:, :], P), AX.X,
                                                    ALU.add).then_inc(repeats_counted, 1)
                            nc.vector.scalar_tensor_tensor(
                                to_junk[q][:, :], seg_f[q][:, :], -1.0, junk_row[0:P, :].to_broadcast([P, TILES]),
                                ALU.mult, ALU.add).then_inc(junk_offset, 1)
                            dve.wait_ge(repeats_counted, g + 1)
                            dve.wait_ge(junk_offset, g + 1)
                            nc.vector.scalar_tensor_tensor(
                                to_junk[q][:, :], repeat_n[q][:, :], 1.0, to_junk[q][:, :],
                                ALU.min, ALU.mult).then_inc(junk_scaled, 1)
                            dve.wait_ge(junk_scaled, g + 1)
                            for k in range(ACCS):
                                wait_from(dve, acc_done[k], 16 * (g - RING + 1) * (TILES // ACCS))
                            nc.vector.tensor_tensor(put_i[q][:, :], to_junk[q][:, :], seg_f[q][:, :],
                                                    ALU.add).then_inc(put_ready, 1)

                        def clamp(g, psum, bias, to, done, pre):
                            dve.wait_ge(pre, g + 1)
                            nc.vector.tensor_scalar(to[:, :], psum[:, 0:GW], bias[:, :], SOFTPLUS_CLAMP,
                                                    ALU.add, ALU.min).then_inc(done, 1)

                        def softplus(g, psum, bias, ln, ln_done, to, done):
                            dve.wait_ge(ln_done, g + 1)
                            nc.vector.scalar_tensor_tensor(to[:, :], psum[:, 0:GW], bias[:, :], ln[:, :],
                                                           ALU.add, ALU.max).then_inc(done, 1)

                        def mlp_steps(g, q, turn):
                            clamp(g, ps_1, b0_s, t1, t1_ready, pre1_done)
                            softplus(g, ps_1, b0_s, e1, l1_ready, h1, h1_ready)
                            clamp(g, ps_2, b1_s, t2, t2_ready, pre2_done)
                            softplus(g, ps_2, b1_s, e2, l2_ready, h2, h2_ready)
                            dve.wait_ge(raw_done, g + 1)
                            nc.vector.tensor_tensor(
                                tiles(message[:, :], D), tiles(ps_raw[0:P, 0:TILES * D], D),
                                b2_s[0:P, :].unsqueeze(1).to_broadcast([P, TILES, D]),
                                ALU.add).then_inc(message_ready, 1)

                        stages = [(0, indices), (COMPUTE_LAG, repeats)]
                        if mlp:
                            stages.append((COMPUTE_LAG, mlp_steps))
                        rounds(dve, stages, GROUPS)

                    @block.tensor
                    def _(pe):
                        def spread(g, q, turn):
                            pe.wait_ge(indices_ready, g + 1)
                            wait_from(pe, same_ready, g)
                            for j in range(TILES):
                                last = nc.tensor.matmul(ps_seg[0:P, j * P:(j + 1) * P],
                                                        seg_f[q][:, j:j + 1].to_broadcast([P, P]), ident[0:P, 0:P],
                                                        start=True, stop=True)
                            last.then_inc(seg_spread, 1)

                        def pairs(g, q, turn):
                            pe.wait_ge(gather_done[q], 16 * TILES * SIDES * (turn + 1))
                            wait_from(pe, pair_t_ready, g)
                            for j in range(TILES):
                                last = nc.tensor.transpose(ps_pair[0:W, j * P:(j + 1) * P],
                                                           gathered[q][:, j * W:(j + 1) * W], ident[0:P, 0:P])
                            last.then_inc(gathered_used, 1)

                        def layers(g, q, turn):
                            pe.wait_ge(pair_t_ready, g + 1)
                            nc.tensor.matmul(ps_1[:, 0:GW], w0_s[:, :], pair_t[:, :], start=True, stop=True)\
                              .then_inc(pre1_done, 1)
                            pe.wait_ge(h1_ready, g + 1)
                            nc.tensor.matmul(ps_2[:, 0:GW], w1_s[:, :], h1[:, :], start=True, stop=True)\
                              .then_inc(pre2_done, 1)
                            pe.wait_ge(h2_ready, g + 1)
                            for j in range(TILES):
                                last = nc.tensor.matmul(ps_raw[0:P, j * D:(j + 1) * D], h2[:, j * P:(j + 1) * P],
                                                        w2_s[:, :], start=True, stop=True)
                            last.then_inc(raw_done, 1)

                        def merge(g, q, turn):
                            pe.wait_ge(same_ready, g + 1)
                            if mlp:
                                pe.wait_ge(message_ready, g + 1)
                            else:
                                pe.wait_ge(gather_done[q], 16 * TILES * SIDES * (turn + 1))
                            wait_from(pe, summed_ready, g)
                            rows_in = message if mlp else gathered[q]
                            for j in range(TILES):
                                last = nc.tensor.matmul(ps_sum[0:P, j * D:(j + 1) * D],
                                                        same[q % 2][:, j * P:(j + 1) * P],
                                                        rows_in[:, j * D:(j + 1) * D], start=True, stop=True)
                            last.then_inc(merged, 1)
                        stages = [(COMPUTE_LAG, spread)]
                        if mlp:
                            stages += [(COMPUTE_LAG, pairs), (COMPUTE_LAG, layers)]
                        rounds(pe, stages + [(COMPUTE_LAG, merge)], GROUPS)

                    @block.scalar
                    def _(act):
                        def mlp_steps(g, q, turn):
                            act.wait_ge(gathered_used, g + 1)
                            wait_from(act, pre1_done, g)
                            nc.scalar.activation(pair_t[:, :], ps_pair[:, 0:GW], ACT.Copy).then_inc(pair_t_ready, 1)
                            for (t_in, t_ready, e, e_ready, l_ready) in ((t1, t1_ready, e1, e1_ready, l1_ready),
                                                                         (t2, t2_ready, e2, e2_ready, l2_ready)):
                                act.wait_ge(t_ready, g + 1)
                                nc.scalar.activation(e[:, :], t_in[:, :], ACT.Exp).then_inc(e_ready, 1)
                                act.wait_ge(e_ready, g + 1)
                                nc.scalar.activation(e[:, :], e[:, :], ACT.Ln, bias=1.0).then_inc(l_ready, 1)

                        def move(g, q, turn):
                            act.wait_ge(merged, g + 1)
                            for k in range(ACCS):
                                wait_from(act, acc_done[k], 16 * (g - RING + 1) * (TILES // ACCS))
                            nc.scalar.activation(summed[q][:, :], ps_sum[0:P, 0:TILES * D], ACT.Copy)\
                               .then_inc(summed_ready, 1)

                        if mlp:
                            act.preload_act_table_set(EXP_LN_SET)
                        stages = ([(COMPUTE_LAG, mlp_steps)] if mlp else []) + [(COMPUTE_LAG, move)]
                        rounds(act, stages, GROUPS)

        z_t = sb("z_t", [128, BLOCKS * TW])
        z_stats = sb("z_stats", [128, BLOCKS * 6])

        def node_phase():
            with ExitStack() as ph:
                def t(n, shape, k=RING):
                    return [ph.enter_context(nc.sbuf_tensor(f"node_{n}_{i}", shape, F32)) for i in range(k)]

                s = phase_semaphores(ph, "node")

                parts = [t(f"part{k}", [P, BW]) for k in range(3)]
                z_in, hid = t("z_in", [128, TW], 2), t("hid", [128, TW], 2)
                loaded = [s(f"loaded_{i}") for i in range(RING)]
                accs_summed, z_summed, turned, z_in_ready, pre_done, hid_ready, post_done, z_ready, stats_done = (
                    s(n) for n in ("accs_summed", "z_summed", "turned", "z_in_ready", "pre_done", "hid_ready",
                                   "post_done", "z_ready", "stats_done"))
                with nc.Block("node_mlp") as block:
                    @block.sync
                    def _(sp):
                        def load(b, q, turn):
                            wait_from(sp, turned, b - RING + 1, passed_sp)
                            for k, source in enumerate([h1_t] + acc1):
                                sp.dma_start(pairs_of(parts[k][q][:, :]), pair_rows(source, b)).then_inc(loaded[q], 16)
                        rounds(sp, [(0, load)], BLOCKS)

                    @block.gpsimd
                    def _(pool):
                        def sum_accs(b, q, turn):
                            hold(pool, loaded[q], 16 * 3 * (turn + 1), passed_pool)
                            nc.gpsimd.tensor_tensor(parts[1][q][:, :], parts[1][q][:, :], parts[2][q][:, :],
                                                    ALU.add).then_inc(accs_summed, 1)
                        rounds(pool, [(0, sum_accs)], BLOCKS)

                    @block.vector
                    def _(dve):
                        def add_self(b, q, turn):
                            dve.wait_ge(accs_summed, b + 1)
                            nc.vector.tensor_tensor(parts[0][q][:, :], parts[0][q][:, :], parts[1][q][:, :],
                                                    ALU.add).then_inc(z_summed, 1)

                        def stats(b, q, turn):
                            dve.wait_ge(z_ready, b + 1)
                            nc.vector.bn_stats(z_stats[:, bass.ds(b * 6, 6)], z_t[:, bass.ds(b * TW, TW)])\
                              .then_inc(stats_done, 1)
                        rounds(dve, [(0, add_self), (2, stats)], BLOCKS)
                        dve.wait_ge(stats_done, BLOCKS)

                    @block.tensor
                    def _(pe):
                        def turn_rows(b, q, turn):
                            pe.wait_ge(z_summed, b + 1)
                            wait_from(pe, z_in_ready, b - 1)
                            for j in range(PAIRS):
                                last = nc.tensor.transpose(banks[q % 2][:, j * P:(j + 1) * P],
                                                           parts[0][q][:, j * 2 * D:(j + 1) * 2 * D], ident[0:P, 0:P])
                            last.then_inc(turned, 1)

                        def first(b, q, turn):
                            pe.wait_ge(z_in_ready, b + 1)
                            wait_from(pe, hid_ready, b - 1)
                            nc.tensor.matmul(banks[2 + q % 2][:, 0:TW], gw1_s[:, :], z_in[q % 2][:, :],
                                             start=True, stop=True).then_inc(pre_done, 1)

                        def second(b, q, turn):
                            pe.wait_ge(hid_ready, b + 1)
                            wait_from(pe, z_ready, b - 1)
                            nc.tensor.matmul(banks[4 + q % 2][:, 0:TW], gw2_s[:, :], hid[q % 2][:, :],
                                             start=True, stop=True).then_inc(post_done, 1)
                        rounds(pe, [(0, turn_rows), (1, first), (2, second)], BLOCKS)

                    @block.scalar
                    def _(act):
                        def take_in(b, q, turn):
                            act.wait_ge(turned, b + 1)
                            wait_from(act, pre_done, b - 1)
                            nc.scalar.activation(z_in[q % 2][:, :], banks[q % 2][:, 0:TW], ACT.Copy)\
                               .then_inc(z_in_ready, 1)

                        def hidden(b, q, turn):
                            act.wait_ge(pre_done, b + 1)
                            wait_from(act, post_done, b - 1)
                            nc.scalar.activation(hid[q % 2][:, :], banks[2 + q % 2][:, 0:TW], ACT.Relu,
                                                 bias=gb1_s[:, :]).then_inc(hid_ready, 1)

                        def result(b, q, turn):
                            act.wait_ge(post_done, b + 1)
                            nc.scalar.activation(z_t[:, bass.ds(b * TW, TW)], banks[4 + q % 2][:, 0:TW], ACT.Identity,
                                                 bias=gb2_s[:, :]).then_inc(z_ready, 1)
                        rounds(act, [(0, take_in), (1, hidden), (2, result)], BLOCKS)

        def fast_edges0():
            GT = 3
            GK = CT // GT
            FW = GT * EP
            HALF = SUBS // 2
            UNITS = (("own", 0), ("far", 0), ("far", 1), ("own", 1), ("far", 2))
            NU = len(UNITS)
            assert FIELDS - 2 == 5
            with ExitStack() as ph:
                def t(n, shape, k, dt=F32):
                    return [ph.enter_context(nc.sbuf_tensor(f"fast0_{n}_{i}", shape, dt)) for i in range(k)]

                s = phase_semaphores(ph, "fast0")

                raw = t("raw", [EP, RAW * FIELDS], 2)
                row_hot = t("row_hot", [EP, RAW * EP], 2, BF16)
                tile_hot = t("tile_hot", [EP, RAW * CT], 2)
                spread_out = t("spread_out", [EP, RAW * CT * 5], 2, BF16)
                packed = t("packed", [EP, CT * 5], 1)[0]
                gather_i = t("gather_i", [EP, 2 * CT], 2, I32)
                filled_f, src_f, local_f, seg_f = (t(n, [EP, CT], 2) for n in ("filled_f", "src_f", "local_f", "seg_f"))
                put_i = t("put_i", [EP, GT], 2 * GK, I32)
                repeat_n, to_junk = t("repeat_n", [EP, GT], 2 * GK), t("to_junk", [EP, GT], 2 * GK)
                gathered = t("gathered", [EP, GT * 2 * D], 2 * GK)
                same, same_earlier = t("same", [EP, FW], 2), t("same_earlier", [EP, FW], 2)
                summed = t("summed", [EP, GT * D], 2 * GK)
                own_rows, own_x, own_out = (t(n, [P, BW], 2) for n in ("own_rows", "own_x", "own_out"))
                own_bias = t("own_bias", [P, BW], 2)
                in_t, t1, e1, h1, t2, e2, h2 = (t(n, [128, 512], 1)[0] for n in
                                                ("in_t", "t1", "e1", "h1", "t2", "e2", "h2"))
                message = t("message", [EP, GT * D], 1)[0]
                w0_own = t("w0_own", [128, 2 * HID], 1)[0]
                w0_parts = t("w0_parts", [128, HID], 2)
                raw_loaded, rows_loaded, x_loaded, own_stored = (
                    [s(f"{n}_{i}") for i in range(2)] for n in ("raw_loaded", "rows_loaded", "x_loaded", "own_stored"))
                gather_done = [s(f"gather_done_{i}") for i in range(2 * GK)]
                acc_done = [s(f"acc_done_{k}") for k in range(ACCS)]
                (w_zeroed, w_loaded, w_ready, tile_hot_ready, spread_ready, packed_done, packed_copied, nodes_ready, seg_filled,
                 indices_ready, seg_spread, same_ready, same_masked, repeats_counted, junk_offset, junk_scaled,
                 put_ready, turned, in_ready, pre1_done, t1_ready, e1_ready, l1_ready, h1_ready, pre2_done, t2_ready,
                 e2_ready, l2_ready, h2_ready, raw_done, message_ready, merged, summed_ready, own_bias_ready) = (
                     s(n) for n in (
                         "w_zeroed", "w_loaded", "w_ready", "tile_hot_ready", "spread_ready", "packed_done", "packed_copied",
                         "nodes_ready", "seg_filled", "indices_ready", "seg_spread", "same_ready", "same_masked",
                         "repeats_counted", "junk_offset", "junk_scaled", "put_ready", "turned", "in_ready",
                         "pre1_done", "t1_ready", "e1_ready", "l1_ready", "h1_ready", "pre2_done", "t2_ready",
                         "e2_ready", "l2_ready", "h2_ready", "raw_done", "message_ready", "merged", "summed_ready",
                         "own_bias_ready"))
                ps_seg, ps_in, ps_1, ps_2, ps_raw, ps_sum, ps_packed = (banks[i] for i in range(7))

                def cols(ap, w):
                    return ap.rearrange("p (j w) -> p j w", w=w)

                def width(i):
                    return FW if UNITS[i][0] == "far" else HALF * P

                def unit_stages(order, lag):
                    out = []
                    for i in range(NU):
                        for back, body in order(i, (i - 1) % NU, (i - 2) % NU):
                            out.append((lag + (1 if i < back else 0), body))
                    return out

                def scatters_over(engine, b, turn, q, k):
                    tile = 2 * CT * (turn - 1) + CT * q + GT * k + GT - 1
                    whole, odd = CT * (turn - 1), CT * q + GT * k + GT - 1
                    for a in range(ACCS):
                        wait_from(engine, acc_done[a], 16 * (whole + (odd + 2 - a) // 2),
                                  passed_pool if engine is nc.gpsimd else None)

                with nc.Block("fast_edges0") as block:
                    @block.sync
                    def _(sp):
                        for h in (0, D):
                            for k in range(2):
                                sp.dma_start(w0_parts[k][h:h + D, :], w0[k * D:(k + 1) * D, :]).then_inc(w_loaded, 16)

                        def load_raw(b, q, turn):
                            wait_from(sp, spread_ready, b - 1, passed_sp)
                            start = sp.value_load(block_start[0:1, bass.ds(b, 1)], min_val=0, max_val=E)
                            sp.dma_start(raw[q][:, :], edge_fields[bass.ds(start, RAW * EP), :]
                                         .rearrange("(p t) k -> p (t k)", p=EP)).then_inc(raw_loaded[q], 16)

                        def load_rows(b, q, turn):
                            wait_from(sp, turned, NU * (b - 2) + 4, passed_sp)
                            sp.dma_start(own_rows[q][:, :], rows(h0_t, b)).then_inc(rows_loaded[q], 16)
                            wait_from(sp, own_bias_ready, b - 1, passed_sp)
                            sp.dma_start(own_x[q][:, :], rows(x, b)).then_inc(x_loaded[q], 16)

                        def store_own(b, q, turn):
                            hold(sp, message_ready, NU * b + 4, passed_sp)
                            sp.dma_start(rows(own_t, b), own_out[q][:, :]).then_inc(own_stored[q], 16)
                        rounds(sp, [(0, load_raw), (0, load_rows), (2, store_own)], BLOCKS, 2)
                        for q in range(2):
                            sp.wait_ge(own_stored[q], 16 * (BLOCKS // 2))

                    @block.gpsimd
                    def _(pool):
                        def gather(n):
                            k, j = divmod(n, GT)

                            def body(b, q, turn):
                                slot = q * GK + k
                                if n == 0:
                                    hold(pool, indices_ready, b + 1, passed_pool)
                                if j == 0:
                                    i = UNITS.index(("far", k))
                                    wait_from(pool, turned, NU * (b - 2) + i + 1, passed_pool)
                                for side in range(2):
                                    at = (2 * j + side) * D
                                    pool.indirect_dma_start(
                                        gathered[slot][:, at:at + D], None, h0_t,
                                        bass.IndirectOffsetOnAxis(ap=gather_i[q][:, side * CT + n:side * CT + n + 1],
                                                                  axis=0)).then_inc(gather_done[slot], 16)
                            return body

                        def scatter(n):
                            k, j = divmod(n, GT)

                            def body(b, q, turn):
                                slot = q * GK + k
                                if j == 0:
                                    hold(pool, summed_ready, GK * b + k + 1, passed_pool)
                                    hold(pool, put_ready, GK * b + k + 1, passed_pool)
                                a = (CT * q + n) % ACCS
                                wait_from(pool, acc_done[a], 16 * (CT * turn + (CT * q + n) // ACCS), passed_pool)
                                pool.indirect_dma_start(
                                    acc0[a], bass.IndirectOffsetOnAxis(ap=put_i[slot][:, j:j + 1], axis=0),
                                    summed[slot][:, j * D:(j + 1) * D], None, compute_op=ALU.add)\
                                    .then_inc(acc_done[a], 16)
                            return body
                        steps = []
                        for n in range(CT):
                            steps += [(0, gather(n)), (1, scatter(n))]
                        rounds(pool, steps, BLOCKS, 2)
                        for a in range(ACCS):
                            pool.wait_ge(acc_done[a], 16 * BLOCKS * CT // ACCS)

                    @block.vector
                    def _(dve):
                        V = nc.vector
                        V.memset(w0_own[:, :], 0.0).then_inc(w_zeroed, 1)
                        dve.wait_ge(w_zeroed, 1)
                        dve.wait_ge(w_loaded, 64)
                        for h in range(2):
                            half = slice(h * D, (h + 1) * D)
                            V.tensor_tensor(w0_own[half, h * HID:(h + 1) * HID], w0_parts[0][half, :],
                                            w0_parts[1][half, :], ALU.add).then_inc(w_ready, 1)

                        def compact(b, q, turn):
                            dve.wait_ge(raw_loaded[q], 16 * (turn + 1))
                            wait_from(dve, packed_done, b - 1)
                            f = cols(raw[q][:, :], FIELDS)
                            V.tensor_tensor(
                                cols(tile_hot[q][:, :], CT), f[:, :, 0:1].to_broadcast([EP, RAW, CT]),
                                iota_tile[:, bass.ds(b * CT, CT)].unsqueeze(1).to_broadcast([EP, RAW, CT]),
                                ALU.is_equal).then_inc(tile_hot_ready, 1)
                            V.tensor_tensor(
                                cols(row_hot[q][:, :], EP), f[:, :, 1:2].to_broadcast([EP, RAW, EP]),
                                iota_row[:, 0:EP].unsqueeze(1).to_broadcast([EP, RAW, EP]), ALU.is_equal)
                            dve.wait_ge(tile_hot_ready, b + 1)
                            V.tensor_tensor(
                                spread_out[q][:, :].rearrange("p (t c k) -> p t c k", c=CT, k=5),
                                cols(tile_hot[q][:, :], CT).unsqueeze(3).to_broadcast([EP, RAW, CT, 5]),
                                f[:, :, 2:7].unsqueeze(2).to_broadcast([EP, RAW, CT, 5]),
                                ALU.mult).then_inc(spread_ready, 1)

                        def unpack(b, q, turn):
                            dve.wait_ge(packed_done, b + 1)
                            V.tensor_copy(packed[:, :], ps_packed[:, 0:CT * 5]).then_inc(packed_copied, 1)
                            dve.wait_ge(packed_copied, b + 1)
                            f = cols(packed[:, :], 5)
                            for slot in range(GK):
                                wait_from(dve, gather_done[q * GK + slot], 96 * turn)
                            wait_from(dve, seg_spread, GK * (b - 1))
                            V.scalar_tensor_tensor(src_f[q][:, :], f[:, :, 0], 256.0, f[:, :, 1], ALU.mult, ALU.add)
                            V.scalar_tensor_tensor(local_f[q][:, :], f[:, :, 2], 256.0, f[:, :, 3], ALU.mult, ALU.add)
                            V.scalar_tensor_tensor(filled_f[q][:, :], f[:, :, 4], -1.0,
                                                   ones[:, 0:CT], ALU.mult, ALU.add).then_inc(nodes_ready, 1)
                            dve.wait_ge(nodes_ready, b + 1)
                            V.tensor_copy(gather_i[q][:, 0:CT], src_f[q][:, :])
                            V.tensor_copy(far_src[:, bass.ds(b * CT, CT)], src_f[q][:, :])
                            V.tensor_tensor(gather_i[q][:, CT:2 * CT], local_f[q][:, :],
                                            block_base[:, bass.ds(b, 1)].to_broadcast([EP, CT]), ALU.add)
                            V.tensor_tensor(far_local[:, bass.ds(b * CT, CT)], local_f[q][:, :], filled_f[q][:, :],
                                            ALU.subtract)
                            V.scalar_tensor_tensor(seg_f[q][:, :], filled_f[q][:, :], junk_row[:, :], src_f[q][:, :],
                                                   ALU.mult, ALU.add).then_inc(indices_ready, 1)

                        def bias(b, q, turn):
                            dve.wait_ge(x_loaded[q], 16 * (turn + 1))
                            wait_from(dve, message_ready, NU * (b - 2) + 4)
                            V.tensor_tensor(blk(own_bias[q][:, :]), blk(own_x[q][:, :]),
                                            b2_s[0:P, :].unsqueeze(1).to_broadcast([P, SUBS, D]),
                                            ALU.add).then_inc(own_bias_ready, 1)

                        def clamp(i, psum, b_s, to, read, done, pre):
                            def body(b, q, turn):
                                dve.wait_ge(pre, NU * b + i + 1)
                                wait_from(dve, read, NU * b + i)
                                w = width(i)
                                V.tensor_scalar(to[:, 0:w], psum[:, 0:w], b_s[:, :], SOFTPLUS_CLAMP,
                                                ALU.add, ALU.min).then_inc(done, 1)
                            return body

                        def softplus(i, psum, b_s, ln, ln_done, to, read, done):
                            def body(b, q, turn):
                                dve.wait_ge(ln_done, NU * b + i + 1)
                                wait_from(dve, read, NU * b + i)
                                w = width(i)
                                V.scalar_tensor_tensor(to[:, 0:w], psum[:, 0:w], b_s[:, :], ln[:, 0:w],
                                                       ALU.add, ALU.max).then_inc(done, 1)
                            return body

                        def repeats(k):
                            def body(b, q, turn):
                                g, slot, r = GK * b + k, q * GK + k, (q + k) % 2
                                mine = seg_f[q][:, k * GT:(k + 1) * GT]
                                dve.wait_ge(seg_spread, g + 1)
                                wait_from(dve, merged, g - 1)
                                V.tensor_tensor(cols(same[r][:, :], EP), cols(ps_seg[:, 0:FW], EP),
                                                mine.unsqueeze(2).to_broadcast([EP, GT, EP]),
                                                ALU.is_equal).then_inc(same_ready, 1)
                                V.scalar_tensor_tensor(to_junk[slot][:, :], mine, -1.0,
                                                       junk_row[:, :].to_broadcast([EP, GT]),
                                                       ALU.mult, ALU.add).then_inc(junk_offset, 1)
                                dve.wait_ge(same_ready, g + 1)
                                V.tensor_tensor(cols(same_earlier[r][:, :], EP), cols(same[r][:, :], EP),
                                                earlier[:, :].unsqueeze(1).to_broadcast([EP, GT, EP]),
                                                ALU.mult).then_inc(same_masked, 1)
                                dve.wait_ge(same_masked, g + 1)
                                V.tensor_reduce(repeat_n[slot][:, :], cols(same_earlier[r][:, :], EP), AX.X,
                                                ALU.add).then_inc(repeats_counted, 1)
                                dve.wait_ge(repeats_counted, g + 1)
                                dve.wait_ge(junk_offset, g + 1)
                                V.scalar_tensor_tensor(to_junk[slot][:, :], repeat_n[slot][:, :], 1.0,
                                                       to_junk[slot][:, :], ALU.min, ALU.mult).then_inc(junk_scaled, 1)
                                dve.wait_ge(junk_scaled, g + 1)
                                scatters_over(dve, b, turn, q, k)
                                V.tensor_tensor(put_i[slot][:, :], to_junk[slot][:, :], mine, ALU.add)\
                                 .then_inc(put_ready, 1)
                            return body

                        def result(i):
                            kind, k = UNITS[i]

                            def body(b, q, turn):
                                dve.wait_ge(raw_done, NU * b + i + 1)
                                if kind == "own":
                                    dve.wait_ge(own_bias_ready, b + 1)
                                    wait_from(dve, own_stored[q], 16 * turn)
                                    at = slice(k * HALF * D, (k + 1) * HALF * D)
                                    V.tensor_tensor(own_out[q][:, at], ps_raw[0:P, 0:HALF * D], own_bias[q][:, at],
                                                    ALU.add).then_inc(message_ready, 1)
                                else:
                                    wait_from(dve, merged, GK * b + k)
                                    V.tensor_tensor(cols(message[:, :], D), cols(ps_raw[:, 0:GT * D], D),
                                                    b2_s[:, :].unsqueeze(1).to_broadcast([EP, GT, D]),
                                                    ALU.add).then_inc(message_ready, 1)
                            return body

                        def order(i, p, pp):
                            out = [(1, clamp(p, ps_2, b1_s, t2, e2_ready, t2_ready, pre2_done)),
                                   (0, clamp(i, ps_1, b0_s, t1, e1_ready, t1_ready, pre1_done))]
                            if UNITS[p][0] == "far":
                                out.append((1, repeats(UNITS[p][1])))
                            out += [(1, softplus(p, ps_2, b1_s, e2, l2_ready, h2, raw_done, h2_ready)),
                                    (0, softplus(i, ps_1, b0_s, e1, l1_ready, h1, pre2_done, h1_ready)),
                                    (1, result(p))]
                            return out
                        stages = unit_stages(order, 1)
                        stages[12:12] = [(0, unpack)]
                        stages[2:2] = [(0, compact)]
                        rounds(dve, [(1, bias)] + stages, BLOCKS, 2)

                    @block.tensor
                    def _(pe):
                        M, T = nc.tensor.matmul, nc.tensor.transpose

                        def pack(b, q, turn):
                            pe.wait_ge(spread_ready, b + 1)
                            wait_from(pe, packed_copied, b)
                            for n in range(RAW):
                                last = M(ps_packed[:, 0:CT * 5], row_hot[q][:, n * EP:(n + 1) * EP],
                                         spread_out[q][:, n * CT * 5:(n + 1) * CT * 5],
                                         start=(n == 0), stop=(n == RAW - 1))
                            last.then_inc(packed_done, 1)

                        def turn_rows(i):
                            kind, k = UNITS[i]

                            def body(b, q, turn):
                                if kind == "own":
                                    pe.wait_ge(rows_loaded[q], 16 * (turn + 1))
                                else:
                                    pe.wait_ge(gather_done[q * GK + k], 96 * (turn + 1))
                                wait_from(pe, in_ready, NU * b + i)
                                if kind == "own":
                                    for j in range(HALF // 2):
                                        at = (k * HALF + 2 * j) * D
                                        last = T(ps_in[:, j * P:(j + 1) * P], own_rows[q][:, at:at + 2 * D],
                                                 ident[0:P, 0:P])
                                else:
                                    for j in range(GT):
                                        last = T(ps_in[:, j * EP:(j + 1) * EP],
                                                 gathered[q * GK + k][:, 2 * j * D:2 * (j + 1) * D], ident[:, :])
                                last.then_inc(turned, 1)
                            return body

                        def layer1(i):
                            def body(b, q, turn):
                                pe.wait_ge(in_ready, NU * b + i + 1)
                                wait_from(pe, h1_ready, NU * b + i)
                                if UNITS[i][0] == "own":
                                    w = HALF // 2 * P
                                    for h in range(2):
                                        last = M(ps_1[:, h * w:(h + 1) * w], w0_own[:, h * HID:(h + 1) * HID],
                                                 in_t[:, 0:w], start=True, stop=True)
                                else:
                                    last = M(ps_1[:, 0:FW], w0_s[:, :], in_t[:, 0:FW], start=True, stop=True)
                                last.then_inc(pre1_done, 1)
                            return body

                        def layer2(i):
                            def body(b, q, turn):
                                pe.wait_ge(h1_ready, NU * b + i + 1)
                                wait_from(pe, h2_ready, NU * b + i)
                                w = width(i)
                                M(ps_2[:, 0:w], w1_s[:, :], h1[:, 0:w], start=True, stop=True).then_inc(pre2_done, 1)
                            return body

                        def layer3(i):
                            def body(b, q, turn):
                                pe.wait_ge(h2_ready, NU * b + i + 1)
                                wait_from(pe, message_ready, NU * b + i)
                                if UNITS[i][0] == "own":
                                    for j in range(HALF):
                                        at = (j % 2 * (HALF // 2) + j // 2) * P
                                        last = M(ps_raw[0:P, j * D:(j + 1) * D], h2[:, at:at + P], w2_s[:, :],
                                                 start=True, stop=True)
                                else:
                                    for j in range(GT):
                                        last = M(ps_raw[:, j * D:(j + 1) * D], h2[:, j * EP:(j + 1) * EP], w2_s[:, :],
                                                 start=True, stop=True)
                                last.then_inc(raw_done, 1)
                            return body

                        def spread(k):
                            def body(b, q, turn):
                                g = GK * b + k
                                if k == 0:
                                    pe.wait_ge(indices_ready, b + 1)
                                wait_from(pe, same_ready, g)
                                for j in range(GT):
                                    n = k * GT + j
                                    last = M(ps_seg[:, j * EP:(j + 1) * EP],
                                             seg_f[q][:, n:n + 1].to_broadcast([EP, EP]), ident[:, :],
                                             start=True, stop=True)
                                last.then_inc(seg_spread, 1)
                            return body

                        def merge(k):
                            i = UNITS.index(("far", k))

                            def body(b, q, turn):
                                g = GK * b + k
                                pe.wait_ge(same_ready, g + 1)
                                pe.wait_ge(message_ready, NU * b + i + 1)
                                wait_from(pe, summed_ready, g)
                                for j in range(GT):
                                    last = M(ps_sum[:, j * D:(j + 1) * D], same[(q + k) % 2][:, j * EP:(j + 1) * EP],
                                             message[:, j * D:(j + 1) * D], start=True, stop=True)
                                last.then_inc(merged, 1)
                            return body

                        def order(i, p, pp):
                            out = [(0, turn_rows(i)), (1, layer2(p)), (0, layer1(i))]
                            if UNITS[pp][0] == "far":
                                out.append((2, merge(UNITS[pp][1])))
                            if UNITS[i][0] == "far":
                                out.append((0, spread(UNITS[i][1])))
                            out.append((1, layer3(p)))
                            return out
                        pe.wait_ge(w_ready, 2)
                        stages = unit_stages(order, 1)
                        stages[5:5] = [(0, pack)]
                        rounds(pe, stages, BLOCKS, 2)

                    @block.scalar
                    def _(act):
                        A = nc.scalar.activation

                        def take_in(i):
                            def body(b, q, turn):
                                act.wait_ge(turned, NU * b + i + 1)
                                wait_from(act, pre1_done, NU * b + i)
                                w = FW if UNITS[i][0] == "far" else HALF // 2 * P
                                A(in_t[:, 0:w], ps_in[:, 0:w], ACT.Copy).then_inc(in_ready, 1)
                            return body

                        def exp_ln(i, t_in, t_ready, e, read, e_ready, l_ready):
                            def body(b, q, turn):
                                act.wait_ge(t_ready, NU * b + i + 1)
                                wait_from(act, read, NU * b + i)
                                w = width(i)
                                A(e[:, 0:w], t_in[:, 0:w], ACT.Exp).then_inc(e_ready, 1)
                                act.wait_ge(e_ready, NU * b + i + 1)
                                A(e[:, 0:w], e[:, 0:w], ACT.Ln, bias=1.0).then_inc(l_ready, 1)
                            return body

                        def move(k):
                            def body(b, q, turn):
                                act.wait_ge(merged, GK * b + k + 1)
                                scatters_over(act, b, turn, q, k)
                                A(summed[q * GK + k][:, :], ps_sum[:, 0:GT * D], ACT.Copy).then_inc(summed_ready, 1)
                            return body

                        def order(i, p, pp):
                            out = [(0, take_in(i)), (1, exp_ln(p, t2, t2_ready, e2, h2_ready, e2_ready, l2_ready)),
                                   (0, exp_ln(i, t1, t1_ready, e1, h1_ready, e1_ready, l1_ready))]
                            if UNITS[pp][0] == "far":
                                out.append((2, move(UNITS[pp][1])))
                            return out
                        act.preload_act_table_set(EXP_LN_SET)
                        rounds(act, unit_stages(order, 1), BLOCKS, 2)

        def fast_edges1():
            reach = [(max(0, c - 1) // 2, (min(SUBS - 1, c + 1)) // 2 + 1) for c in range(CT)]
            reach_at = [sum(hi - lo for lo, hi in reach[:c]) * 2 * P for c in range(CT)]
            HOT = sum(hi - lo for lo, hi in reach) * 2 * P
            with ExitStack() as ph:
                def t(n, shape, k=2, dt=F32):
                    return [ph.enter_context(nc.sbuf_tensor(f"fast1_{n}_{i}", shape, dt)) for i in range(k)]

                s = phase_semaphores(ph, "fast1")

                index_i = t("index_i", [EP, CT], 2, I32)
                gathered, hot = t("gathered", [EP, CT * D]), t("hot", [EP, HOT])
                self_rows = t("self_rows", [P, BW])
                z_in, hid = t("z_in", [128, TW]), t("hid", [128, TW])
                gather_done, self_loaded = ([s(f"{n}_{i}") for i in range(2)] for n in ("gather_done", "self_loaded"))
                (index_ready, hot_ready, nodes_summed, z_in_ready, pre_done, hid_ready, post_done,
                 z_ready, stats_done) = (s(n) for n in (
                     "index_ready", "hot_ready", "nodes_summed", "z_in_ready", "pre_done",
                     "hid_ready", "post_done", "z_ready", "stats_done"))
                with nc.Block("fast_edges1") as block:
                    @block.sync
                    def _(sp):
                        def load(b, q, turn):
                            wait_from(sp, nodes_summed, b - 1, passed_sp)
                            sp.dma_start(pairs_of(self_rows[q][:, :]), pair_rows(h1_t, b)).then_inc(self_loaded[q], 16)
                        rounds(sp, [(0, load)], BLOCKS, 2)

                    @block.gpsimd
                    def _(pool):
                        def gather(b, q, turn):
                            hold(pool, index_ready, b + 1, passed_pool)
                            wait_from(pool, nodes_summed, b - 1, passed_pool)
                            for c in range(CT):
                                pool.indirect_dma_start(
                                    gathered[q][:, c * D:(c + 1) * D], None, h1_t,
                                    bass.IndirectOffsetOnAxis(ap=index_i[q][:, c:c + 1], axis=0))\
                                    .then_inc(gather_done[q], 16)
                        rounds(pool, [(0, gather)], BLOCKS, 2)

                    @block.vector
                    def _(dve):
                        V = nc.vector

                        def index(b, q, turn):
                            wait_from(dve, gather_done[q], 16 * CT * turn)
                            V.tensor_copy(index_i[q][:, :], far_src[:, bass.ds(b * CT, CT)]).then_inc(index_ready, 1)

                        def one_hot(b, q, turn):
                            wait_from(dve, nodes_summed, b - 1)
                            for c, (lo, hi) in enumerate(reach):
                                last = V.tensor_scalar(
                                    hot[q][:, reach_at[c]:reach_at[c] + (hi - lo) * 2 * P],
                                    iota_row[:, lo * 2 * P:hi * 2 * P],
                                    far_local[:, bass.ds(b * CT + c, 1)], None, ALU.is_equal)
                            last.then_inc(hot_ready, 1)

                        def stats(b, q, turn):
                            dve.wait_ge(z_ready, b + 1)
                            V.bn_stats(z_stats[:, bass.ds(b * 6, 6)], z_t[:, bass.ds(b * TW, TW)])\
                             .then_inc(stats_done, 1)
                        rounds(dve, [(0, index), (0, one_hot), (3, stats)], BLOCKS, 2)
                        dve.wait_ge(stats_done, BLOCKS)

                    @block.tensor
                    def _(pe):
                        def sum_nodes(b, q, turn):
                            pe.wait_ge(hot_ready, b + 1)
                            pe.wait_ge(gather_done[q], 16 * CT * (turn + 1))
                            pe.wait_ge(self_loaded[q], 16 * (turn + 1))
                            wait_from(pe, z_in_ready, b - 1)
                            for t in range(PAIRS):
                                at = slice(t * P, (t + 1) * P)
                                nc.tensor.matmul(banks[6 + q][:, at], self_rows[q][:, t * 2 * D:(t + 1) * 2 * D],
                                                 twice[:, :], start=True, stop=False)
                                tiles = [c for c in range(CT) if reach[c][0] <= t < reach[c][1]]
                                for c in tiles:
                                    hot_at = reach_at[c] + (t - reach[c][0]) * 2 * P
                                    ends = hot[q][:, hot_at:hot_at + 2 * P].rearrange("p (i h) -> p h i", h=2)
                                    for h in range(2):
                                        last = nc.tensor.matmul(
                                            banks[6 + q][h * D:(h + 1) * D, at],
                                            gathered[q][:, c * D:(c + 1) * D], ends[:, h, :],
                                            start=False, stop=(c == tiles[-1]))
                            last.then_inc(nodes_summed, 1)

                        def first(b, q, turn):
                            pe.wait_ge(z_in_ready, b + 1)
                            wait_from(pe, hid_ready, b - 1)
                            nc.tensor.matmul(banks[2 + q][:, 0:TW], gw1_s[:, :], z_in[q][:, :],
                                             start=True, stop=True).then_inc(pre_done, 1)

                        def second(b, q, turn):
                            pe.wait_ge(hid_ready, b + 1)
                            wait_from(pe, z_ready, b - 1)
                            nc.tensor.matmul(banks[4 + q][:, 0:TW], gw2_s[:, :], hid[q][:, :],
                                             start=True, stop=True).then_inc(post_done, 1)
                        rounds(pe, [(1, first), (2, second), (0, sum_nodes)], BLOCKS, 2)

                    @block.scalar
                    def _(act):
                        def take_in(b, q, turn):
                            act.wait_ge(nodes_summed, b + 1)
                            wait_from(act, pre_done, b - 1)
                            nc.scalar.activation(z_in[q][:, :], banks[6 + q][:, 0:TW], ACT.Copy).then_inc(z_in_ready, 1)

                        def hidden(b, q, turn):
                            act.wait_ge(pre_done, b + 1)
                            wait_from(act, post_done, b - 1)
                            nc.scalar.activation(hid[q][:, :], banks[2 + q][:, 0:TW], ACT.Relu,
                                                 bias=gb1_s[:, :]).then_inc(hid_ready, 1)

                        def result(b, q, turn):
                            act.wait_ge(post_done, b + 1)
                            nc.scalar.activation(z_t[:, bass.ds(b * TW, TW)], banks[4 + q][:, 0:TW], ACT.Identity,
                                                 bias=gb2_s[:, :]).then_inc(z_ready, 1)
                        rounds(act, [(0, take_in), (1, hidden), (2, result)], BLOCKS, 2)

        stat, mean_ps, var_ps, std_ready, scale_ready = (
            sem(f"last_{n}") for n in ("stat", "mean_ps", "var_ps", "std_ready", "scale_ready"))
        loaded, stored = ([sem(f"last_{n}_{i}") for i in range(RING)] for n in ("loaded", "stored"))
        y_ready, turned, out_ready = (sem(f"last_{n}") for n in ("y_ready", "turned", "out_ready"))

        fast = nc.values_load(fast_ok[0:1, 0:1], min_val=0, max_val=1)
        with nc.If(fast == 1):
            fast_edges0()
            norm_phase("fast_norm1", [own_t] + acc0, h1_t, r_t, [])
            fast_edges1()
        with nc.Else():
            edge_phase("edges0", h0_t, src_s, acc0, True)
            norm_phase("norm1", [x] + acc0, h1_t, r_t, acc1)
            edge_phase("edges1", h1_t, dst_s, acc1, False)
            node_phase()

        with ExitStack() as ph:
            def t(n, shape, k=RING):
                return [ph.enter_context(nc.sbuf_tensor(f"last_{n}_{i}", shape, F32)) for i in range(k)]

            halves, both, dev, var2, std, scale, shift = (
                t(n, [128, w], 1)[0] for n, w in (("halves", 2), ("both", 1), ("dev", 1), ("var2", 1),
                                                  ("std", 1), ("scale", 1), ("shift", 1)))
            bn_eps = t("bn_eps", [128, 1], 1)[0]
            resid, outs = t("resid", [P, BW]), t("outs", [P, BW])
            y = t("y", [128, TW], 2)
            with nc.Block("finish") as block:
                @block.sync
                def _(sp):
                    def load(b, q, turn):
                        wait_from(sp, out_ready, b - RING + 1, passed_sp)
                        sp.dma_start(pairs_of(resid[q][:, :]), pair_rows(r_t, b)).then_inc(loaded[q], 16)

                    rounds(sp, [(0, load)], BLOCKS)

                @block.vector
                def _(dve):
                    n = 0
                    nc.vector.memset(bn_eps[:, :], BN_EPS).then_inc(stat, 1)
                    nc.vector.bn_aggr(halves[:, :], z_stats[:, :].rearrange("p (b k) -> p b k", k=6)).then_inc(stat, 1)
                    dve.wait_ge(mean_ps, 1)
                    nc.vector.tensor_copy(both[:, :], banks[6][:, 0:1]).then_inc(stat, 1)
                    dve.wait_ge(stat, 3)
                    nc.vector.tensor_tensor(dev[:, :], halves[:, 0:1], both[:, :], ALU.subtract).then_inc(stat, 1)
                    dve.wait_ge(stat, 4)
                    nc.vector.tensor_tensor(dev[:, :], dev[:, :], dev[:, :], ALU.mult).then_inc(stat, 1)
                    dve.wait_ge(stat, 5)
                    nc.vector.tensor_tensor(var2[:, :], dev[:, :], halves[:, 1:2], ALU.add).then_inc(stat, 1)
                    dve.wait_ge(std_ready, 1)
                    nc.vector.reciprocal(std[:, :], std[:, :]).then_inc(stat, 1)
                    dve.wait_ge(stat, 7)
                    nc.vector.tensor_tensor(scale[:, :], std[:, :], gamma_s[:, :], ALU.mult).then_inc(stat, 1)
                    dve.wait_ge(stat, 8)
                    nc.vector.tensor_tensor(shift[:, :], both[:, :], scale[:, :], ALU.mult).then_inc(stat, 1)
                    dve.wait_ge(stat, 9)
                    nc.vector.tensor_tensor(shift[:, :], beta_s[:, :], shift[:, :], ALU.subtract)\
                      .then_inc(scale_ready, 1)

                    def add(b, q, turn):
                        dve.wait_ge(turned, b + 1)
                        dve.wait_ge(loaded[q], 16 * (turn + 1))
                        wait_from(dve, stored[q], 16 * turn)
                        nc.vector.tensor_tensor(outs[q][:, :], banks[q % 2][0:P, 0:BW], resid[q][:, :], ALU.add)\
                          .then_inc(out_ready, 1)
                    rounds(dve, [(1, add)], BLOCKS)

                @block.tensor
                def _(pe):
                    pe.wait_ge(stat, 2)
                    nc.tensor.matmul(banks[6][:, 0:1], pair_mean[:, :], halves[:, 0:1], start=True, stop=True)\
                      .then_inc(mean_ps, 1)
                    pe.wait_ge(stat, 6)
                    nc.tensor.matmul(banks[7][:, 0:1], pair_mean[:, :], var2[:, :], start=True, stop=True)\
                      .then_inc(var_ps, 1)

                    def turn_back(b, q, turn):
                        pe.wait_ge(y_ready, b + 1)
                        wait_from(pe, out_ready, b - 1)
                        for j in range(PAIRS):
                            last = nc.tensor.transpose(banks[q % 2][0:P, j * 2 * D:(j + 1) * 2 * D],
                                                       y[q % 2][:, j * P:(j + 1) * P], ident[:, :])
                        last.then_inc(turned, 1)
                    rounds(pe, [(0, turn_back)], BLOCKS)

                @block.scalar
                def _(act):
                    act.wait_ge(var_ps, 1)
                    nc.scalar.activation(std[:, :], banks[7][:, 0:1], ACT.Sqrt, bias=bn_eps[:, :])\
                       .then_inc(std_ready, 1)
                    act.wait_ge(scale_ready, 1)

                    def normalise(b, q, turn):
                        wait_from(act, turned, b - 1)
                        nc.scalar.activation(y[q % 2][:, :], z_t[:, bass.ds(b * TW, TW)], ACT.Relu,
                                             bias=shift[:, :], scale=scale[:, :]).then_inc(y_ready, 1)

                    def store(b, q, turn):
                        hold(act, out_ready, b + 1, passed_act)
                        act.dma_start(pair_rows(out, b), pairs_of(outs[q][:, :])).then_inc(stored[q], 16)
                    rounds(act, [(0, normalise), (2, store)], BLOCKS)
                    for q in range(RING):
                        act.wait_ge(stored[q], 16 * ((BLOCKS - q + RING - 1) // RING))


_INS = ["x", "src", "dst", "L0_gnn_W0", "L0_gnn_b0", "L0_gnn_W1", "L0_gnn_b1", "L0_gnn_W2", "L0_gnn_b2",
        "L1_gnn_W1", "L1_gnn_b1", "L1_gnn_W2", "L1_gnn_b2", "L1_gnn_gamma", "L1_gnn_beta"]


def kernel(**inputs):
    import numpy as _np
    import concourse.bacc as _bacc
    from concourse import mybir as _mybir
    from concourse.bass_utils import run_bass_kernel_spmd as _run

    nc = _bacc.Bacc("TRN2", target_bir_lowering=False, num_devices=1)
    arrays, args = {}, []
    for name in _INS:
        a = _np.ascontiguousarray(inputs[name])
        arrays[f"in_{name}"] = a
        args.append(nc.dram_tensor(f"in_{name}", a.shape, _mybir.dt.from_np(a.dtype), kind="ExternalInput").ap())
    shape = inputs["x"].shape
    args.append(nc.dram_tensor("out_0", shape, _mybir.dt.float32, kind="ExternalOutput").ap())
    gnn_program(nc, *args)
    r = _run(nc, [arrays], core_ids=[0])
    return r.results[0]["out_0"]
```

```python
import concourse.bass as bass
import concourse.mybir as mybir
from contextlib import ExitStack

F32 = mybir.dt.float32
I32 = mybir.dt.int32
BF16 = mybir.dt.bfloat16
ALU = mybir.AluOpType
ACT = mybir.ActivationFunctionType
AX = mybir.AxisListType

EXP_LN_SET = "natural_log_exp_and_others"
LN_EPS = 1e-5
BN_EPS = 1e-5
SOFTPLUS_CLAMP = 40.0
P = 125
SUBS = 8
TILES = 4
ACCS = 2
RING = 4


def rounds(engine, stages, total, ring=RING):
    last = total + max(lag for lag, _ in stages)

    def step(u, turn, static):
        for lag, body in stages:
            v = u - lag
            slot, t = v % ring, turn + v // ring
            item = t * ring + slot
            if static and not 0 <= item < total:
                continue
            body(item, slot, t)

    head = 1 + max(1, -(-max(lag for lag, _ in stages) // ring))
    tail = total // ring
    for turn in range(head):
        for u in range(ring):
            step(u, turn, True)
    with engine.Fori(head, tail) as turn:
        for u in range(ring):
            step(u, turn, False)
    for s in range(tail * ring, last):
        step(s % ring, s // ring, True)


def hold(engine, semaphore, value, passed):
    engine.wait_ge(semaphore, value)
    if not isinstance(value, int):
        engine.sem_inc(passed, 1)


def wait_from(engine, semaphore, value, passed=None):
    if isinstance(value, int) and value < 1:
        return
    if passed is None:
        engine.wait_ge(semaphore, value)
    else:
        hold(engine, semaphore, value, passed)


def gnn_program(nc, x, src, dst, w0, b0, w1, b1, w2, b2, g_w1, g_b1, g_w2, g_b2, gamma, beta, out):
    N, D = x.shape
    E = src.shape[0]
    HID = w0.shape[1]
    BLOCKS = N // (P * SUBS)
    COLS = E // P
    GROUPS = COLS // TILES
    BW = SUBS * D
    PAIRS = SUBS // 2
    TW = PAIRS * P
    GW = TILES * P
    NB = P * SUBS
    EP = 128
    CT = 9
    RAW = -(-(NB + CT * EP) // EP)
    PAD = -(-RAW * EP // (P * 2)) * P * 2
    FIELDS = 7
    assert N == BLOCKS * P * SUBS and E == COLS * P and COLS == GROUPS * TILES and HID == 2 * D == 128

    h0_t = nc.dram_tensor("h0_table", [N, D], F32).ap()
    h1_t = nc.dram_tensor("h1_table", [N, D], F32).ap()
    r_t = nc.dram_tensor("x1_plus_h1", [N, D], F32).ap()
    own_t = nc.dram_tensor("own_table", [N, D], F32).ap()
    acc0 = [nc.dram_tensor(f"acc0_{k}", [N + 128, D], F32).ap() for k in range(ACCS)]
    acc1 = [nc.dram_tensor(f"acc1_{k}", [N + 128, D], F32).ap() for k in range(ACCS)]

    def rows(table, block):
        return table[bass.ds(block * NB, NB), :].rearrange("(p s) f -> p (s f)", p=P)

    def pair_rows(table, block):
        return table[bass.ds(block * NB, NB), :].rearrange("(t i h) f -> i t (h f)", i=P, h=2)

    def blk(ap):
        return ap.rearrange("p (s f) -> p s f", f=D)

    def pairs_of(ap):
        return ap.rearrange("p (t w) -> p t w", w=2 * D)

    with ExitStack() as ctx:
        def sb(name, shape, dt=F32):
            return ctx.enter_context(nc.sbuf_tensor(name, shape, dt))

        def sem(name):
            return ctx.enter_context(nc.semaphore(name))

        def phase_semaphores(phase, prefix):
            taken = []

            def clear():
                nc.clear_and_free_semaphores(taken)
                nc.all_engine_barrier()
            phase.callback(clear)

            def take(name):
                taken.append(nc.alloc_semaphore(f"{prefix}_{name}"))
                return taken[-1]
            return take

        def bank(name):
            return ctx.enter_context(nc.psum_tensor(name, [128, 512], F32))

        ident = sb("ident", [128, 128])
        earlier = sb("earlier", [128, 128])
        up_to = sb("up_to", [128, 128])
        ident_b = sb("ident_b", [128, 128], BF16)
        iota_b = sb("iota_b", [128, 128], BF16)
        junk_row = sb("junk_row", [128, 1])
        zeros = sb("zeros", [128, 10 * D])
        ln_eps = sb("ln_eps", [P, 1])
        w0_s = sb("w0_s", [128, HID])
        w1_s = sb("w1_s", [HID, HID])
        w2_s = sb("w2_s", [HID, D])
        b0_s = sb("b0_s", [HID, 1])
        b1_s = sb("b1_s", [HID, 1])
        b2_s = sb("b2_s", [128, D])
        gw1_s = sb("gw1_s", [128, 128])
        gw2_s = sb("gw2_s", [128, 128])
        gb1_s = sb("gb1_s", [128, 1])
        gb2_s = sb("gb2_s", [128, 1])
        gamma_s = sb("gamma_s", [128, 1])
        beta_s = sb("beta_s", [128, 1])
        pair_mean = sb("pair_mean", [128, 128])
        ones = sb("ones", [128, 128])
        twice = sb("twice", [P, P])
        iota_row = sb("iota_row", [128, NB])
        iota_tile = sb("iota_tile", [128, BLOCKS * CT])
        block_base = sb("block_base", [128, BLOCKS])
        src_s = sb("src_s", [P, COLS], I32)
        dst_s = sb("dst_s", [P, COLS], I32)

        edge_fields = nc.dram_tensor("edge_fields", [E + PAD, FIELDS], F32).ap()
        block_start = sb("block_start", [128, BLOCKS], I32)
        fast_ok = sb("fast_ok", [128, 1], I32)
        far_src = sb("far_src", [EP, BLOCKS * CT], I32)
        far_local = sb("far_local", [EP, BLOCKS * CT])

        banks = [bank(f"bank{i}") for i in range(8)]

        s_cz, s_ci, s_w, s_pm = sem("const_zeroed"), sem("const_made"), sem("weights_loaded"), sem("pair_mean_made")
        s_gz = sem("diagonal_zeroed")
        passed_sp, passed_pool, passed_act = sem("passed_sp"), sem("passed_pool"), sem("passed_act")
        with nc.Block("setup") as block:
            @block.gpsimd
            def _(pool):
                nc.gpsimd.memset(ident[:, :], 0.0).then_inc(s_cz, 1)
                nc.gpsimd.memset(earlier[:, :], 1.0).then_inc(s_cz, 1)
                nc.gpsimd.memset(up_to[:, :], 1.0).then_inc(s_cz, 1)
                nc.gpsimd.memset(pair_mean[:, :], 0.0).then_inc(s_cz, 1)
                nc.gpsimd.memset(ln_eps[:, :], LN_EPS).then_inc(s_cz, 1)
                nc.gpsimd.memset(ones[:, :], 1.0).then_inc(s_cz, 1)
                nc.gpsimd.iota(iota_row[:, :], [[1, NB]], base=0, channel_multiplier=0,
                               allow_small_or_imprecise_dtypes=True).then_inc(s_cz, 1)
                nc.gpsimd.iota(iota_tile[:, :], [[1, BLOCKS * CT]], base=0, channel_multiplier=0,
                               allow_small_or_imprecise_dtypes=True).then_inc(s_cz, 1)
                nc.gpsimd.iota(block_base[:, :], [[NB, BLOCKS]], base=0, channel_multiplier=0,
                               allow_small_or_imprecise_dtypes=True).then_inc(s_cz, 1)
                nc.gpsimd.iota(junk_row[:, :], [[0, 1]], base=N, channel_multiplier=1,
                               allow_small_or_imprecise_dtypes=True).then_inc(s_cz, 1)
                pool.wait_ge(s_cz, 10)
                nc.gpsimd.affine_select(out=ident[:, :], in_=ident[:, :], compare_op=ALU.not_equal, fill=1.0,
                                        base=0, pattern=[[-1, 128]], channel_multiplier=1).then_inc(s_ci, 1)
                nc.gpsimd.affine_select(out=earlier[:, :], in_=earlier[:, :], compare_op=ALU.is_gt, fill=0.0,
                                        base=0, pattern=[[-1, 128]], channel_multiplier=1).then_inc(s_ci, 1)
                nc.gpsimd.affine_select(out=up_to[:, :], in_=up_to[:, :], compare_op=ALU.is_ge, fill=0.0,
                                        base=0, pattern=[[-1, 128]], channel_multiplier=1).then_inc(s_ci, 1)
                for n, off in enumerate((0, D, -D)):
                    if n:
                        pool.wait_ge(s_pm, n)
                    nc.gpsimd.affine_select(out=pair_mean[:, :], in_=pair_mean[:, :], compare_op=ALU.not_equal,
                                            fill=0.5, base=off, pattern=[[-1, 128]],
                                            channel_multiplier=1).then_inc(s_pm, 1)
                pool.wait_ge(s_pm, 3)
                pool.wait_ge(s_ci, 3)

            @block.vector
            def _(dve):
                dve.wait_ge(s_ci, 1)
                nc.vector.tensor_scalar(twice[:, :], ident[0:P, 0:P], 2.0, None, ALU.mult)
                nc.vector.tensor_copy(ident_b[:, :], ident[:, :])
                nc.vector.tensor_copy(iota_b[:, :], iota_row[:, 0:128])
                nc.vector.memset(gw1_s[:, :], 0.0).then_inc(s_gz, 1)
                nc.vector.memset(gw2_s[:, :], 0.0).then_inc(s_gz, 1)
                nc.vector.memset(zeros[:, :], 0.0).then_inc(s_gz, 1)

            @block.sync
            def _(sp):
                col = lambda v: v.rearrange("(p a) -> p a", a=1)
                loads = [(w0_s[:, :], w0), (w1_s[:, :], w1), (w2_s[:, :], w2),
                         (b0_s[:, :], col(b0)), (b1_s[:, :], col(b1)),
                         (b2_s[:, :], b2.rearrange("(a f) -> a f", a=1).to_broadcast([128, D])),
                         (src_s[:, :], src.rearrange("(p j) -> p j", p=P)),
                         (dst_s[:, :], dst.rearrange("(p j) -> p j", p=P))]
                for h in (0, D):
                    loads += [(gb1_s[h:h + D, :], col(g_b1)), (gb2_s[h:h + D, :], col(g_b2)),
                              (gamma_s[h:h + D, :], col(gamma)), (beta_s[h:h + D, :], col(beta))]
                for to, fr in loads:
                    sp.dma_start(to, fr).then_inc(s_w, 16)
                sp.wait_ge(s_gz, 3)
                diag = [(gw1_s[h:h + D, h:h + D], g_w1) for h in (0, D)]
                diag += [(gw2_s[h:h + D, h:h + D], g_w2) for h in (0, D)]
                for to, fr in diag:
                    sp.dma_start(to, fr).then_inc(s_w, 16)
                sp.wait_ge(s_w, 16 * (len(loads) + len(diag)))



        def clear_rows(engine, tables, done):
            zw = zeros.shape[1] // D
            count = 0
            for table in tables:
                for r0 in range(0, N, P * zw):
                    engine.dma_start(table[r0:r0 + P * zw, :].rearrange("(p w) f -> p (w f)", p=P),
                                     zeros[0:P, :]).then_inc(done, 16)
                engine.dma_start(table[N:N + 128, :], zeros[:, 0:D]).then_inc(done, 16)
                count += N // (P * zw) + 1
            return count

        def norm_phase(name, sources, table, residual, zeroed, zero_wait=None):
            with ExitStack() as ph:
                def t(n, shape, k=RING):
                    return [ph.enter_context(nc.sbuf_tensor(f"{name}_{n}_{i}", shape, F32)) for i in range(k)]

                s = phase_semaphores(ph, f"{name}")

                def ss(n):
                    return [s(f"{n}_{i}") for i in range(RING)]

                parts = [t(f"part{k}", [P, BW]) for k in range(len(sources))]
                resid = t("resid", [P, BW]) if residual is not None else None
                centred, squared, normed = t("centred", [P, BW]), t("squared", [P, BW]), t("normed", [P, BW])
                mean, var, std, rstd = (t(n, [P, SUBS]) for n in ("mean", "var", "std", "rstd"))
                loaded = ss("loaded")
                table_out, resid_out = ss("table_out"), ss("resid_out")
                zero_out = s("zero_out")
                accs_summed, x_summed = s("accs_summed"), s("x_summed")
                rowsum_done, mean_done, centred_done = s("rowsum_done"), s("mean_done"), s("centred_done")
                squared_done, var_done, std_done = s("squared_done"), s("var_done"), s("std_done")
                rstd_done, normed_done, resid_done = s("rstd_done"), s("normed_done"), s("resid_done")
                summed = len(sources) > 1
                resid_lag = 4
                rows_in = t("total", [P, BW]) if summed else parts[0]

                with nc.Block(name) as block:
                    @block.sync
                    def _(sp):
                        def load(b, q, turn):
                            wait_from(sp, x_summed if summed else centred_done, b - RING + 1, passed_sp)
                            for k, source in enumerate(sources):
                                sp.dma_start(parts[k][q][:, :], rows(source, b)).then_inc(loaded[q], 16)
                        rounds(sp, [(0, load)], BLOCKS)

                    @block.gpsimd
                    def _(pool):
                        def sum_accs(b, q, turn):
                            hold(pool, loaded[q], 16 * len(sources) * (turn + 1), passed_pool)
                            nc.gpsimd.tensor_tensor(parts[1][q][:, :], parts[1][q][:, :], parts[2][q][:, :],
                                                    ALU.add).then_inc(accs_summed, 1)

                        def centre(b, q, turn):
                            hold(pool, mean_done, b + 1, passed_pool)
                            wait_from(pool, normed_done, b - RING + 1, passed_pool)
                            nc.gpsimd.tensor_tensor(blk(centred[q][:, :]), blk(rows_in[q][:, :]),
                                                    mean[q][:, :].unsqueeze(2).to_broadcast([P, SUBS, D]),
                                                    ALU.subtract).then_inc(centred_done, 1)

                        def add_resid(b, q, turn):
                            hold(pool, normed_done, b + 1, passed_pool)
                            wait_from(pool, resid_out[q], 16 * turn, passed_pool)
                            nc.gpsimd.tensor_tensor(resid[q][:, :], rows_in[q][:, :], normed[q][:, :],
                                                    ALU.add).then_inc(resid_done, 1)

                        if summed:
                            rounds(pool, [(0, sum_accs), (resid_lag, add_resid)], BLOCKS)
                        else:
                            rounds(pool, [(0, centre)], BLOCKS)

                    @block.vector
                    def _(dve):
                        def sum_rows(b, q, turn):
                            dve.wait_ge(accs_summed, b + 1)
                            wait_from(dve, resid_done, b - RING + 1)
                            nc.vector.tensor_tensor(rows_in[q][:, :], parts[0][q][:, :], parts[1][q][:, :],
                                                    ALU.add).then_inc(x_summed, 1)

                        def sum_columns(b, q, turn):
                            if summed:
                                dve.wait_ge(x_summed, b + 1)
                            else:
                                dve.wait_ge(loaded[q], 16 * (turn + 1))
                            nc.vector.tensor_reduce(mean[q][:, :], blk(rows_in[q][:, :]), AX.X, ALU.add)\
                              .then_inc(rowsum_done, 1)

                        def mean_of_sum(b, q, turn):
                            dve.wait_ge(rowsum_done, b + 1)
                            nc.vector.tensor_scalar(mean[q][:, :], mean[q][:, :], 1.0 / D, None, ALU.mult)\
                              .then_inc(mean_done, 1)

                        def centre(b, q, turn):
                            dve.wait_ge(mean_done, b + 1)
                            nc.vector.tensor_tensor(blk(centred[q][:, :]), blk(rows_in[q][:, :]),
                                                    mean[q][:, :].unsqueeze(2).to_broadcast([P, SUBS, D]),
                                                    ALU.subtract).then_inc(centred_done, 1)

                        def variance(b, q, turn):
                            dve.wait_ge(squared_done, b + 1)
                            nc.vector.tensor_reduce(var[q][:, :], blk(squared[q][:, :]), AX.X, ALU.add)\
                              .then_inc(var_done, 1)

                        def invert(b, q, turn):
                            dve.wait_ge(std_done, b + 1)
                            nc.vector.reciprocal(rstd[q][:, :], std[q][:, :]).then_inc(rstd_done, 1)

                        def normalise(b, q, turn):
                            wait_from(dve, table_out[q], 16 * turn)
                            if summed:
                                wait_from(dve, resid_done, b - RING + 1)
                            dve.wait_ge(rstd_done, b + 1)
                            nc.vector.scalar_tensor_tensor(blk(normed[q][:, :]), blk(centred[q][:, :]), 0.0,
                                                           rstd[q][:, :].unsqueeze(2).to_broadcast([P, SUBS, D]),
                                                           ALU.max, ALU.mult).then_inc(normed_done, 1)

                        if summed:
                            stages = [(2, variance), (1, centre), (0, sum_rows), (3, invert), (0, sum_columns),
                                      (3, normalise), (0, mean_of_sum)]
                        else:
                            stages = [(2, variance), (0, sum_columns), (3, invert), (0, mean_of_sum), (3, normalise)]
                        rounds(dve, stages, BLOCKS)

                    @block.scalar
                    def _(act):
                        for table_z in zeroed:
                            act.dma_start(table_z[N:N + 128, :], zeros[:, 0:D]).then_inc(zero_out, 16)

                        def clear(b, q, turn):
                            for table_z in zeroed:
                                act.dma_start(rows(table_z, b), zeros[0:P, 0:BW]).then_inc(zero_out, 16)

                        def square(b, q, turn):
                            act.wait_ge(centred_done, b + 1)
                            wait_from(act, var_done, b - RING + 1)
                            nc.scalar.activation(squared[q][:, :], centred[q][:, :], ACT.Square)\
                              .then_inc(squared_done, 1)

                        def deviation(b, q, turn):
                            act.wait_ge(var_done, b + 1)
                            wait_from(act, rstd_done, b - RING + 1)
                            nc.scalar.activation(std[q][:, :], var[q][:, :], ACT.Sqrt, bias=ln_eps[:, :],
                                                 scale=1.0 / D).then_inc(std_done, 1)

                        def store(b, q, turn):
                            hold(act, normed_done, b + 1, passed_act)
                            act.dma_start(rows(table, b), normed[q][:, :]).then_inc(table_out[q], 16)

                        def store_resid(b, q, turn):
                            hold(act, resid_done, b + 1, passed_act)
                            act.dma_start(rows(residual, b), resid[q][:, :]).then_inc(resid_out[q], 16)

                        stages = [(2, deviation), (1 if summed else 0, square), (4, store)]
                        if residual is not None:
                            stages.append((resid_lag + 1, store_resid))
                        if zeroed:
                            stages.append((0, clear))
                        rounds(act, stages, BLOCKS)
                        if zeroed:
                            act.wait_ge(zero_out, 16 * len(zeroed) * (BLOCKS + 1))
                        if zero_wait:
                            act.wait_ge(*zero_wait)
                        for q in range(RING):
                            n = (BLOCKS - q + RING - 1) // RING
                            act.wait_ge(table_out[q], 16 * n)
                            if residual is not None:
                                act.wait_ge(resid_out[q], 16 * n)

        cleared0 = sem("cleared0")
        cleared0_total = []
        with ExitStack() as ph:
            def whole(n, dt=F32):
                return ph.enter_context(nc.sbuf_tensor(f"survey_{n}", [P, COLS], dt))

            def small(n, w=1, p=P):
                return ph.enter_context(nc.sbuf_tensor(f"survey_{n}", [p, w], F32))

            s = phase_semaphores(ph, "survey")

            next_s, as_int = whole("next_s", I32), whole("as_int", I32)
            (src_f, dst_f, next_f, own, own_upto, own_before, edge, rank, blk_of, next_blk, seam, tile_of, sub_of,
             local, place, far, work, none) = (whole(n) for n in (
                 "src_f", "dst_f", "next_f", "own", "own_upto", "own_before", "edge", "rank", "blk_of", "next_blk",
                 "seam", "tile_of", "sub_of", "local", "place", "far", "work", "none"))
            fields = ph.enter_context(nc.sbuf_tensor("survey_fields", [P, COLS, FIELDS], F32))
            pad = ph.enter_context(nc.sbuf_tensor("survey_pad", [P, PAD // P * FIELDS], F32))
            later = small("later", 128, 128)
            end_of_all = ph.enter_context(nc.sbuf_tensor("survey_end_of_all", [1, 1], I32))
            offset, total, seam_at, seam_blk, first_start, start_step = (
                small(n) for n in ("offset", "total", "seam_at", "seam_blk", "first_start", "start_step"))
            seam_hot, starts = small("seam_hot", BLOCKS), small("starts", BLOCKS, 128)
            faults, fault_sums, fault_sum, total_off = (small("faults", 4), small("fault_sums", 4, 128),
                                                        small("fault_sum", 1, 128), small("total_off", 1, 128))
            s_next, s_end, s_const, s_later, s_chain, s_pe, s_out = (
                s(n) for n in ("next_loaded", "end_made", "const_made", "later_made", "dve_steps", "pe_steps",
                               "fields_out"))
            UPTO, SEAM, FAULTS, PLACED = "upto", "seam", "faults", "placed"
            at_step = {}
            with nc.Block("survey") as block:
                @block.vector
                def _(dve):
                    steps = [0]

                    def link(instruction, mark=None):
                        steps[0] += 1
                        instruction.then_inc(s_chain, 1)
                        dve.wait_ge(s_chain, steps[0])
                        if mark:
                            at_step[mark] = steps[0]

                    V = nc.vector

                    def floor_of(to, value, divisor):
                        link(V.tensor_scalar(as_int[:, :], value, 1.0 / divisor, 0.5 / divisor - 0.5,
                                             ALU.mult, ALU.add))
                        link(V.tensor_copy(to, as_int[:, :]))

                    V.memset(none[:, :], 0.0)
                    V.memset(pad[:, :], -1.0)
                    V.memset(fields[:, :, 6], 1.0)
                    V.tensor_copy(src_f[:, :], src_s[:, :])
                    link(V.tensor_copy(dst_f[:, :], dst_s[:, :]))
                    dve.wait_ge(s_next, 16 * 3)
                    link(V.tensor_copy(next_f[:, :], next_s[:, :]))
                    V.tensor_tensor(own[:, :], src_f[:, :], dst_f[:, :], ALU.is_equal)
                    link(V.tensor_tensor(work[:, :], next_f[:, :], dst_f[:, :], ALU.not_equal))
                    link(V.tensor_tensor(own[:, :], own[:, :], work[:, :], ALU.mult))
                    link(V.tensor_tensor_scan(own_upto[:, :], own[:, :], none[:, :], 0.0, ALU.add, ALU.add), UPTO)
                    V.tensor_scalar(far[:, :], own[:, :], -1.0, 1.0, ALU.mult, ALU.add)
                    floor_of(blk_of[:, :], dst_f[:, :], NB)
                    floor_of(next_blk[:, :], next_f[:, :], NB)
                    dve.wait_ge(s_pe, 1)
                    link(V.tensor_copy(offset[:, :], banks[0][0:P, 0:1]))
                    link(V.scalar_tensor_tensor(own_before[:, :], own_upto[:, :], offset[:, :], own[:, :],
                                                ALU.add, ALU.subtract))
                    dve.wait_ge(s_const, 1)
                    V.tensor_tensor(rank[:, :], edge[:, :], own_before[:, :], ALU.subtract)
                    link(V.tensor_tensor(seam[:, :], next_blk[:, :], blk_of[:, :], ALU.not_equal))
                    link(V.scalar_tensor_tensor(seam[:, :], next_blk[:, :], float(BLOCKS), seam[:, :],
                                                ALU.is_lt, ALU.mult))
                    link(V.scalar_tensor_tensor(work[:, :], edge[:, :], 1.0, seam[:, :], ALU.add, ALU.mult,
                                                accum_out=seam_at[:, :]))
                    link(V.scalar_tensor_tensor(work[:, :], next_blk[:, :], 1.0, seam[:, :], ALU.mult, ALU.mult,
                                                accum_out=seam_blk[:, :]))
                    link(V.tensor_scalar(seam_hot[:, :], iota_row[0:P, 0:BLOCKS], seam_blk[:, :], seam_at[:, :],
                                         ALU.is_equal, ALU.mult), SEAM)
                    dve.wait_ge(s_pe, 2)
                    V.tensor_copy(block_start[:, :], banks[1][:, 0:BLOCKS])
                    link(V.tensor_copy(starts[:, :], banks[1][:, 0:BLOCKS]))
                    link(V.scalar_tensor_tensor(seam_hot[:, :], iota_row[0:P, 0:BLOCKS], blk_of[:, 0:1],
                                                starts[0:P, :], ALU.is_equal, ALU.mult,
                                                accum_out=first_start[:, :]))
                    link(V.tensor_tensor(start_step[:, :], seam_at[:, :], first_start[:, :], ALU.subtract))
                    link(V.tensor_scalar(work[:, :], blk_of[:, :], blk_of[:, 0:1], start_step[:, :],
                                         ALU.subtract, ALU.mult))
                    link(V.scalar_tensor_tensor(work[:, :], work[:, :], first_start[:, :], rank[:, :],
                                                ALU.add, ALU.subtract))
                    link(V.scalar_tensor_tensor(place[:, :], blk_of[:, :], float(NB), work[:, :],
                                                ALU.mult, ALU.subtract))
                    V.scalar_tensor_tensor(local[:, :], blk_of[:, :], -float(NB), dst_f[:, :], ALU.mult, ALU.add)
                    floor_of(tile_of[:, :], place[:, :], EP)
                    floor_of(sub_of[:, :], local[:, :], P)
                    V.scalar_tensor_tensor(fields[:, :, 1], tile_of[:, :], -float(EP), place[:, :], ALU.mult, ALU.add)
                    link(V.scalar_tensor_tensor(work[:, :], blk_of[:, :], float(CT), tile_of[:, :],
                                                ALU.mult, ALU.add))
                    link(V.scalar_tensor_tensor(work[:, :], work[:, :], 1.0, far[:, :], ALU.add, ALU.mult))
                    V.tensor_scalar(fields[:, :, 0], work[:, :], -1.0, None, ALU.add)
                    floor_of(fields[:, :, 2], src_f[:, :], 256)
                    V.scalar_tensor_tensor(fields[:, :, 3], fields[:, :, 2], -256.0, src_f[:, :], ALU.mult, ALU.add)
                    floor_of(fields[:, :, 4], local[:, :], 256)
                    link(V.scalar_tensor_tensor(fields[:, :, 5], fields[:, :, 4], -256.0, local[:, :],
                                                ALU.mult, ALU.add), PLACED)
                    V.tensor_tensor(place[:, :], own_before[:, :], dst_f[:, :], ALU.not_equal)
                    link(V.tensor_tensor(sub_of[:, :], sub_of[:, :], tile_of[:, :], ALU.subtract))
                    link(V.tensor_tensor(sub_of[:, :], sub_of[:, :], sub_of[:, :], ALU.mult))
                    for n, (in0, scalar, op0, in1, op1) in enumerate((
                            (place, 1.0, ALU.mult, own, ALU.mult), (next_f, 0.0, ALU.add, dst_f, ALU.is_lt),
                            (sub_of, 1.5, ALU.is_gt, far, ALU.mult), (tile_of, CT - 0.5, ALU.is_gt, far, ALU.mult))):
                        link(V.scalar_tensor_tensor(work[:, :], in0[:, :], scalar, in1[:, :], op0, op1,
                                                    accum_out=faults[:, n:n + 1]), FAULTS)
                    dve.wait_ge(s_pe, 3)
                    link(V.tensor_copy(fault_sums[:, :], banks[2][:, 0:4]))
                    V.tensor_scalar(total_off[:, :], banks[0][:, 1:2], float(N), None, ALU.not_equal)
                    link(V.tensor_reduce(fault_sum[:, :], fault_sums[:, :], AX.X, ALU.add))
                    link(V.tensor_tensor(fault_sum[:, :], fault_sum[:, :], total_off[:, :], ALU.add))
                    link(V.tensor_scalar(fast_ok[:, :], fault_sum[:, :], 0.0, None, ALU.is_equal))

                @block.tensor
                def _(pe):
                    pe.wait_ge(s_later, 1)
                    pe.wait_ge(s_chain, at_step[UPTO])
                    nc.tensor.matmul(banks[0][:, 0:1], later[0:P, :], own_upto[:, COLS - 1:COLS], start=True, stop=True)
                    nc.tensor.matmul(banks[0][:, 1:2], ones[0:P, :], own_upto[:, COLS - 1:COLS],
                                     start=True, stop=True).then_inc(s_pe, 1)
                    pe.wait_ge(s_chain, at_step[SEAM])
                    nc.tensor.matmul(banks[1][:, 0:BLOCKS], ones[0:P, :], seam_hot[:, :],
                                     start=True, stop=True).then_inc(s_pe, 1)
                    pe.wait_ge(s_chain, at_step[FAULTS])
                    nc.tensor.matmul(banks[2][:, 0:4], ones[0:P, :], faults[:, :],
                                     start=True, stop=True).then_inc(s_pe, 1)

                @block.scalar
                def _(act):
                    cleared0_total.append(16 * clear_rows(act, acc0[:1], cleared0))

                @block.gpsimd
                def _(pool):
                    nc.gpsimd.iota(end_of_all[:, :], [[0, 1]], base=N, channel_multiplier=0).then_inc(s_end, 1)
                    nc.gpsimd.iota(edge[:, :], [[1, COLS]], base=0, channel_multiplier=COLS,
                                   allow_small_or_imprecise_dtypes=True).then_inc(s_const, 1)
                    nc.gpsimd.affine_select(out=later[:, :], in_=ones[:, :], compare_op=ALU.is_gt, fill=0.0,
                                            base=0, pattern=[[1, 128]], channel_multiplier=-1).then_inc(s_later, 1)

                @block.sync
                def _(sp):
                    sp.dma_start(next_s[0:P - 1, :], dst[1:1 + (P - 1) * COLS].rearrange("(p j) -> p j", j=COLS))\
                      .then_inc(s_next, 16)
                    sp.dma_start(next_s[P - 1:P, 0:COLS - 1], dst[1 + (P - 1) * COLS:E].rearrange("(p j) -> p j", p=1))\
                      .then_inc(s_next, 16)
                    sp.wait_ge(s_end, 1)
                    sp.dma_start(next_s[P - 1:P, COLS - 1:COLS], end_of_all[:, :]).then_inc(s_next, 16)
                    sp.wait_ge(s_chain, at_step[PLACED])
                    sp.dma_start(edge_fields[0:E, :].rearrange("(p j) k -> p (j k)", p=P),
                                 fields[:, :, :].rearrange("p j k -> p (j k)")).then_inc(s_out, 16)
                    sp.dma_start(edge_fields[E:E + PAD, :].rearrange("(p j) k -> p (j k)", p=P), pad[:, :])\
                      .then_inc(s_out, 16)
                    sp.wait_ge(s_out, 32)

        norm_phase("norm0", [x], h0_t, None, acc0[1:], (cleared0, cleared0_total[0]))

        def edge_phase(name, table, seg_s, accs, mlp):
            with ExitStack() as ph:
                def t(n, shape, k=RING, dt=F32):
                    return [ph.enter_context(nc.sbuf_tensor(f"{name}_{n}_{i}", shape, dt)) for i in range(k)]

                s = phase_semaphores(ph, f"{name}")

                def ss(n):
                    return [s(f"{n}_{i}") for i in range(RING)]

                SIDES = 2 if mlp else 1
                W = SIDES * D
                src_i, dst_i, put_i = (t(n, [P, TILES], RING, I32) for n in ("src_i", "dst_i", "put_i"))
                seg_f = t("seg_f", [P, TILES])
                repeat_n, to_junk = t("repeat_n", [P, TILES]), t("to_junk", [P, TILES])
                gathered = t("gathered", [P, TILES * W])
                same, same_earlier = t("same", [P, GW], 2), t("same_earlier", [P, GW], 2)
                summed = t("summed", [P, TILES * D])
                indices_ready, same_ready, put_ready = s("indices_ready"), s("same_ready"), s("put_ready")
                seg_spread, same_masked, repeats_counted, junk_offset, junk_scaled = (
                    s(n) for n in ("seg_spread", "same_masked", "repeats_counted", "junk_offset", "junk_scaled"))
                gather_done = ss("gather_done")
                acc_done = [s(f"acc_done_{k}") for k in range(ACCS)]
                merged, summed_ready = s("merged"), s("summed_ready")
                gathered_used = s("gathered_used")
                if mlp:
                    pair_t, t1, e1, h1, t2, e2, h2 = (t(n, [128, GW], 1)[0] for n in
                                                      ("pair_t", "t1", "e1", "h1", "t2", "e2", "h2"))
                    message = t("message", [P, TILES * D], 1)[0]
                    (pair_t_ready, pre1_done, t1_ready, e1_ready, l1_ready, h1_ready, pre2_done, t2_ready,
                     e2_ready, l2_ready, h2_ready, raw_done, message_ready) = (s(n) for n in (
                         "pair_t_ready", "pre1_done", "t1_ready", "e1_ready", "l1_ready", "h1_ready", "pre2_done",
                         "t2_ready", "e2_ready", "l2_ready", "h2_ready", "raw_done", "message_ready"))
                ps_seg, ps_pair, ps_1, ps_2, ps_raw, ps_sum = (banks[i] for i in range(6))
                SCATTER_LAG = 2
                COMPUTE_LAG = 2

                def tiles(ap, w):
                    return ap.rearrange("p (j w) -> p j w", w=w)

                with nc.Block(name) as block:
                    @block.gpsimd
                    def _(pool):
                        def gather(j):
                            def body(g, q, turn):
                                if j == 0:
                                    hold(pool, indices_ready, g + 1, passed_pool)
                                    wait_from(pool, gathered_used if mlp else merged, g - RING + 1, passed_pool)
                                for side in range(SIDES):
                                    idx = (src_i, dst_i)[side][q][:, j:j + 1]
                                    at = j * W + side * D
                                    pool.indirect_dma_start(
                                        gathered[q][:, at:at + D], None, table,
                                        bass.IndirectOffsetOnAxis(ap=idx, axis=0)).then_inc(gather_done[q], 16)
                            return body

                        def scatter(j):
                            def body(g, q, turn):
                                if j == 0:
                                    hold(pool, summed_ready, g + 1, passed_pool)
                                    hold(pool, put_ready, g + 1, passed_pool)
                                k = j % ACCS
                                wait_from(pool, acc_done[k], 16 * (g * (TILES // ACCS) + j // ACCS), passed_pool)
                                pool.indirect_dma_start(
                                    accs[k], bass.IndirectOffsetOnAxis(ap=put_i[q][:, j:j + 1], axis=0),
                                    summed[q][:, j * D:(j + 1) * D], None, compute_op=ALU.add)\
                                    .then_inc(acc_done[k], 16)
                            return body

                        steps = []
                        for j in range(TILES):
                            steps += [(0, gather(j)), (SCATTER_LAG, scatter(j))]
                        rounds(pool, steps, GROUPS)
                        for k in range(ACCS):
                            pool.wait_ge(acc_done[k], 16 * GROUPS * TILES // ACCS)

                    @block.vector
                    def _(dve):
                        def indices(g, q, turn):
                            wait_from(dve, gather_done[q], 16 * TILES * SIDES * turn)
                            wait_from(dve, seg_spread, g - RING + 1)
                            at = bass.ds(g * TILES, TILES)
                            nc.vector.tensor_copy(src_i[q][:, :], src_s[:, at])
                            if mlp:
                                nc.vector.tensor_copy(dst_i[q][:, :], dst_s[:, at])
                            nc.vector.tensor_copy(seg_f[q][:, :], seg_s[:, at]).then_inc(indices_ready, 1)

                        def repeats(g, q, turn):
                            r = q % 2
                            dve.wait_ge(seg_spread, g + 1)
                            wait_from(dve, merged, g - 1)
                            nc.vector.tensor_tensor(
                                tiles(same[r][:, :], P), tiles(ps_seg[0:P, 0:GW], P),
                                seg_f[q][:, :].unsqueeze(2).to_broadcast([P, TILES, P]),
                                ALU.is_equal).then_inc(same_ready, 1)
                            dve.wait_ge(same_ready, g + 1)
                            nc.vector.tensor_tensor(
                                tiles(same_earlier[r][:, :], P), tiles(same[r][:, :], P),
                                earlier[0:P, 0:P].unsqueeze(1).to_broadcast([P, TILES, P]),
                                ALU.mult).then_inc(same_masked, 1)
                            dve.wait_ge(same_masked, g + 1)
                            nc.vector.tensor_reduce(repeat_n[q][:, :], tiles(same_earlier[r][:, :], P), AX.X,
                                                    ALU.add).then_inc(repeats_counted, 1)
                            nc.vector.scalar_tensor_tensor(
                                to_junk[q][:, :], seg_f[q][:, :], -1.0, junk_row[0:P, :].to_broadcast([P, TILES]),
                                ALU.mult, ALU.add).then_inc(junk_offset, 1)
                            dve.wait_ge(repeats_counted, g + 1)
                            dve.wait_ge(junk_offset, g + 1)
                            nc.vector.scalar_tensor_tensor(
                                to_junk[q][:, :], repeat_n[q][:, :], 1.0, to_junk[q][:, :],
                                ALU.min, ALU.mult).then_inc(junk_scaled, 1)
                            dve.wait_ge(junk_scaled, g + 1)
                            for k in range(ACCS):
                                wait_from(dve, acc_done[k], 16 * (g - RING + 1) * (TILES // ACCS))
                            nc.vector.tensor_tensor(put_i[q][:, :], to_junk[q][:, :], seg_f[q][:, :],
                                                    ALU.add).then_inc(put_ready, 1)

                        def clamp(g, psum, bias, to, done, pre):
                            dve.wait_ge(pre, g + 1)
                            nc.vector.tensor_scalar(to[:, :], psum[:, 0:GW], bias[:, :], SOFTPLUS_CLAMP,
                                                    ALU.add, ALU.min).then_inc(done, 1)

                        def softplus(g, psum, bias, ln, ln_done, to, done):
                            dve.wait_ge(ln_done, g + 1)
                            nc.vector.scalar_tensor_tensor(to[:, :], psum[:, 0:GW], bias[:, :], ln[:, :],
                                                           ALU.add, ALU.max).then_inc(done, 1)

                        def mlp_steps(g, q, turn):
                            clamp(g, ps_1, b0_s, t1, t1_ready, pre1_done)
                            softplus(g, ps_1, b0_s, e1, l1_ready, h1, h1_ready)
                            clamp(g, ps_2, b1_s, t2, t2_ready, pre2_done)
                            softplus(g, ps_2, b1_s, e2, l2_ready, h2, h2_ready)
                            dve.wait_ge(raw_done, g + 1)
                            nc.vector.tensor_tensor(
                                tiles(message[:, :], D), tiles(ps_raw[0:P, 0:TILES * D], D),
                                b2_s[0:P, :].unsqueeze(1).to_broadcast([P, TILES, D]),
                                ALU.add).then_inc(message_ready, 1)

                        stages = [(0, indices), (COMPUTE_LAG, repeats)]
                        if mlp:
                            stages.append((COMPUTE_LAG, mlp_steps))
                        rounds(dve, stages, GROUPS)

                    @block.tensor
                    def _(pe):
                        def spread(g, q, turn):
                            pe.wait_ge(indices_ready, g + 1)
                            wait_from(pe, same_ready, g)
                            for j in range(TILES):
                                last = nc.tensor.matmul(ps_seg[0:P, j * P:(j + 1) * P],
                                                        seg_f[q][:, j:j + 1].to_broadcast([P, P]), ident[0:P, 0:P],
                                                        start=True, stop=True)
                            last.then_inc(seg_spread, 1)

                        def pairs(g, q, turn):
                            pe.wait_ge(gather_done[q], 16 * TILES * SIDES * (turn + 1))
                            wait_from(pe, pair_t_ready, g)
                            for j in range(TILES):
                                last = nc.tensor.transpose(ps_pair[0:W, j * P:(j + 1) * P],
                                                           gathered[q][:, j * W:(j + 1) * W], ident[0:P, 0:P])
                            last.then_inc(gathered_used, 1)

                        def layers(g, q, turn):
                            pe.wait_ge(pair_t_ready, g + 1)
                            nc.tensor.matmul(ps_1[:, 0:GW], w0_s[:, :], pair_t[:, :], start=True, stop=True)\
                              .then_inc(pre1_done, 1)
                            pe.wait_ge(h1_ready, g + 1)
                            nc.tensor.matmul(ps_2[:, 0:GW], w1_s[:, :], h1[:, :], start=True, stop=True)\
                              .then_inc(pre2_done, 1)
                            pe.wait_ge(h2_ready, g + 1)
                            for j in range(TILES):
                                last = nc.tensor.matmul(ps_raw[0:P, j * D:(j + 1) * D], h2[:, j * P:(j + 1) * P],
                                                        w2_s[:, :], start=True, stop=True)
                            last.then_inc(raw_done, 1)

                        def merge(g, q, turn):
                            pe.wait_ge(same_ready, g + 1)
                            if mlp:
                                pe.wait_ge(message_ready, g + 1)
                            else:
                                pe.wait_ge(gather_done[q], 16 * TILES * SIDES * (turn + 1))
                            wait_from(pe, summed_ready, g)
                            rows_in = message if mlp else gathered[q]
                            for j in range(TILES):
                                last = nc.tensor.matmul(ps_sum[0:P, j * D:(j + 1) * D],
                                                        same[q % 2][:, j * P:(j + 1) * P],
                                                        rows_in[:, j * D:(j + 1) * D], start=True, stop=True)
                            last.then_inc(merged, 1)
                        stages = [(COMPUTE_LAG, spread)]
                        if mlp:
                            stages += [(COMPUTE_LAG, pairs), (COMPUTE_LAG, layers)]
                        rounds(pe, stages + [(COMPUTE_LAG, merge)], GROUPS)

                    @block.scalar
                    def _(act):
                        def mlp_steps(g, q, turn):
                            act.wait_ge(gathered_used, g + 1)
                            wait_from(act, pre1_done, g)
                            nc.scalar.activation(pair_t[:, :], ps_pair[:, 0:GW], ACT.Copy).then_inc(pair_t_ready, 1)
                            for (t_in, t_ready, e, e_ready, l_ready) in ((t1, t1_ready, e1, e1_ready, l1_ready),
                                                                         (t2, t2_ready, e2, e2_ready, l2_ready)):
                                act.wait_ge(t_ready, g + 1)
                                nc.scalar.activation(e[:, :], t_in[:, :], ACT.Exp).then_inc(e_ready, 1)
                                act.wait_ge(e_ready, g + 1)
                                nc.scalar.activation(e[:, :], e[:, :], ACT.Ln, bias=1.0).then_inc(l_ready, 1)

                        def move(g, q, turn):
                            act.wait_ge(merged, g + 1)
                            for k in range(ACCS):
                                wait_from(act, acc_done[k], 16 * (g - RING + 1) * (TILES // ACCS))
                            nc.scalar.activation(summed[q][:, :], ps_sum[0:P, 0:TILES * D], ACT.Copy)\
                               .then_inc(summed_ready, 1)

                        if mlp:
                            act.preload_act_table_set(EXP_LN_SET)
                        stages = ([(COMPUTE_LAG, mlp_steps)] if mlp else []) + [(COMPUTE_LAG, move)]
                        rounds(act, stages, GROUPS)

        z_t = sb("z_t", [128, BLOCKS * TW])
        z_stats = sb("z_stats", [128, BLOCKS * 6])

        def node_phase():
            with ExitStack() as ph:
                def t(n, shape, k=RING):
                    return [ph.enter_context(nc.sbuf_tensor(f"node_{n}_{i}", shape, F32)) for i in range(k)]

                s = phase_semaphores(ph, "node")

                parts = [t(f"part{k}", [P, BW]) for k in range(3)]
                z_in, hid = t("z_in", [128, TW], 2), t("hid", [128, TW], 2)
                loaded = [s(f"loaded_{i}") for i in range(RING)]
                accs_summed, z_summed, turned, z_in_ready, pre_done, hid_ready, post_done, z_ready, stats_done = (
                    s(n) for n in ("accs_summed", "z_summed", "turned", "z_in_ready", "pre_done", "hid_ready",
                                   "post_done", "z_ready", "stats_done"))
                with nc.Block("node_mlp") as block:
                    @block.sync
                    def _(sp):
                        def load(b, q, turn):
                            wait_from(sp, turned, b - RING + 1, passed_sp)
                            for k, source in enumerate([h1_t] + acc1):
                                sp.dma_start(pairs_of(parts[k][q][:, :]), pair_rows(source, b)).then_inc(loaded[q], 16)
                        rounds(sp, [(0, load)], BLOCKS)

                    @block.gpsimd
                    def _(pool):
                        def sum_accs(b, q, turn):
                            hold(pool, loaded[q], 16 * 3 * (turn + 1), passed_pool)
                            nc.gpsimd.tensor_tensor(parts[1][q][:, :], parts[1][q][:, :], parts[2][q][:, :],
                                                    ALU.add).then_inc(accs_summed, 1)
                        rounds(pool, [(0, sum_accs)], BLOCKS)

                    @block.vector
                    def _(dve):
                        def add_self(b, q, turn):
                            dve.wait_ge(accs_summed, b + 1)
                            nc.vector.tensor_tensor(parts[0][q][:, :], parts[0][q][:, :], parts[1][q][:, :],
                                                    ALU.add).then_inc(z_summed, 1)

                        def stats(b, q, turn):
                            dve.wait_ge(z_ready, b + 1)
                            nc.vector.bn_stats(z_stats[:, bass.ds(b * 6, 6)], z_t[:, bass.ds(b * TW, TW)])\
                              .then_inc(stats_done, 1)
                        rounds(dve, [(0, add_self), (2, stats)], BLOCKS)
                        dve.wait_ge(stats_done, BLOCKS)

                    @block.tensor
                    def _(pe):
                        def turn_rows(b, q, turn):
                            pe.wait_ge(z_summed, b + 1)
                            wait_from(pe, z_in_ready, b - 1)
                            for j in range(PAIRS):
                                last = nc.tensor.transpose(banks[q % 2][:, j * P:(j + 1) * P],
                                                           parts[0][q][:, j * 2 * D:(j + 1) * 2 * D], ident[0:P, 0:P])
                            last.then_inc(turned, 1)

                        def first(b, q, turn):
                            pe.wait_ge(z_in_ready, b + 1)
                            wait_from(pe, hid_ready, b - 1)
                            nc.tensor.matmul(banks[2 + q % 2][:, 0:TW], gw1_s[:, :], z_in[q % 2][:, :],
                                             start=True, stop=True).then_inc(pre_done, 1)

                        def second(b, q, turn):
                            pe.wait_ge(hid_ready, b + 1)
                            wait_from(pe, z_ready, b - 1)
                            nc.tensor.matmul(banks[4 + q % 2][:, 0:TW], gw2_s[:, :], hid[q % 2][:, :],
                                             start=True, stop=True).then_inc(post_done, 1)
                        rounds(pe, [(0, turn_rows), (1, first), (2, second)], BLOCKS)

                    @block.scalar
                    def _(act):
                        def take_in(b, q, turn):
                            act.wait_ge(turned, b + 1)
                            wait_from(act, pre_done, b - 1)
                            nc.scalar.activation(z_in[q % 2][:, :], banks[q % 2][:, 0:TW], ACT.Copy)\
                               .then_inc(z_in_ready, 1)

                        def hidden(b, q, turn):
                            act.wait_ge(pre_done, b + 1)
                            wait_from(act, post_done, b - 1)
                            nc.scalar.activation(hid[q % 2][:, :], banks[2 + q % 2][:, 0:TW], ACT.Relu,
                                                 bias=gb1_s[:, :]).then_inc(hid_ready, 1)

                        def result(b, q, turn):
                            act.wait_ge(post_done, b + 1)
                            nc.scalar.activation(z_t[:, bass.ds(b * TW, TW)], banks[4 + q % 2][:, 0:TW], ACT.Identity,
                                                 bias=gb2_s[:, :]).then_inc(z_ready, 1)
                        rounds(act, [(0, take_in), (1, hidden), (2, result)], BLOCKS)

        def fast_edges0():
            GT = 3
            GK = CT // GT
            FW = GT * EP
            HALF = SUBS // 2
            UNITS = (("own", 0), ("far", 0), ("far", 1), ("own", 1), ("far", 2))
            NU = len(UNITS)
            UNIT_LAG = 2
            SCATTER_LAG = 2
            JUNK_HIGH = N // 256 * 256
            CHUNK = -(-RAW // NU)
            assert N % 256 + EP <= 256
            assert FIELDS - 2 == 5
            with ExitStack() as ph:
                def t(n, shape, k, dt=F32):
                    return [ph.enter_context(nc.sbuf_tensor(f"fast0_{n}_{i}", shape, dt)) for i in range(k)]

                s = phase_semaphores(ph, "fast0")

                raw = t("raw", [EP, RAW * FIELDS], 2)
                row_hot = t("row_hot", [EP, RAW * EP], 2, BF16)
                tile_hot = t("tile_hot", [EP, RAW * CT], 2)
                spread_out = t("spread_out", [EP, RAW * CT * 5], 2, BF16)
                packed = t("packed", [EP, CT * 5], 1)[0]
                gather_i = t("gather_i", [EP, 2 * CT], 2, I32)
                empty, src_f, local_f, seg_f, src_high, equals, to_junk, shift_n = (
                    t(n, [EP, CT], 2) for n in ("empty", "src_f", "local_f", "seg_f", "src_high", "equals", "to_junk",
                                                "shift_n"))
                seg_high, seg_low = (t(n, [EP, CT], 2, BF16) for n in ("seg_high", "seg_low"))
                put_i = t("put_i", [EP, CT], 2, I32)
                junk_low = t("junk_low", [EP, 1], 1)[0]
                gathered = t("gathered", [EP, GT * 2 * D], 2 * GK)
                same = t("same", [EP, FW], 2)
                summed = t("summed", [EP, GT * D], 2 * GK)
                own_rows, own_x, own_out = (t(n, [P, BW], 2) for n in ("own_rows", "own_x", "own_out"))
                own_bias = t("own_bias", [P, BW], 2)
                in_t, t1, e1, h1, t2, e2, h2 = (t(n, [128, 512], 1)[0] for n in
                                                ("in_t", "t1", "e1", "h1", "t2", "e2", "h2"))
                message = t("message", [EP, GT * D], 1)[0]
                w0_own = t("w0_own", [128, 2 * HID], 1)[0]
                w0_parts = t("w0_parts", [128, HID], 2)
                junk_low_made = s("junk_low_made")
                raw_loaded, rows_loaded, x_loaded, own_stored = (
                    [s(f"{n}_{i}") for i in range(2)] for n in ("raw_loaded", "rows_loaded", "x_loaded", "own_stored"))
                gather_done = [s(f"gather_done_{i}") for i in range(2 * GK)]
                acc_done = [s(f"acc_done_{k}") for k in range(ACCS)]
                (w_zeroed, w_loaded, w_ready, tile_hot_ready, spread_ready, packed_done, packed_copied, nodes_ready, seg_filled,
                 indices_ready, seg_spread, same_ready, shift_ready, put_ready, turned, in_ready, pre1_done, t1_ready, e1_ready, l1_ready, h1_ready, pre2_done, t2_ready,
                 e2_ready, l2_ready, h2_ready, raw_done, message_ready, merged, summed_ready, own_bias_ready) = (
                     s(n) for n in (
                         "w_zeroed", "w_loaded", "w_ready", "tile_hot_ready", "spread_ready", "packed_done", "packed_copied",
                         "nodes_ready", "seg_filled", "indices_ready", "seg_spread", "same_ready", "shift_ready",
                         "put_ready", "turned", "in_ready",
                         "pre1_done", "t1_ready", "e1_ready", "l1_ready", "h1_ready", "pre2_done", "t2_ready",
                         "e2_ready", "l2_ready", "h2_ready", "raw_done", "message_ready", "merged", "summed_ready",
                         "own_bias_ready"))
                ps_seg, ps_in, ps_1, ps_2, ps_raw, ps_sum, ps_packed = (banks[i] for i in range(7))

                def cols(ap, w):
                    return ap.rearrange("p (j w) -> p j w", w=w)

                def width(i):
                    return FW if UNITS[i][0] == "far" else HALF * P

                def unit_stages(order, lag):
                    out = []
                    for i in range(NU):
                        for back, body in order(i, lambda back: (i - back) % NU):
                            out.append((lag - (i - back) // NU, body))
                    return out

                def scatters_over(engine, b, turn, q, k):
                    whole, odd = CT * (turn - 1), CT * q + GT * k + GT - 1
                    for a in range(ACCS):
                        wait_from(engine, acc_done[a], 16 * (whole + (odd + 2 - a) // 2),
                                  passed_pool if engine is nc.gpsimd else None)

                with nc.Block("fast_edges0") as block:
                    @block.sync
                    def _(sp):
                        for h in (0, D):
                            for k in range(2):
                                sp.dma_start(w0_parts[k][h:h + D, :], w0[k * D:(k + 1) * D, :]).then_inc(w_loaded, 16)

                        def load_raw(b, q, turn):
                            wait_from(sp, spread_ready, NU * (b - 1), passed_sp)
                            start = sp.value_load(block_start[0:1, bass.ds(b, 1)], min_val=0, max_val=E)
                            sp.dma_start(raw[q][:, :], edge_fields[bass.ds(start, RAW * EP), :]
                                         .rearrange("(p t) k -> p (t k)", p=EP)).then_inc(raw_loaded[q], 16)

                        def load_rows(b, q, turn):
                            wait_from(sp, turned, NU * (b - 2) + 4, passed_sp)
                            sp.dma_start(own_rows[q][:, :], rows(h0_t, b)).then_inc(rows_loaded[q], 16)
                            wait_from(sp, own_bias_ready, b - 1, passed_sp)
                            sp.dma_start(own_x[q][:, :], rows(x, b)).then_inc(x_loaded[q], 16)

                        def store_own(b, q, turn):
                            hold(sp, message_ready, NU * b + 4, passed_sp)
                            sp.dma_start(rows(own_t, b), own_out[q][:, :]).then_inc(own_stored[q], 16)
                        rounds(sp, [(0, load_raw), (1, load_rows), (UNIT_LAG + 1, store_own)], BLOCKS, 2)
                        for q in range(2):
                            sp.wait_ge(own_stored[q], 16 * (BLOCKS // 2))

                    @block.gpsimd
                    def _(pool):
                        def gather(n):
                            k, j = divmod(n, GT)

                            def body(b, q, turn):
                                slot = q * GK + k
                                if n == 0:
                                    hold(pool, indices_ready, b + 1, passed_pool)
                                if j == 0:
                                    i = UNITS.index(("far", k))
                                    wait_from(pool, turned, NU * (b - 2) + i + 1, passed_pool)
                                for side in range(2):
                                    at = (2 * j + side) * D
                                    pool.indirect_dma_start(
                                        gathered[slot][:, at:at + D], None, h0_t,
                                        bass.IndirectOffsetOnAxis(ap=gather_i[q][:, side * CT + n:side * CT + n + 1],
                                                                  axis=0)).then_inc(gather_done[slot], 16)
                            return body

                        def scatter(n):
                            k, j = divmod(n, GT)

                            def body(b, q, turn):
                                slot = q * GK + k
                                if n == 0:
                                    hold(pool, put_ready, b + 1, passed_pool)
                                if j == 0:
                                    hold(pool, summed_ready, GK * b + k + 1, passed_pool)
                                a = (CT * q + n) % ACCS
                                wait_from(pool, acc_done[a], 16 * (CT * turn + (CT * q + n) // ACCS), passed_pool)
                                pool.indirect_dma_start(
                                    acc0[a], bass.IndirectOffsetOnAxis(ap=put_i[q][:, n:n + 1], axis=0),
                                    summed[slot][:, j * D:(j + 1) * D], None, compute_op=ALU.add)\
                                    .then_inc(acc_done[a], 16)
                            return body
                        steps = []
                        for n in range(CT):
                            steps += [(0, gather(n)), (SCATTER_LAG, scatter(n))]
                        rounds(pool, steps, BLOCKS, 2)
                        for a in range(ACCS):
                            pool.wait_ge(acc_done[a], 16 * BLOCKS * CT // ACCS)

                    @block.vector
                    def _(dve):
                        V = nc.vector
                        V.memset(w0_own[:, :], 0.0).then_inc(w_zeroed, 1)
                        dve.wait_ge(w_zeroed, 1)
                        dve.wait_ge(w_loaded, 64)
                        for h in range(2):
                            half = slice(h * D, (h + 1) * D)
                            V.tensor_tensor(w0_own[half, h * HID:(h + 1) * HID], w0_parts[0][half, :],
                                            w0_parts[1][half, :], ALU.add).then_inc(w_ready, 1)

                        def compact(i):
                            at = slice(i * CHUNK, min((i + 1) * CHUNK, RAW))
                            n = at.stop - at.start

                            def body(b, q, turn):
                                f = cols(raw[q][:, :], FIELDS)
                                if i == 0:
                                    dve.wait_ge(raw_loaded[q], 16 * (turn + 1))
                                    wait_from(dve, packed_done, b - 1)
                                    V.tensor_tensor(
                                        cols(tile_hot[q][:, :], CT), f[:, :, 0:1].to_broadcast([EP, RAW, CT]),
                                        iota_tile[:, bass.ds(b * CT, CT)].unsqueeze(1).to_broadcast([EP, RAW, CT]),
                                        ALU.is_equal).then_inc(tile_hot_ready, 1)
                                for m in range(at.start, at.stop):
                                    V.tensor_scalar(row_hot[q][:, m * EP:(m + 1) * EP], iota_b[:, :],
                                                    f[:, m, 1:2], None, ALU.is_equal)
                                if i == 0:
                                    dve.wait_ge(tile_hot_ready, b + 1)
                                V.tensor_tensor(
                                    spread_out[q][:, :].rearrange("p (t c k) -> p t c k", c=CT, k=5)[:, at],
                                    cols(tile_hot[q][:, :], CT)[:, at].unsqueeze(3).to_broadcast([EP, n, CT, 5]),
                                    f[:, at, 2:7].unsqueeze(2).to_broadcast([EP, n, CT, 5]),
                                    ALU.mult).then_inc(spread_ready, 1)
                            return body

                        def unpack(b, q, turn):
                            dve.wait_ge(packed_done, b + 1)
                            V.tensor_copy(packed[:, :], ps_packed[:, 0:CT * 5]).then_inc(packed_copied, 1)
                            dve.wait_ge(packed_copied, b + 1)
                            f = cols(packed[:, :], 5)
                            for slot in range(GK):
                                wait_from(dve, gather_done[q * GK + slot], 96 * turn)
                            wait_from(dve, seg_spread, GK * (b - 1))
                            V.tensor_scalar(src_high[q][:, :], f[:, :, 0], 256.0, None, ALU.mult)
                            V.tensor_scalar(empty[q][:, :], f[:, :, 4], -1.0, 1.0, ALU.mult, ALU.add)
                            V.scalar_tensor_tensor(src_f[q][:, :], f[:, :, 0], 256.0, f[:, :, 1], ALU.mult, ALU.add)
                            V.scalar_tensor_tensor(local_f[q][:, :], f[:, :, 2], 256.0, f[:, :, 3], ALU.mult,
                                                   ALU.add).then_inc(nodes_ready, 1)
                            dve.wait_ge(nodes_ready, b + 1)
                            V.tensor_copy(gather_i[q][:, 0:CT], src_f[q][:, :])
                            V.tensor_tensor(gather_i[q][:, CT:2 * CT], local_f[q][:, :],
                                            block_base[:, bass.ds(b, 1)].to_broadcast([EP, CT]),
                                            ALU.add).then_inc(indices_ready, 1)
                            V.scalar_tensor_tensor(seg_high[q][:, :], empty[q][:, :], float(JUNK_HIGH),
                                                   src_high[q][:, :], ALU.mult, ALU.add)
                            V.scalar_tensor_tensor(seg_low[q][:, :], empty[q][:, :], junk_low[:, :], f[:, :, 1],
                                                   ALU.mult, ALU.add)
                            V.scalar_tensor_tensor(seg_f[q][:, :], empty[q][:, :], junk_row[:, :], src_f[q][:, :],
                                                   ALU.mult, ALU.add).then_inc(seg_filled, 1)
                            V.tensor_copy(far_src[:, bass.ds(b * CT, CT)], src_f[q][:, :])
                            V.tensor_tensor(far_local[:, bass.ds(b * CT, CT)], local_f[q][:, :], empty[q][:, :],
                                            ALU.subtract)
                            dve.wait_ge(seg_filled, b + 1)
                            V.scalar_tensor_tensor(to_junk[q][:, :], seg_f[q][:, :], -1.0,
                                                   junk_row[:, :].to_broadcast([EP, CT]), ALU.mult, ALU.add)

                        def bias(b, q, turn):
                            dve.wait_ge(x_loaded[q], 16 * (turn + 1))
                            wait_from(dve, message_ready, NU * (b - 2) + 4)
                            V.tensor_tensor(blk(own_bias[q][:, :]), blk(own_x[q][:, :]),
                                            b2_s[0:P, :].unsqueeze(1).to_broadcast([P, SUBS, D]),
                                            ALU.add).then_inc(own_bias_ready, 1)

                        def clamp(i, psum, b_s, to, read, done, pre):
                            def body(b, q, turn):
                                dve.wait_ge(pre, NU * b + i + 1)
                                wait_from(dve, read, NU * b + i)
                                w = width(i)
                                V.tensor_scalar(to[:, 0:w], psum[:, 0:w], b_s[:, :], SOFTPLUS_CLAMP,
                                                ALU.add, ALU.min).then_inc(done, 1)
                            return body

                        def softplus(i, psum, b_s, ln, ln_done, to, read, done):
                            def body(b, q, turn):
                                dve.wait_ge(ln_done, NU * b + i + 1)
                                wait_from(dve, read, NU * b + i)
                                w = width(i)
                                V.scalar_tensor_tensor(to[:, 0:w], psum[:, 0:w], b_s[:, :], ln[:, 0:w],
                                                       ALU.add, ALU.max).then_inc(done, 1)
                            return body

                        def repeats(k):
                            def body(b, q, turn):
                                g, r = GK * b + k, (q + k) % 2
                                dve.wait_ge(seg_spread, g + 1)
                                wait_from(dve, merged, g - 1)
                                for j in range(GT):
                                    n = k * GT + j
                                    at = slice(j * EP, (j + 1) * EP)
                                    last = V.scalar_tensor_tensor(
                                        same[r][:, at], ps_seg[:, at], seg_f[q][:, n:n + 1], up_to[:, :],
                                        ALU.is_equal, ALU.mult, accum_out=equals[q][:, n:n + 1])
                                last.then_inc(same_ready, 1)
                            return body

                        def put(b, q, turn):
                            dve.wait_ge(same_ready, GK * (b + 1))
                            V.scalar_tensor_tensor(shift_n[q][:, :], equals[q][:, :], 1.5, to_junk[q][:, :],
                                                   ALU.is_gt, ALU.mult).then_inc(shift_ready, 1)
                            for a in range(ACCS):
                                wait_from(dve, acc_done[a], 16 * (CT * (turn - 1) + (CT * (q + 1) + 1 - a) // ACCS))
                            dve.wait_ge(shift_ready, b + 1)
                            V.tensor_tensor(put_i[q][:, :], shift_n[q][:, :], seg_f[q][:, :], ALU.add)\
                             .then_inc(put_ready, 1)

                        def result(i):
                            kind, k = UNITS[i]

                            def body(b, q, turn):
                                dve.wait_ge(raw_done, NU * b + i + 1)
                                if kind == "own":
                                    dve.wait_ge(own_bias_ready, b + 1)
                                    wait_from(dve, own_stored[q], 16 * turn)
                                    at = slice(k * HALF * D, (k + 1) * HALF * D)
                                    V.tensor_tensor(own_out[q][:, at], ps_raw[0:P, 0:HALF * D], own_bias[q][:, at],
                                                    ALU.add).then_inc(message_ready, 1)
                                else:
                                    wait_from(dve, merged, GK * b + k)
                                    V.tensor_tensor(cols(message[:, :], D), cols(ps_raw[:, 0:GT * D], D),
                                                    b2_s[:, :].unsqueeze(1).to_broadcast([EP, GT, D]),
                                                    ALU.add).then_inc(message_ready, 1)
                            return body

                        def order(i, unit):
                            p = unit(1)
                            out = [(1, clamp(p, ps_2, b1_s, t2, e2_ready, t2_ready, pre2_done)),
                                   (0, clamp(i, ps_1, b0_s, t1, e1_ready, t1_ready, pre1_done)),
                                   (-UNIT_LAG * NU, compact(i)),
                                   (1, softplus(p, ps_2, b1_s, e2, l2_ready, h2, raw_done, h2_ready)),
                                   (0, softplus(i, ps_1, b0_s, e1, l1_ready, h1, pre2_done, h1_ready))]
                            if UNITS[i][0] == "far":
                                out.append((0, repeats(UNITS[i][1])))
                            out.append((1, result(p)))
                            return out
                        V.tensor_scalar(junk_low[:, :], junk_row[:, :], -float(JUNK_HIGH), None, ALU.add)\
                         .then_inc(junk_low_made, 1)
                        dve.wait_ge(junk_low_made, 1)
                        stages = unit_stages(order, UNIT_LAG)
                        stages[6:6] = [(1, unpack)]
                        rounds(dve, [(UNIT_LAG, bias)] + stages + [(UNIT_LAG, put)], BLOCKS, 2)

                    @block.tensor
                    def _(pe):
                        M, T = nc.tensor.matmul, nc.tensor.transpose

                        def pack(b, q, turn):
                            pe.wait_ge(spread_ready, NU * (b + 1))
                            wait_from(pe, packed_copied, b)
                            for n in range(RAW):
                                last = M(ps_packed[:, 0:CT * 5], row_hot[q][:, n * EP:(n + 1) * EP],
                                         spread_out[q][:, n * CT * 5:(n + 1) * CT * 5],
                                         start=(n == 0), stop=(n == RAW - 1))
                            last.then_inc(packed_done, 1)

                        def turn_rows(i):
                            kind, k = UNITS[i]

                            def body(b, q, turn):
                                if kind == "own":
                                    pe.wait_ge(rows_loaded[q], 16 * (turn + 1))
                                else:
                                    pe.wait_ge(gather_done[q * GK + k], 96 * (turn + 1))
                                wait_from(pe, in_ready, NU * b + i)
                                if kind == "own":
                                    for j in range(HALF // 2):
                                        at = (k * HALF + 2 * j) * D
                                        last = T(ps_in[:, j * P:(j + 1) * P], own_rows[q][:, at:at + 2 * D],
                                                 ident[0:P, 0:P])
                                else:
                                    for j in range(GT):
                                        last = T(ps_in[:, j * EP:(j + 1) * EP],
                                                 gathered[q * GK + k][:, 2 * j * D:2 * (j + 1) * D], ident[:, :])
                                last.then_inc(turned, 1)
                            return body

                        def layer1(i):
                            def body(b, q, turn):
                                pe.wait_ge(in_ready, NU * b + i + 1)
                                wait_from(pe, h1_ready, NU * b + i)
                                if UNITS[i][0] == "own":
                                    w = HALF // 2 * P
                                    for h in range(2):
                                        last = M(ps_1[:, h * w:(h + 1) * w], w0_own[:, h * HID:(h + 1) * HID],
                                                 in_t[:, 0:w], start=True, stop=True)
                                else:
                                    last = M(ps_1[:, 0:FW], w0_s[:, :], in_t[:, 0:FW], start=True, stop=True)
                                last.then_inc(pre1_done, 1)
                            return body

                        def layer2(i):
                            def body(b, q, turn):
                                pe.wait_ge(h1_ready, NU * b + i + 1)
                                wait_from(pe, h2_ready, NU * b + i)
                                w = width(i)
                                M(ps_2[:, 0:w], w1_s[:, :], h1[:, 0:w], start=True, stop=True).then_inc(pre2_done, 1)
                            return body

                        def layer3(i):
                            def body(b, q, turn):
                                pe.wait_ge(h2_ready, NU * b + i + 1)
                                wait_from(pe, message_ready, NU * b + i)
                                if UNITS[i][0] == "own":
                                    for j in range(HALF):
                                        at = (j % 2 * (HALF // 2) + j // 2) * P
                                        last = M(ps_raw[0:P, j * D:(j + 1) * D], h2[:, at:at + P], w2_s[:, :],
                                                 start=True, stop=True)
                                else:
                                    for j in range(GT):
                                        last = M(ps_raw[:, j * D:(j + 1) * D], h2[:, j * EP:(j + 1) * EP], w2_s[:, :],
                                                 start=True, stop=True)
                                last.then_inc(raw_done, 1)
                            return body

                        def spread(k):
                            def body(b, q, turn):
                                g = GK * b + k
                                if k == 0:
                                    pe.wait_ge(seg_filled, b + 1)
                                wait_from(pe, same_ready, g)
                                for j in range(GT):
                                    n = k * GT + j
                                    for part in (seg_high, seg_low):
                                        last = M(ps_seg[:, j * EP:(j + 1) * EP],
                                                 part[q][:, n:n + 1].to_broadcast([EP, EP]), ident_b[:, :],
                                                 start=(part is seg_high), stop=(part is seg_low))
                                last.then_inc(seg_spread, 1)
                            return body

                        def merge(k):
                            i = UNITS.index(("far", k))

                            def body(b, q, turn):
                                g = GK * b + k
                                pe.wait_ge(same_ready, g + 1)
                                pe.wait_ge(message_ready, NU * b + i + 1)
                                wait_from(pe, summed_ready, g)
                                for j in range(GT):
                                    last = M(ps_sum[:, j * D:(j + 1) * D], same[(q + k) % 2][:, j * EP:(j + 1) * EP],
                                             message[:, j * D:(j + 1) * D], start=True, stop=True)
                                last.then_inc(merged, 1)
                            return body

                        def order(i, unit):
                            out = [(1, layer2(unit(1))), (0, layer1(i)), (-1, turn_rows(unit(-1)))]
                            if UNITS[unit(2)][0] == "far":
                                out.append((2, merge(UNITS[unit(2)][1])))
                            if UNITS[i][0] == "far":
                                out.append((0, spread(UNITS[i][1])))
                            out.append((1, layer3(unit(1))))
                            return out
                        pe.wait_ge(w_ready, 2)
                        rounds(pe, unit_stages(order, UNIT_LAG) + [(0, pack)], BLOCKS, 2)

                    @block.scalar
                    def _(act):
                        A = nc.scalar.activation

                        def take_in(i):
                            def body(b, q, turn):
                                act.wait_ge(turned, NU * b + i + 1)
                                wait_from(act, pre1_done, NU * b + i)
                                w = FW if UNITS[i][0] == "far" else HALF // 2 * P
                                A(in_t[:, 0:w], ps_in[:, 0:w], ACT.Copy).then_inc(in_ready, 1)
                            return body

                        def exp_ln(i, t_in, t_ready, e, read, e_ready, l_ready):
                            def body(b, q, turn):
                                act.wait_ge(t_ready, NU * b + i + 1)
                                wait_from(act, read, NU * b + i)
                                w = width(i)
                                A(e[:, 0:w], t_in[:, 0:w], ACT.Exp).then_inc(e_ready, 1)
                                act.wait_ge(e_ready, NU * b + i + 1)
                                A(e[:, 0:w], e[:, 0:w], ACT.Ln, bias=1.0).then_inc(l_ready, 1)
                            return body

                        def move(k):
                            def body(b, q, turn):
                                act.wait_ge(merged, GK * b + k + 1)
                                scatters_over(act, b, turn, q, k)
                                A(summed[q * GK + k][:, :], ps_sum[:, 0:GT * D], ACT.Copy).then_inc(summed_ready, 1)
                            return body

                        def order(i, unit):
                            p = unit(1)
                            out = [(1, exp_ln(p, t2, t2_ready, e2, h2_ready, e2_ready, l2_ready)),
                                   (0, exp_ln(i, t1, t1_ready, e1, h1_ready, e1_ready, l1_ready)),
                                   (-1, take_in(unit(-1)))]
                            if UNITS[unit(2)][0] == "far":
                                out.append((2, move(UNITS[unit(2)][1])))
                            return out
                        act.preload_act_table_set(EXP_LN_SET)
                        rounds(act, unit_stages(order, UNIT_LAG), BLOCKS, 2)

        def fast_edges1():
            reach = [(max(0, c - 1) // 2, (min(SUBS - 1, c + 1)) // 2 + 1) for c in range(CT)]
            reach_at = [sum(hi - lo for lo, hi in reach[:c]) * 2 * P for c in range(CT)]
            HOT = sum(hi - lo for lo, hi in reach) * 2 * P
            with ExitStack() as ph:
                def t(n, shape, k=2, dt=F32):
                    return [ph.enter_context(nc.sbuf_tensor(f"fast1_{n}_{i}", shape, dt)) for i in range(k)]

                s = phase_semaphores(ph, "fast1")

                index_i = t("index_i", [EP, CT], RING, I32)
                gathered, hot = t("gathered", [EP, CT * D], RING), t("hot", [EP, HOT])
                self_rows = t("self_rows", [P, BW], RING)
                z_in, hid = t("z_in", [128, TW]), t("hid", [128, TW])
                gather_done, self_loaded = ([s(f"{n}_{i}") for i in range(RING)] for n in ("gather_done", "self_loaded"))
                (index_ready, hot_ready, nodes_summed, z_in_ready, pre_done, hid_ready, post_done,
                 z_ready, stats_done) = (s(n) for n in (
                     "index_ready", "hot_ready", "nodes_summed", "z_in_ready", "pre_done",
                     "hid_ready", "post_done", "z_ready", "stats_done"))
                with nc.Block("fast_edges1") as block:
                    @block.sync
                    def _(sp):
                        def load(b, q, turn):
                            wait_from(sp, nodes_summed, b - RING + 1, passed_sp)
                            sp.dma_start(pairs_of(self_rows[q][:, :]), pair_rows(h1_t, b)).then_inc(self_loaded[q], 16)
                        rounds(sp, [(0, load)], BLOCKS)

                    @block.gpsimd
                    def _(pool):
                        def gather(b, q, turn):
                            hold(pool, index_ready, b + 1, passed_pool)
                            wait_from(pool, nodes_summed, b - RING + 1, passed_pool)
                            for c in range(CT):
                                pool.indirect_dma_start(
                                    gathered[q][:, c * D:(c + 1) * D], None, h1_t,
                                    bass.IndirectOffsetOnAxis(ap=index_i[q][:, c:c + 1], axis=0))\
                                    .then_inc(gather_done[q], 16)
                        rounds(pool, [(0, gather)], BLOCKS)

                    @block.vector
                    def _(dve):
                        V = nc.vector

                        def index(b, q, turn):
                            wait_from(dve, gather_done[q], 16 * CT * turn)
                            V.tensor_copy(index_i[q][:, :], far_src[:, bass.ds(b * CT, CT)]).then_inc(index_ready, 1)

                        def one_hot(b, q, turn):
                            wait_from(dve, nodes_summed, b - 1)
                            for c, (lo, hi) in enumerate(reach):
                                last = V.tensor_scalar(
                                    hot[q % 2][:, reach_at[c]:reach_at[c] + (hi - lo) * 2 * P],
                                    iota_row[:, lo * 2 * P:hi * 2 * P],
                                    far_local[:, bass.ds(b * CT + c, 1)], None, ALU.is_equal)
                            last.then_inc(hot_ready, 1)

                        def stats(b, q, turn):
                            dve.wait_ge(z_ready, b + 1)
                            V.bn_stats(z_stats[:, bass.ds(b * 6, 6)], z_t[:, bass.ds(b * TW, TW)])\
                             .then_inc(stats_done, 1)
                        rounds(dve, [(0, index), (1, one_hot), (4, stats)], BLOCKS)
                        dve.wait_ge(stats_done, BLOCKS)

                    @block.tensor
                    def _(pe):
                        def sum_nodes(b, q, turn):
                            pe.wait_ge(hot_ready, b + 1)
                            pe.wait_ge(gather_done[q], 16 * CT * (turn + 1))
                            pe.wait_ge(self_loaded[q], 16 * (turn + 1))
                            wait_from(pe, z_in_ready, b - 1)
                            for t in range(PAIRS):
                                at = slice(t * P, (t + 1) * P)
                                nc.tensor.matmul(banks[6 + q % 2][:, at], self_rows[q][:, t * 2 * D:(t + 1) * 2 * D],
                                                 twice[:, :], start=True, stop=False)
                                tiles = [c for c in range(CT) if reach[c][0] <= t < reach[c][1]]
                                for c in tiles:
                                    hot_at = reach_at[c] + (t - reach[c][0]) * 2 * P
                                    ends = hot[q % 2][:, hot_at:hot_at + 2 * P].rearrange("p (i h) -> p h i", h=2)
                                    for h in range(2):
                                        last = nc.tensor.matmul(
                                            banks[6 + q % 2][h * D:(h + 1) * D, at],
                                            gathered[q][:, c * D:(c + 1) * D], ends[:, h, :],
                                            start=False, stop=(c == tiles[-1]))
                            last.then_inc(nodes_summed, 1)

                        def first(b, q, turn):
                            pe.wait_ge(z_in_ready, b + 1)
                            wait_from(pe, hid_ready, b - 1)
                            nc.tensor.matmul(banks[2 + q % 2][:, 0:TW], gw1_s[:, :], z_in[q % 2][:, :],
                                             start=True, stop=True).then_inc(pre_done, 1)

                        def second(b, q, turn):
                            pe.wait_ge(hid_ready, b + 1)
                            wait_from(pe, z_ready, b - 1)
                            nc.tensor.matmul(banks[4 + q % 2][:, 0:TW], gw2_s[:, :], hid[q % 2][:, :],
                                             start=True, stop=True).then_inc(post_done, 1)
                        rounds(pe, [(1, first), (2, second), (0, sum_nodes)], BLOCKS)

                    @block.scalar
                    def _(act):
                        def take_in(b, q, turn):
                            act.wait_ge(nodes_summed, b + 1)
                            wait_from(act, pre_done, b - 1)
                            nc.scalar.activation(z_in[q % 2][:, :], banks[6 + q % 2][:, 0:TW], ACT.Copy).then_inc(z_in_ready, 1)

                        def hidden(b, q, turn):
                            act.wait_ge(pre_done, b + 1)
                            wait_from(act, post_done, b - 1)
                            nc.scalar.activation(hid[q % 2][:, :], banks[2 + q % 2][:, 0:TW], ACT.Relu,
                                                 bias=gb1_s[:, :]).then_inc(hid_ready, 1)

                        def result(b, q, turn):
                            act.wait_ge(post_done, b + 1)
                            nc.scalar.activation(z_t[:, bass.ds(b * TW, TW)], banks[4 + q % 2][:, 0:TW], ACT.Identity,
                                                 bias=gb2_s[:, :]).then_inc(z_ready, 1)
                        rounds(act, [(0, take_in), (1, hidden), (2, result)], BLOCKS)

        stat, mean_ps, var_ps, std_ready, scale_ready = (
            sem(f"last_{n}") for n in ("stat", "mean_ps", "var_ps", "std_ready", "scale_ready"))
        loaded, stored = ([sem(f"last_{n}_{i}") for i in range(RING)] for n in ("loaded", "stored"))
        y_ready, turned, out_ready = (sem(f"last_{n}") for n in ("y_ready", "turned", "out_ready"))

        fast = nc.values_load(fast_ok[0:1, 0:1], min_val=0, max_val=1)
        with nc.If(fast == 1):
            fast_edges0()
            norm_phase("fast_norm1", [own_t] + acc0, h1_t, r_t, [])
            fast_edges1()
        with nc.Else():
            edge_phase("edges0", h0_t, src_s, acc0, True)
            norm_phase("norm1", [x] + acc0, h1_t, r_t, acc1)
            edge_phase("edges1", h1_t, dst_s, acc1, False)
            node_phase()

        with ExitStack() as ph:
            def t(n, shape, k=RING):
                return [ph.enter_context(nc.sbuf_tensor(f"last_{n}_{i}", shape, F32)) for i in range(k)]

            halves, both, dev, var2, std, scale, shift = (
                t(n, [128, w], 1)[0] for n, w in (("halves", 2), ("both", 1), ("dev", 1), ("var2", 1),
                                                  ("std", 1), ("scale", 1), ("shift", 1)))
            bn_eps = t("bn_eps", [128, 1], 1)[0]
            resid, outs = t("resid", [P, BW]), t("outs", [P, BW])
            y = t("y", [128, TW], 2)
            with nc.Block("finish") as block:
                @block.sync
                def _(sp):
                    def load(b, q, turn):
                        wait_from(sp, out_ready, b - RING + 1, passed_sp)
                        sp.dma_start(pairs_of(resid[q][:, :]), pair_rows(r_t, b)).then_inc(loaded[q], 16)

                    rounds(sp, [(0, load)], BLOCKS)

                @block.vector
                def _(dve):
                    n = 0
                    nc.vector.memset(bn_eps[:, :], BN_EPS).then_inc(stat, 1)
                    nc.vector.bn_aggr(halves[:, :], z_stats[:, :].rearrange("p (b k) -> p b k", k=6)).then_inc(stat, 1)
                    dve.wait_ge(mean_ps, 1)
                    nc.vector.tensor_copy(both[:, :], banks[6][:, 0:1]).then_inc(stat, 1)
                    dve.wait_ge(stat, 3)
                    nc.vector.tensor_tensor(dev[:, :], halves[:, 0:1], both[:, :], ALU.subtract).then_inc(stat, 1)
                    dve.wait_ge(stat, 4)
                    nc.vector.tensor_tensor(dev[:, :], dev[:, :], dev[:, :], ALU.mult).then_inc(stat, 1)
                    dve.wait_ge(stat, 5)
                    nc.vector.tensor_tensor(var2[:, :], dev[:, :], halves[:, 1:2], ALU.add).then_inc(stat, 1)
                    dve.wait_ge(std_ready, 1)
                    nc.vector.reciprocal(std[:, :], std[:, :]).then_inc(stat, 1)
                    dve.wait_ge(stat, 7)
                    nc.vector.tensor_tensor(scale[:, :], std[:, :], gamma_s[:, :], ALU.mult).then_inc(stat, 1)
                    dve.wait_ge(stat, 8)
                    nc.vector.tensor_tensor(shift[:, :], both[:, :], scale[:, :], ALU.mult).then_inc(stat, 1)
                    dve.wait_ge(stat, 9)
                    nc.vector.tensor_tensor(shift[:, :], beta_s[:, :], shift[:, :], ALU.subtract)\
                      .then_inc(scale_ready, 1)

                    def add(b, q, turn):
                        dve.wait_ge(turned, b + 1)
                        dve.wait_ge(loaded[q], 16 * (turn + 1))
                        wait_from(dve, stored[q], 16 * turn)
                        nc.vector.tensor_tensor(outs[q][:, :], banks[q % 2][0:P, 0:BW], resid[q][:, :], ALU.add)\
                          .then_inc(out_ready, 1)
                    rounds(dve, [(1, add)], BLOCKS)

                @block.tensor
                def _(pe):
                    pe.wait_ge(stat, 2)
                    nc.tensor.matmul(banks[6][:, 0:1], pair_mean[:, :], halves[:, 0:1], start=True, stop=True)\
                      .then_inc(mean_ps, 1)
                    pe.wait_ge(stat, 6)
                    nc.tensor.matmul(banks[7][:, 0:1], pair_mean[:, :], var2[:, :], start=True, stop=True)\
                      .then_inc(var_ps, 1)

                    def turn_back(b, q, turn):
                        pe.wait_ge(y_ready, b + 1)
                        wait_from(pe, out_ready, b - 1)
                        for j in range(PAIRS):
                            last = nc.tensor.transpose(banks[q % 2][0:P, j * 2 * D:(j + 1) * 2 * D],
                                                       y[q % 2][:, j * P:(j + 1) * P], ident[:, :])
                        last.then_inc(turned, 1)
                    rounds(pe, [(0, turn_back)], BLOCKS)

                @block.scalar
                def _(act):
                    act.wait_ge(var_ps, 1)
                    nc.scalar.activation(std[:, :], banks[7][:, 0:1], ACT.Sqrt, bias=bn_eps[:, :])\
                       .then_inc(std_ready, 1)
                    act.wait_ge(scale_ready, 1)

                    def normalise(b, q, turn):
                        wait_from(act, turned, b - 1)
                        nc.scalar.activation(y[q % 2][:, :], z_t[:, bass.ds(b * TW, TW)], ACT.Relu,
                                             bias=shift[:, :], scale=scale[:, :]).then_inc(y_ready, 1)

                    def store(b, q, turn):
                        hold(act, out_ready, b + 1, passed_act)
                        act.dma_start(pair_rows(out, b), pairs_of(outs[q][:, :])).then_inc(stored[q], 16)
                    rounds(act, [(0, normalise), (2, store)], BLOCKS)
                    for q in range(RING):
                        act.wait_ge(stored[q], 16 * ((BLOCKS - q + RING - 1) // RING))


_INS = ["x", "src", "dst", "L0_gnn_W0", "L0_gnn_b0", "L0_gnn_W1", "L0_gnn_b1", "L0_gnn_W2", "L0_gnn_b2",
        "L1_gnn_W1", "L1_gnn_b1", "L1_gnn_W2", "L1_gnn_b2", "L1_gnn_gamma", "L1_gnn_beta"]


def kernel(**inputs):
    import numpy as _np
    import concourse.bacc as _bacc
    from concourse import mybir as _mybir
    from concourse.bass_utils import run_bass_kernel_spmd as _run

    nc = _bacc.Bacc("TRN2", target_bir_lowering=False, num_devices=1)
    arrays, args = {}, []
    for name in _INS:
        a = _np.ascontiguousarray(inputs[name])
        arrays[f"in_{name}"] = a
        args.append(nc.dram_tensor(f"in_{name}", a.shape, _mybir.dt.from_np(a.dtype), kind="ExternalInput").ap())
    shape = inputs["x"].shape
    args.append(nc.dram_tensor("out_0", shape, _mybir.dt.float32, kind="ExternalOutput").ap())
    gnn_program(nc, *args)
    r = _run(nc, [arrays], core_ids=[0])
    return r.results[0]["out_0"]
```
